# Optimizing a Trainium2 kernel written in Bass

```python
import numpy as np
import jax
import jax.numpy as jnp

def _softmax(x, axis=-1):
    return jax.nn.softmax(x, axis=axis)

def _gelu(x):
    return jax.nn.gelu(x, approximate=True)

def _silu(x):
    return jax.nn.silu(x)

def _sigmoid(x):
    return jax.nn.sigmoid(x)

def _layernorm(x, axis=-1, eps=1e-05):
    m = jnp.mean(x, axis=axis, keepdims=True)
    v = jnp.var(x, axis=axis, keepdims=True)
    return (x - m) / jnp.sqrt(v + eps)

def _scatter_add(tgt, idx, src, axis=0):
    return tgt.at[idx].add(src)

def _segment_sum(src, seg, n):
    return jax.ops.segment_sum(src, seg, n)
kernel_name = 'mk_decoder_preln_d1_seqx_r4_ada215'

def setup_inputs(seed: int=0):
    np.random.seed(seed)
    _w = jnp.asarray

    def _rec_inputs():
        import jax
        import jax.numpy as jnp
        _rk = jax.random.key(seed)
        x = -0.000125 + 0.9999 * jax.random.normal(jax.random.fold_in(_rk, 1), (4, 512, 512), jnp.float32)
        _lenS = 512 - jax.random.randint(jax.random.fold_in(_rk, 7), (4,), 0, max(1, 512 // 4) + 1, jnp.int32)
        _lenS2 = 64 - jax.random.randint(jax.random.fold_in(_rk, 8), (4,), 0, max(1, 64 // 4) + 1, jnp.int32)
        _ctx_2048P = jax.random.normal(jax.random.fold_in(_rk, 11), (4, 16, 512), jnp.float32)
        _ctx_2048c = jax.random.dirichlet(jax.random.fold_in(_rk, 511), 0.3 * jnp.ones((16,), jnp.float32), (4, 64))
        _ctx_2048t = jnp.einsum('bsk,bkd->bsd', _ctx_2048c, _ctx_2048P)
        _ctx_2048t = _ctx_2048t * jax.lax.rsqrt(jnp.mean(jnp.square(_ctx_2048t)) + 1e-12) * 0.953939
        ctx_2048 = -0.000514642 + 1.00011 * (_ctx_2048t + 0.3 * jax.random.normal(jax.random.fold_in(_rk, 611), (4, 64, 512), jnp.float32))
        _validS = jnp.arange(512)[None, :] < _lenS[:, None]
        _validS2 = jnp.arange(64)[None, :] < _lenS2[:, None]
        _causal = jnp.tril(jnp.ones((512, 512), dtype=bool))
        mask_BxS2_bk0 = jnp.logical_not(jnp.broadcast_to(_validS2[:, :], (4, 64)))
        return (x, ctx_2048, mask_BxS2_bk0)
    x, ctx_2048, mask_BxS2_bk0 = _rec_inputs()

    def _L0_attn_setup():
        import jax, jax.numpy as jnp
        import numpy as np
        HQ, HKV, HD = (32, 8, 64)
        G = HQ // HKV
        SCALE = HD ** (-0.5)

        def _rope(x, offset=0):
            B, L, H, hd = x.shape
            inv = 1.0 / 10000.0 ** (jnp.arange(0, hd, 2, dtype=jnp.float32) / hd)
            pos = jnp.arange(offset, offset + L, dtype=jnp.float32)
            f = pos[:, None] * inv[None, :]
            c = jnp.cos(f)[None, :, None, :]
            s = jnp.sin(f)[None, :, None, :]
            x1, x2 = (x[..., 0::2], x[..., 1::2])
            out = jnp.stack([x1 * c - x2 * s, x1 * s + x2 * c], axis=-1)
            return out.reshape(x.shape)
        key = jax.random.key(seed)
        ks = jax.random.split(key, 5)
        B, L, D = (2, 512, 512)
        w = 0.02
        return {'x': jax.random.normal(ks[0], (B, L, D), dtype=jnp.float32), 'Wq': jax.random.normal(ks[1], (HQ * HD, D), dtype=jnp.float32) * w, 'Wk': jax.random.normal(ks[2], (HKV * HD, D), dtype=jnp.float32) * w, 'Wv': jax.random.normal(ks[3], (HKV * HD, D), dtype=jnp.float32) * w, 'Wo': jax.random.normal(ks[4], (D, HQ * HD), dtype=jnp.float32) * w}
    _L0_attn_all = _L0_attn_setup()
    _L0_attn_in = {k: v for k, v in _L0_attn_all.items() if k in ('Wq', 'Wk', 'Wv', 'Wo')}
    del _L0_attn_all

    def _L0_xattn_setup():
        import jax, jax.numpy as jnp
        import numpy as np
        key = jax.random.key(seed)
        k1, k2, k3 = jax.random.split(key, 3)
        B, S, D, M = (8, 512, 512, 128)
        hidden_states = jax.random.normal(k1, (B, S, D), dtype=jnp.float32)
        memory_tokens = jax.random.normal(k2, (B, M, D), dtype=jnp.float32)
        memory_mask = jax.random.randint(k3, (B, M), 0, 2).astype(jnp.bool_)
        return {'hidden_states': hidden_states, 'memory_tokens': memory_tokens, 'memory_mask': memory_mask}
    _L0_xattn_all = _L0_xattn_setup()
    _L0_xattn_in = {k: v for k, v in _L0_xattn_all.items() if k in ()}
    del _L0_xattn_all

    def _L0_ffn_setup():
        import jax, jax.numpy as jnp
        import numpy as np
        ALPHA = 1.702
        LIMIT = 7.0
        TOP_K = 2
        E, H, I = (8, 512, 512)
        B, S = (2, 512)
        key = jax.random.key(seed)
        ks = jax.random.split(key, 7)
        return {'hidden_states': jax.random.normal(ks[0], (B, S, H), dtype=jnp.float32), 'router_weight': jax.random.normal(ks[1], (E, H), dtype=jnp.float32) * 0.02, 'router_bias': jax.random.normal(ks[2], (E,), dtype=jnp.float32) * 0.02, 'gate_up_proj': jax.random.normal(ks[3], (E, H, 2 * I), dtype=jnp.float32) * 0.02, 'gate_up_proj_bias': jax.random.normal(ks[4], (E, 2 * I), dtype=jnp.float32) * 0.02, 'down_proj': jax.random.normal(ks[5], (E, I, H), dtype=jnp.float32) * 0.02, 'down_proj_bias': jax.random.normal(ks[6], (E, H), dtype=jnp.float32) * 0.02}
    _L0_ffn_all = _L0_ffn_setup()
    _L0_ffn_in = {k: v for k, v in _L0_ffn_all.items() if k in ('router_weight', 'router_bias', 'gate_up_proj', 'gate_up_proj_bias', 'down_proj', 'down_proj_bias')}
    del _L0_ffn_all
    return {'x': x, 'ctx_2048': ctx_2048, 'mask_BxS2_bk0': mask_BxS2_bk0, 'L0_attn_Wq': _L0_attn_in['Wq'], 'L0_attn_Wk': _L0_attn_in['Wk'], 'L0_attn_Wv': _L0_attn_in['Wv'], 'L0_attn_Wo': _L0_attn_in['Wo'], 'L0_ffn_router_weight': _L0_ffn_in['router_weight'], 'L0_ffn_router_bias': _L0_ffn_in['router_bias'], 'L0_ffn_gate_up_proj': _L0_ffn_in['gate_up_proj'], 'L0_ffn_gate_up_proj_bias': _L0_ffn_in['gate_up_proj_bias'], 'L0_ffn_down_proj': _L0_ffn_in['down_proj'], 'L0_ffn_down_proj_bias': _L0_ffn_in['down_proj_bias']}

def reference(x, ctx_2048, mask_BxS2_bk0, L0_attn_Wq, L0_attn_Wk, L0_attn_Wv, L0_attn_Wo, L0_ffn_router_weight, L0_ffn_router_bias, L0_ffn_gate_up_proj, L0_ffn_gate_up_proj_bias, L0_ffn_down_proj, L0_ffn_down_proj_bias):
    import jax
    import jax.numpy as jnp

    def _L0_attn_ref(x, Wq, Wk, Wv, Wo):
        import jax, jax.numpy as jnp
        import numpy as np
        HQ, HKV, HD = (32, 8, 64)
        G = HQ // HKV
        SCALE = HD ** (-0.5)

        def _rope(x, offset=0):
            B, L, H, hd = x.shape
            inv = 1.0 / 10000.0 ** (jnp.arange(0, hd, 2, dtype=jnp.float32) / hd)
            pos = jnp.arange(offset, offset + L, dtype=jnp.float32)
            f = pos[:, None] * inv[None, :]
            c = jnp.cos(f)[None, :, None, :]
            s = jnp.sin(f)[None, :, None, :]
            x1, x2 = (x[..., 0::2], x[..., 1::2])
            out = jnp.stack([x1 * c - x2 * s, x1 * s + x2 * c], axis=-1)
            return out.reshape(x.shape)
        B, L, D = x.shape
        q = (x @ Wq.T).reshape(B, L, HQ, HD)
        k = (x @ Wk.T).reshape(B, L, HKV, HD)
        v = (x @ Wv.T).reshape(B, L, HKV, HD)
        q = _rope(q)
        k = _rope(k)
        qh = q.transpose(0, 2, 1, 3).reshape(B, HKV, G, L, HD)
        kh = k.transpose(0, 2, 1, 3)
        vh = v.transpose(0, 2, 1, 3)
        attn = jnp.einsum('bkgqd,bkld->bkgql', qh, kh) * SCALE
        causal = jnp.arange(L)[:, None] >= jnp.arange(L)[None, :]
        attn = jnp.where(causal[None, None, None], attn, -jnp.inf)
        p = jax.nn.softmax(attn, axis=-1)
        out = jnp.einsum('bkgql,bkld->bkgqd', p, vh)
        out = out.reshape(B, HQ, L, HD).transpose(0, 2, 1, 3).reshape(B, L, HQ * HD)
        return out @ Wo.T

    def _L0_xattn_ref(hidden_states, memory_tokens, memory_mask):
        import jax, jax.numpy as jnp
        import numpy as np
        B, S, D = hidden_states.shape
        scale = 1.0 / jnp.sqrt(jnp.asarray(D, hidden_states.dtype))
        scores = jnp.einsum('bsd,bmd->bsm', hidden_states, memory_tokens) * scale
        neg_inf = jnp.asarray(-1e+30, scores.dtype)
        scores = jnp.where(memory_mask[:, None, :], scores, neg_inf)
        attn = jax.nn.softmax(scores, axis=-1)
        readout = jnp.einsum('bsm,bmd->bsd', attn, memory_tokens)
        valid_b = jnp.any(memory_mask, axis=-1)
        out = jnp.where(valid_b[:, None, None], readout, jnp.zeros_like(readout))
        return out

    def _L0_ffn_ref(hidden_states, router_weight, router_bias, gate_up_proj, gate_up_proj_bias, down_proj, down_proj_bias):
        import jax, jax.numpy as jnp
        import numpy as np
        ALPHA = 1.702
        LIMIT = 7.0
        TOP_K = 2
        E, H, I = (8, 512, 512)
        B, S = (2, 512)
        bsz, seq_len, hidden = hidden_states.shape
        h = hidden_states.reshape(-1, hidden)
        T = h.shape[0]
        logits = h @ router_weight.T + router_bias
        top_vals, top_idx = jax.lax.top_k(logits, TOP_K)
        top_w = jax.nn.softmax(top_vals, axis=-1)
        scores = jnp.zeros_like(logits).at[jnp.arange(T)[:, None], top_idx].set(top_w)
        gate_up = jnp.einsum('th,ehj->etj', h, gate_up_proj) + gate_up_proj_bias[:, None, :]
        gate = gate_up[..., ::2]
        up = gate_up[..., 1::2]
        gate = jnp.minimum(gate, LIMIT)
        up = jnp.clip(up, -LIMIT, LIMIT)
        glu = gate * jax.nn.sigmoid(gate * ALPHA)
        act = (up + 1.0) * glu
        expert_out = jnp.einsum('eti,eih->eth', act, down_proj) + down_proj_bias[:, None, :]
        out = jnp.einsum('te,eth->th', scores, expert_out)
        return out.reshape(bsz, seq_len, hidden)
    x = x + _L0_attn_ref(_layernorm(x, axis=-1), L0_attn_Wq, L0_attn_Wk, L0_attn_Wv, L0_attn_Wo)
    x = x + _L0_xattn_ref(_layernorm(x, axis=-1), ctx_2048, mask_BxS2_bk0)
    x = x + _L0_ffn_ref(_layernorm(x, axis=-1), L0_ffn_router_weight, L0_ffn_router_bias, L0_ffn_gate_up_proj, L0_ffn_gate_up_proj_bias, L0_ffn_down_proj, L0_ffn_down_proj_bias)
    return x

_drawn_inputs = setup_inputs


def setup_inputs(seed=0):
    import zlib

    import numpy as np

    out = dict(_drawn_inputs(seed))
    spreads = {}
    factors = {'L0_attn_Wq': 5.91,
     'L0_attn_Wk': 5.687,
     'L0_ffn_router_bias': 4.413,
     'L0_ffn_gate_up_proj_bias': 8.0,
     'L0_ffn_down_proj_bias': 4.883}
    for name, (base, spread) in spreads.items():
        noise = np.random.default_rng([zlib.crc32(name.encode()), seed]).standard_normal(out[name].shape)
        drawn = base * np.exp(spread * noise) if base else spread * noise
        out[name] = jnp.asarray(drawn.astype(out[name].dtype))
    for name, factor in factors.items():
        out[name] = (out[name] * factor).astype(out[name].dtype)
    return out
```

```python
from contextlib import ExitStack

import numpy as np

import concourse.bass as bass
from concourse import mybir

F32 = mybir.dt.float32
F32R = mybir.dt.float32r
U32 = mybir.dt.uint32
U8 = mybir.dt.uint8
ALU = mybir.AluOpType
ACT = mybir.ActivationFunctionType
AX = mybir.AxisListType

P = 128
B, L, D = 4, 512, 512
T = B * L
TT = T // P
DC = D // P
HQ, HKV, HD = 32, 8, 64
G = HQ // HKV
QB = L // P
MEM = 64
E, I = 8, 512
IB = I // P
EPS = 1e-5
NEG = -3.0e38
MASKED = -1e30
ALPHA, LIMIT = 1.702, 7.0
GROUPS = HKV
HEADS = B * G
PASSES = ((0, 0), (0, 1), (1, 0))

P_AT = [0, P, 3 * P, 6 * P]
P_LEN = 10 * P
PT_ZERO = 4 * P
PT_AT = [0, 5 * P, 9 * P, 8 * P]
PT_LEN = 12 * P
UNITS = [[(0, 0), (0, 1), (0, 2), (0, 3)], [(1, 1), (1, 2), (1, 3), (3, 3)], [(2, 2), (2, 3)]]
UNIT_PT = [0, PT_AT[1], PT_AT[2]]


def wait(eng, sem, value):
    if isinstance(value, int) and value <= 0:
        return
    eng.wait_ge(sem, value)


def ln_stats(nc, dve, s, pre, t, src, stats, mv, var_eps):
    k = t % 2
    nc.vector.bn_stats(stats[:, k, :], src).then_inc(s[pre + "stat_done"], 1)
    dve.wait_ge(s[pre + "stat_done"], t + 1)
    wait(dve, s[pre + "norm_done"], t - 1)
    nc.vector.bn_aggr(mv[:, k, :], stats[:, k, :]).then_inc(s[pre + "aggr_done"], 1)
    dve.wait_ge(s[pre + "aggr_done"], t + 1)
    nc.vector.tensor_scalar(var_eps[:, k:k + 1], mv[:, k, 1:2], EPS, None, ALU.add).then_inc(s[pre + "eps_done"], 1)


def ln_rstd(nc, pool, s, pre, t, var_eps, half, rstd):
    k = t % 2
    pool.wait_ge(s[pre + "eps_done"], t + 1)
    nc.gpsimd.tensor_tensor(rstd[:, k:k + 1], var_eps[:, k:k + 1], half[:, :], ALU.pow).then_inc(s[pre + "rstd_done"], 1)


def ln_norm(nc, dve, s, pre, t, src, dst, mv, rstd):
    k = t % 2
    dve.wait_ge(s[pre + "rstd_done"], t + 1)
    nc.vector.tensor_scalar(dst, src, mv[:, k, 0:1], rstd[:, k:k + 1], ALU.subtract, ALU.mult).then_inc(s[pre + "norm_done"], 1)


def decoder_layer(nc, x, ctx, mem_mask, wq, wk, wv, wo, router_w, router_b, gu_w, gu_b, down_w, down_b,
                  cos_t, sin_t, causal_t, ident_t, iota_t, out):
    stack = ExitStack()
    with stack:
        def sb(name, shape, dt=F32):
            return stack.enter_context(nc.sbuf_tensor(name, shape, dt))

        def sem(name):
            return stack.enter_context(nc.semaphore(name))

        x_res = sb("x_res", [P, TT, D])
        xn = [sb("xn_hi", [P, DC, T], F32R), sb("xn_lo", [P, DC, T], F32R)]
        ident = sb("ident", [P, P])
        stats = sb("stats", [P, 2, 6])
        mv = sb("mv", [P, 2, 2])
        var_eps = sb("var_eps", [P, 2])
        half = sb("half", [P, 1])
        rstd = sb("rstd", [P, 2])

        bank = [stack.enter_context(nc.psum_tensor(f"bank{i}", [P, 512], F32)) for i in range(8)]
        xr = x.rearrange("b (t p) d -> p (b t) d", p=P)
        outr = out.rearrange("b (t p) d -> p (b t) d", p=P)

        attn = ExitStack()

        def sa(name, shape, dt=F32):
            return attn.enter_context(nc.sbuf_tensor(name, shape, dt))

        w1_raw = sa("w1_raw", [P, 3, D])
        w2_raw = sa("w2_raw", [P, DC, G * HD])
        w1 = [sa("w1_hi", [P, DC, 3 * P], F32R), sa("w1_lo", [P, DC, 3 * P], F32R)]
        w2 = [sa("w2_hi", [P, 2, D], F32R), sa("w2_lo", [P, 2, D], F32R)]
        cos = sa("cos", [P, L])
        sin = sa("sin", [P, L])
        causal = sa("causal", [P, L])
        probs = sa("probs", [P, 2, P_LEN])
        pt = [[sa(f"pt{b}_hi", [P, PT_LEN], F32R), sa(f"pt{b}_lo", [P, PT_LEN], F32R)] for b in range(2)]
        q_st = sa("q_st", [P, G, L], F32R)
        k_hi = sa("k_hi", [P, 2, L], F32R)
        k_lo = sa("k_lo", [P, 2, L], F32R)
        v_t = sa("v_t", [HD, L])
        v_st = sa("v_st", [P, 2, QB, P], F32R)
        rot = sa("rot", [P, L])
        rope = sa("rope", [P, L])
        o_part = sa("o_part", [HD, L])
        o_f = sa("o_f", [P, L])
        o_st = [sa("o_hi", [P, 2, L], F32R), sa("o_lo", [P, 2, L], F32R)]
        row_max = sa("row_max", [P, 2, QB])
        neg_max = sa("neg_max", [P, 2, QB])
        row_sum = sa("row_sum", [P, 2, QB])
        row_inv = sa("row_inv", [P, 2, QB])
        ln_out = probs

        S_BANK, T_BANK, O_BANK, PJ_BANK, WO_BANK = bank[0:3], bank[3:5], bank[5], bank[6], bank[7]

        s = {name: sem(name) for name in (
            "const_in", "ident_in", "x_in0", "x_in1", "x_in2", "x_in3", "zero_done", "stat_done", "aggr_done", "eps_done", "half_done", "rstd_done", "norm_done", "lnt_done",
            "ln_hi", "ln_lo", "w1_in", "w2_in", "w1_tr", "w1_hi_done", "w1_lo_done", "w2_tr", "w2_hi_done",
            "w2_lo_done", "proj_done", "vt_done", "rope_in", "rot_sin", "rope_sum", "rope_hi", "rope_lo",
            "v_tr", "v_hi_done", "v_lo_done", "scores_done", "masked_done", "negmax_done", "exp_done",
            "recip_done", "pnorm_done", "ptrans_done", "pt_hi_done", "pt_lo_done", "pv_done", "opart_done",
            "oadd_done", "o_hi_done", "o_lo_done", "wo_done", "woacc_done")}

        def settled(eng):
            eng.nop(nofuse=True)

        def pe_ln(pe, t):
            pe.wait_ge(s["norm_done"], t + 1)
            wait(pe, s["ln_lo"], t - 3)
            for c in range(DC):
                last = nc.tensor.transpose(bank[t % 4][:, c * P:(c + 1) * P], ln_out[:, t % 2, c * P:(c + 1) * P], ident[:, :])
            last.then_inc(s["lnt_done"], 1)

        def pe_w1(pe, g, bank_free):
            pe.wait_ge(s["w1_in"], 48 * g + 48)
            for r in range(3):
                if bank_free[r]:
                    wait(pe, *bank_free[r])
                else:
                    pe.wait_ge(s["w1_lo_done"], 3 * g + r - 1)
                for c in range(DC):
                    last = nc.tensor.transpose((PJ_BANK, WO_BANK)[r % 2][:, c * P:(c + 1) * P], w1_raw[:, r, c * P:(c + 1) * P], ident[:, :])
                last.then_inc(s["w1_tr"], 1)

        def pe_w2(pe, g, bank_free):
            pe.wait_ge(s["w2_in"], 16 * g + 16)
            for k in range(2):
                wait(pe, *bank_free[k])
                for c in range(DC):
                    last = nc.tensor.transpose((PJ_BANK, WO_BANK)[k][:, c * P:(c + 1) * P], w2_raw[:, c, k * P:(k + 1) * P], ident[:, :])
                last.then_inc(s["w2_tr"], 1)

        def pe_proj(pe, b, r):
            first = True
            for c in range(DC):
                for sp, mp in PASSES:
                    last = nc.tensor.matmul(PJ_BANK[:, :], w1[sp][:, c, r * P:(r + 1) * P], xn[mp][:, c, b * L:(b + 1) * L],
                                            start=first, stop=(c == DC - 1 and (sp, mp) == PASSES[-1]))
                    first = False
            last.then_inc(s["proj_done"], 1)

        def pe_vt(pe, m):
            pe.wait_ge(s["vt_done"], m + 1)
            settled(pe)
            for j in range(QB):
                last = nc.tensor.transpose(PJ_BANK[:, j * HD:(j + 1) * HD], v_t[:, j * P:(j + 1) * P], ident[0:HD, 0:HD])
            last.then_inc(s["v_tr"], 1)

        def pe_scores(pe, n, m, h, kb):
            pe.wait_ge(s["rope_lo"], 3 * m + 2 + (h >= 2))
            for k, blocks in enumerate(((3,), (2,), (1, 0))):
                wait(pe, s["masked_done"], 3 * n - 2 + k)
                for i in blocks:
                    cols = P * (i + 1) if i else 2 * P
                    at = 2 * P if i == 0 else 0
                    for a, kk in enumerate((k_hi, k_lo)):
                        last = nc.tensor.matmul(S_BANK[k][:, at:at + cols], q_st[:, h, i * P:(i + 1) * P], kk[:, kb, 0:cols],
                                                start=(a == 0), stop=(a == 1))
                last.then_inc(s["scores_done"], 1)

        def pe_ptrans(pe, n, hb, u):
            if u == 0:
                pe.wait_ge(s["pnorm_done"], 4 * n + 4)
            wait(pe, s["pt_lo_done"], 3 * n + (0, 0, 1)[u])
            for k, (j, i) in enumerate(UNITS[u]):
                last = nc.tensor.transpose(T_BANK[u % 2][:, k * P:(k + 1) * P],
                                           probs[:, hb, P_AT[i] + j * P:P_AT[i] + (j + 1) * P], ident[:, :])
            last.then_inc(s["ptrans_done"], 1)

        def pe_pv(pe, n, m, hb, vb):
            pe.wait_ge(s["pt_lo_done"], 3 * n + 3)
            pe.wait_ge(s["v_lo_done"], m + 1)
            wait(pe, s["oadd_done"], n)
            for j in range(QB):
                for a in range(2):
                    if j == 3:
                        rhs = pt[hb][a][:, PT_ZERO:PT_ZERO + 8 * P].rearrange("p (z c) -> p z c", z=2)[:, :, 0:P]
                        dst = O_BANK[:, 2 * P:4 * P].rearrange("p (z c) -> p z c", z=2)
                    else:
                        rhs = pt[hb][a][:, PT_AT[j]:PT_AT[j] + (QB - j) * P]
                        dst = O_BANK[:, j * P:4 * P]
                    last = nc.tensor.matmul(dst, v_st[:, vb, j, :], rhs, start=(j == 0 and a == 0), stop=(j == QB - 1 and a == 1))
            last.then_inc(s["pv_done"], 1)

        def pe_wo(pe, m, t):
            pe.wait_ge(s["o_lo_done"], 2 * m + 2)
            wait(pe, s["woacc_done"], 4 * m + t)
            first = True
            for k in range(2):
                for sp, mp in PASSES:
                    last = nc.tensor.matmul(WO_BANK[:, :], o_st[sp][:, k, t * P:(t + 1) * P], w2[mp][:, k, :],
                                            start=first, stop=(k == 1 and (sp, mp) == PASSES[-1]))
                    first = False
            last.then_inc(s["wo_done"], 1)

        def pe_group(pe, g):
            for c in range(HEADS):
                b, h = divmod(c, G)
                n, m = HEADS * g + c, B * g + b
                nx = c + 1
                begun = not (isinstance(g, int) and g == 0 and c == 0)
                more = not (isinstance(g, int) and g == GROUPS - 1 and c == HEADS - 1)
                next_batch = not (isinstance(g, int) and g == GROUPS - 1 and b == B - 1)
                last_batch = not (isinstance(g, int) and g == 0 and b == 0)
                if more:
                    pe_scores(pe, n + 1, m + nx // G - b if nx % G == 0 else m, nx % G, (nx // G) % 2)
                if h == 0 and next_batch:
                    if b == 1:
                        pe.wait_ge(s["w2_lo_done"], 2 * g + 1)
                    elif b == 3:
                        pe.wait_ge(s["w1_lo_done"], 3 * g + 6)
                    else:
                        pe.wait_ge(s["v_lo_done"], m + 1)
                    pe_proj(pe, (b + 1) % B, 2)
                if h == 1:
                    if next_batch:
                        pe.wait_ge(s["rope_in"], 3 * m + 4)
                        pe_proj(pe, (b + 1) % B, 0)
                    if last_batch:
                        if b == 1:
                            pe.wait_ge(s["w2_lo_done"], 2 * g + 2)
                        elif b == 3 and not (isinstance(g, int) and g == GROUPS - 1):
                            pe.wait_ge(s["w1_lo_done"], 3 * g + 5)
                        pe_wo(pe, m - 1, 0)
                if h == 2:
                    if last_batch:
                        pe_wo(pe, m - 1, 3)
                    if next_batch:
                        pe.wait_ge(s["rope_in"], 3 * m + 5)
                        pe_proj(pe, (b + 1) % B, 1)
                if h == 3:
                    if next_batch:
                        pe.wait_ge(s["rope_in"], 3 * m + 6)
                        pe_vt(pe, m + 1)
                    if b == 0:
                        pe_w2(pe, g, ((s["v_lo_done"], m + 2), (s["woacc_done"], 4 * m)))
                    if b == 2 and next_batch and not (isinstance(g, int) and g == GROUPS - 1):
                        pe_w1(pe, g + 1, ((s["v_lo_done"], m + 2), (s["woacc_done"], 4 * m), None))
                pe_ptrans(pe, n, c % 2, 0)
                pe_ptrans(pe, n, c % 2, 1)
                if h == 1 and last_batch:
                    pe_wo(pe, m - 1, 1)
                if begun:
                    pe_pv(pe, n - 1, m if h else m - 1, (c + 1) % 2, (b if h else b + 1) % 2)
                if h == 1 and last_batch:
                    pe_wo(pe, m - 1, 2)
                pe_ptrans(pe, n, c % 2, 2)

        def act_split(dst, src, sem_):
            nc.scalar.activation(dst, src, ACT.Copy).then_inc(sem_, 1)

        def act_exp(act, n, hb):
            act.wait_ge(s["negmax_done"], n + 1)
            for i in (3, 2, 1, 0):
                row = probs[:, hb, P_AT[i]:P_AT[i] + (i + 1) * P]
                nc.scalar.activation(row, row, ACT.Exp, bias=neg_max[:, hb, i:i + 1], scale=HD ** -0.5,
                                     accum_out=row_sum[:, hb, i:i + 1]).then_inc(s["exp_done"], 1)

        def act_rope(act, m, r, mb):
            act.wait_ge(s["rope_sum"], 3 * m + r + 1)
            if r == 0:
                wait(act, s["scores_done"], 12 * m - 12)
                act_split(k_hi[0:HD, mb, :], rope[0:HD, :], s["rope_hi"])
                act_split(k_hi[HD:P, mb, :], rope[0:HD, :], s["rope_hi"])
            else:
                wait(act, s["scores_done"], 12 * m - 12 + 6 * r)
                act_split(q_st[0:HD, 2 * r - 2, :], rope[0:HD, :], s["rope_hi"])
                act_split(q_st[HD:P, 2 * r - 1, :], rope[HD:P, :], s["rope_hi"])

        def act_vt(act, m, r_sem_value):
            act.wait_ge(s["proj_done"], r_sem_value)
            wait(act, s["v_tr"], m)
            act_split(v_t[:, :], PJ_BANK[HD:P, :], s["vt_done"])

        def act_v(act, m, vb):
            act.wait_ge(s["v_tr"], m + 1)
            wait(act, s["pv_done"], 4 * m - 4)
            act_split(v_st[:, vb, :, 0:HD], PJ_BANK[:, 0:QB * HD].rearrange("p (j d) -> p j d", j=QB), s["v_hi_done"])

        def act_w1(act, g):
            wait(act, s["proj_done"], 12 * g)
            for r in range(3):
                act.wait_ge(s["w1_tr"], 3 * g + r + 1)
                act_split(w1[0][:, :, r * P:(r + 1) * P], (PJ_BANK, WO_BANK)[r % 2][:, :].rearrange("p (c n) -> p c n", c=DC), s["w1_hi_done"])

        def act_w2(act, g):
            wait(act, s["wo_done"], 16 * g)
            for k in range(2):
                act.wait_ge(s["w2_tr"], 2 * g + k + 1)
                act_split(w2[0][:, k, :], (PJ_BANK, WO_BANK)[k][:, :], s["w2_hi_done"])

        def act_pt(act, n, hb, u):
            act.wait_ge(s["ptrans_done"], 3 * n + u + 1)
            if u == 0:
                wait(act, s["pv_done"], n - 1)
            w = P * len(UNITS[u])
            act_split(pt[hb][0][:, UNIT_PT[u]:UNIT_PT[u] + w], T_BANK[u % 2][:, 0:w], s["pt_hi_done"])

        def act_opart(act, n):
            act.wait_ge(s["pv_done"], n + 1)
            wait(act, s["oadd_done"], n)
            act_split(o_part[:, :], O_BANK[HD:P, :], s["opart_done"])

        def act_o(act, n, m, k):
            act.wait_ge(s["oadd_done"], n + 1)
            wait(act, s["wo_done"], 4 * m)
            act_split(o_st[0][:, k, :], o_f[:, :], s["o_hi_done"])

        def act_group(act, g):
            for c in range(HEADS):
                b, h = divmod(c, G)
                n, m = HEADS * g + c, B * g + b
                begun = not (isinstance(g, int) and g == 0 and c == 0)
                more = not (isinstance(g, int) and g == GROUPS - 1 and c == HEADS - 1)
                next_batch = not (isinstance(g, int) and g == GROUPS - 1 and b == B - 1)
                if more:
                    act_exp(act, n + 1, (c + 1) % 2)
                if next_batch:
                    if h:
                        act_rope(act, m + 1, h - 1, (b + 1) % 2)
                    else:
                        act_vt(act, m + 1, 3 * m + 4)
                    if h == 3:
                        act_v(act, m + 1, (b + 1) % 2)
                if h == 3 and b == 0:
                    act_w2(act, g)
                if h == 3 and b == 2 and not (isinstance(g, int) and g == GROUPS - 1):
                    act_w1(act, g + 1)
                act_pt(act, n, c % 2, 0)
                act_pt(act, n, c % 2, 1)
                if begun:
                    act_opart(act, n - 1)
                    if h == 2:
                        act_o(act, n - 1, m, 0)
                    if h == 0:
                        act_o(act, n - 1, m - 1, 1)
                act_pt(act, n, c % 2, 2)

        def dve_lo(dst, src, hi, sem_):
            nc.vector.tensor_tensor(dst, src, hi.bitcast(F32), ALU.subtract).then_inc(sem_, 1)

        def dve_masked(dve, n, hb):
            wait(dve, s["ptrans_done"], 3 * n - 3)
            for i in (3, 2, 1, 0):
                k = (2, 2, 1, 0)[i]
                if i:
                    dve.wait_ge(s["scores_done"], 3 * n + k + 1)
                    settled(dve)
                at = 2 * P if i == 0 else 0
                done = nc.vector.tensor_tensor_reduce(
                    out=probs[:, hb, P_AT[i]:P_AT[i] + (i + 1) * P], in0=S_BANK[k][:, at:at + (i + 1) * P],
                    in1=causal[:, (QB - 1 - i) * P:L], scale=1.0, scalar=NEG, op0=ALU.add, op1=ALU.max,
                    accum_out=row_max[:, hb, i:i + 1])
                if i != 1:
                    done.then_inc(s["masked_done"], 1)
            dve.wait_ge(s["masked_done"], 3 * n + 3)
            nc.vector.tensor_scalar(neg_max[:, hb, :], row_max[:, hb, :], -HD ** -0.5, None, ALU.mult).then_inc(s["negmax_done"], 1)

        def dve_recip(dve, n, hb):
            dve.wait_ge(s["exp_done"], 4 * n + 4)
            nc.vector.reciprocal(row_inv[:, hb, :], row_sum[:, hb, :]).then_inc(s["recip_done"], 1)

        def dve_rope_in(dve, m, r):
            dve.wait_ge(s["proj_done"], 3 * m + r + 1)
            wait(dve, s["rope_lo"], 3 * m + r)
            rows = HD if r == 0 else P
            if r == 0:
                dve.wait_ge(s["vt_done"], m + 1)
            nc.vector.tensor_tensor(rope[0:rows, :], PJ_BANK[0:rows, :], cos[0:rows, :], ALU.mult)
            nc.vector.stream_shuffle(rot[0:rows, :], PJ_BANK[0:rows, :], [p ^ 1 for p in range(32)]).then_inc(s["rope_in"], 1)

        def dve_rope_lo(dve, m, r, mb):
            dve.wait_ge(s["rope_hi"], 6 * m + 2 * r + 2)
            if r == 0:
                hi = k_hi[0:HD, mb, :].bitcast(F32)
                nc.vector.tensor_tensor(k_lo[0:HD, mb, :], rope[0:HD, :], hi, ALU.subtract)
                nc.vector.tensor_tensor(k_lo[HD:P, mb, :], rope[0:HD, :], hi, ALU.subtract).then_inc(s["rope_lo"], 1)
            else:
                a, c = 2 * r - 2, 2 * r - 1
                nc.vector.tensor_tensor(q_st[HD:P, a, :], rope[0:HD, :], q_st[0:HD, a, :].bitcast(F32), ALU.subtract)
                nc.vector.tensor_tensor(q_st[0:HD, c, :], rope[HD:P, :], q_st[HD:P, c, :].bitcast(F32), ALU.subtract).then_inc(s["rope_lo"], 1)

        def dve_v(dve, m, vb):
            dve.wait_ge(s["v_hi_done"], m + 1)
            dve_lo(v_st[:, vb, :, HD:P], PJ_BANK[:, 0:QB * HD].rearrange("p (j d) -> p j d", j=QB), v_st[:, vb, :, 0:HD], s["v_lo_done"])

        def dve_w1(dve, g):
            for r in range(3):
                dve.wait_ge(s["w1_hi_done"], 3 * g + r + 1)
                dve_lo(w1[1][:, :, r * P:(r + 1) * P], (PJ_BANK, WO_BANK)[r % 2][:, :].rearrange("p (c n) -> p c n", c=DC),
                       w1[0][:, :, r * P:(r + 1) * P], s["w1_lo_done"])

        def dve_w2(dve, g):
            for k in range(2):
                dve.wait_ge(s["w2_hi_done"], 2 * g + k + 1)
                dve_lo(w2[1][:, k, :], (PJ_BANK, WO_BANK)[k][:, :], w2[0][:, k, :], s["w2_lo_done"])

        def dve_pt(dve, n, hb, u):
            dve.wait_ge(s["pt_hi_done"], 3 * n + u + 1)
            w = P * len(UNITS[u])
            dve_lo(pt[hb][1][:, UNIT_PT[u]:UNIT_PT[u] + w], T_BANK[u % 2][:, 0:w], pt[hb][0][:, UNIT_PT[u]:UNIT_PT[u] + w], s["pt_lo_done"])

        def dve_oadd(dve, n, odd, pairs_before):
            dve.wait_ge(s["opart_done"], n + 1)
            wait(dve, s["o_lo_done"], pairs_before)
            r = HD if odd else 0
            nc.vector.tensor_tensor(o_f[r:r + HD, :], O_BANK[0:HD, :], o_part[:, :], ALU.add).then_inc(s["oadd_done"], 1)

        def dve_o(dve, pair, k):
            dve.wait_ge(s["o_hi_done"], pair + 1)
            dve_lo(o_st[1][:, k, :], o_f[:, :], o_st[0][:, k, :], s["o_lo_done"])

        def dve_woacc(dve, m, b, t):
            dve.wait_ge(s["wo_done"], 4 * m + t + 1)
            wait(dve, s["woacc_done"], 4 * m + t)
            tile = x_res[:, b * QB + t, :]
            nc.vector.tensor_tensor(tile, WO_BANK[:, :], tile, ALU.add).then_inc(s["woacc_done"], 1)

        def dve_group(dve, g):
            for c in range(HEADS):
                b, h = divmod(c, G)
                n, m = HEADS * g + c, B * g + b
                begun = not (isinstance(g, int) and g == 0 and c == 0)
                more = not (isinstance(g, int) and g == GROUPS - 1 and c == HEADS - 1)
                next_batch = not (isinstance(g, int) and g == GROUPS - 1 and b == B - 1)
                last_batch = not (isinstance(g, int) and g == 0 and b == 0)
                if more:
                    dve_masked(dve, n + 1, (c + 1) % 2)
                if h and next_batch:
                    dve_rope_lo(dve, m + 1, h - 1, (b + 1) % 2)
                if h == 2 and last_batch:
                    dve_woacc(dve, m - 1, (b - 1) % B, 3)
                if h < 3 and next_batch:
                    dve_rope_in(dve, m + 1, h)
                if h == 1 and last_batch:
                    dve_woacc(dve, m - 1, (b - 1) % B, 0)
                if h == 3 and next_batch:
                    dve_v(dve, m + 1, (b + 1) % 2)
                if h == 3 and b == 0:
                    dve_w2(dve, g)
                if h == 3 and b == 2 and not (isinstance(g, int) and g == GROUPS - 1):
                    dve_w1(dve, g + 1)
                if more:
                    dve_recip(dve, n + 1, (c + 1) % 2)
                dve_pt(dve, n, c % 2, 0)
                dve_pt(dve, n, c % 2, 1)
                if h == 1 and last_batch:
                    dve_woacc(dve, m - 1, (b - 1) % B, 1)
                if begun:
                    dve_oadd(dve, n - 1, (c - 1) % 2, HEADS // 2 * g + ((c - 1) // 2 if c else -1))
                    if h % 2 == 0:
                        dve_o(dve, HEADS // 2 * g + (c // 2 - 1), (c // 2 - 1) % 2)
                if h == 1 and last_batch:
                    dve_woacc(dve, m - 1, (b - 1) % B, 2)
                dve_pt(dve, n, c % 2, 2)

        def pool_rope(pool, m, r):
            pool.wait_ge(s["rope_in"], 3 * m + r + 1)
            rows = HD if r == 0 else P
            nc.gpsimd.tensor_tensor(rot[0:rows, :], rot[0:rows, :], sin[0:rows, :], ALU.mult).then_inc(s["rot_sin"], 1)
            pool.wait_ge(s["rot_sin"], 3 * m + r + 1)
            nc.gpsimd.tensor_tensor(rope[0:rows, :], rope[0:rows, :], rot[0:rows, :], ALU.add).then_inc(s["rope_sum"], 1)

        def pool_norm(pool, n, hb):
            pool.wait_ge(s["recip_done"], n + 1)
            settled(pool)
            for i in (3, 2, 1, 0):
                row = probs[:, hb, P_AT[i]:P_AT[i] + (i + 1) * P]
                nc.gpsimd.tensor_scalar(row, row, row_inv[:, hb, i:i + 1], 0.0, ALU.mult, ALU.add).then_inc(s["pnorm_done"], 1)

        def pool_group(pool, g):
            for c in range(HEADS):
                b, h = divmod(c, G)
                n, m = HEADS * g + c, B * g + b
                if h < 3 and not (isinstance(g, int) and g == GROUPS - 1 and b == B - 1):
                    pool_rope(pool, m + 1, h)
                if not (isinstance(g, int) and g == GROUPS - 1 and c == HEADS - 1):
                    pool_norm(pool, n + 1, (c + 1) % 2)

        def sp_w1(sp, g):
            wait(sp, s["w1_tr"], 3 * g)
            if not isinstance(g, int):
                settled(sp)
            sp.dma_start(w1_raw[:, 0:2, :], wq[bass.ds(g * G * HD, G * HD), :].rearrange("(r p) d -> p r d", p=P)).then_inc(s["w1_in"], 16)
            sp.dma_start(w1_raw[0:HD, 2, :], wk[bass.ds(g * HD, HD), :]).then_inc(s["w1_in"], 16)
            sp.dma_start(w1_raw[HD:P, 2, :], wv[bass.ds(g * HD, HD), :]).then_inc(s["w1_in"], 16)

        def sp_w2(sp, g):
            wait(sp, s["w2_tr"], 2 * g)
            if not isinstance(g, int):
                settled(sp)
            sp.dma_start(w2_raw[:, :, :], wo[:, bass.ds(g * G * HD, G * HD)].rearrange("(c p) n -> p c n", p=P)).then_inc(s["w2_in"], 16)

        with nc.Block() as block:

            @block.sync
            def _(sp):
                for b in range(B):
                    sp.dma_start(x_res[:, b * QB:(b + 1) * QB, :], xr[:, b * QB:(b + 1) * QB, :]).then_inc(s[f"x_in{b}"], 16)
                    if b == 0:
                        sp_w1(sp, 0)
                        sp.dma_start(cos[:, :], cos_t).then_inc(s["const_in"], 16)
                        sp.dma_start(sin[:, :], sin_t).then_inc(s["const_in"], 16)
                        sp.dma_start(causal[:, :], causal_t).then_inc(s["const_in"], 16)
                sp_w2(sp, 0)
                with sp.Fori(1, GROUPS) as g:
                    sp_w1(sp, g)
                    sp_w2(sp, g)

            @block.tensor
            def _(pe):
                pe.wait_ge(s["ident_in"], 16)
                pe.wait_ge(s["zero_done"], 4)
                for t in range(4):
                    pe_ln(pe, t)
                pe_w1(pe, 0, ((s["w1_lo_done"], 0), (s["w1_lo_done"], 0), None))
                for t in range(4, TT):
                    pe_ln(pe, t)
                pe.wait_ge(s["w1_lo_done"], 3)
                pe.wait_ge(s["ln_lo"], TT)
                pe_proj(pe, 0, 2)
                for r in range(2):
                    pe.wait_ge(s["rope_in"], r + 1)
                    pe_proj(pe, 0, r)
                pe.wait_ge(s["rope_in"], 3)
                pe_vt(pe, 0)
                pe_scores(pe, 0, 0, 0, 0)
                pe_group(pe, 0)
                with pe.Fori(1, GROUPS - 1) as g:
                    pe_group(pe, g)
                pe_group(pe, GROUPS - 1)
                pe_pv(pe, HEADS * GROUPS - 1, B * GROUPS - 1, 1, 1)
                for t in range(QB):
                    pe_wo(pe, B * GROUPS - 1, t)

            @block.scalar
            def _(act):
                act.dma_start(ident[:, :], ident_t).then_inc(s["ident_in"], 16)

                def ln_hi(t):
                    act.wait_ge(s["lnt_done"], t + 1)
                    act_split(xn[0][:, :, t * P:(t + 1) * P], bank[t % 4][:, :].rearrange("p (c n) -> p c n", c=DC), s["ln_hi"])

                for t in range(4):
                    ln_hi(t)
                act_w1(act, 0)
                for t in range(4, TT):
                    ln_hi(t)
                act_vt(act, 0, 1)
                for r in range(3):
                    act_rope(act, 0, r, 0)
                act_v(act, 0, 0)
                act_exp(act, 0, 0)
                act_group(act, 0)
                with act.Fori(1, GROUPS - 1) as g:
                    act_group(act, g)
                act_group(act, GROUPS - 1)
                act_opart(act, HEADS * GROUPS - 1)
                act_o(act, HEADS * GROUPS - 1, B * GROUPS - 1, 1)

            @block.vector
            def _(dve):
                for hb in range(2):
                    for a in range(2):
                        nc.vector.memset(pt[hb][a][:, PT_ZERO:PT_ZERO + P].bitcast(F32), 0.0).then_inc(s["zero_done"], 1)

                def ln_lo(t):
                    dve.wait_ge(s["ln_hi"], t + 1)
                    dve_lo(xn[1][:, :, t * P:(t + 1) * P], bank[t % 4][:, :].rearrange("p (c n) -> p c n", c=DC),
                           xn[0][:, :, t * P:(t + 1) * P], s["ln_lo"])

                for t in range(TT + 1):
                    if t < TT:
                        dve.wait_ge(s[f"x_in{t // QB}"], 16)
                        ln_stats(nc, dve, s, "", t, x_res[:, t, :], stats, mv, var_eps)
                    if t >= 1:
                        wait(dve, s["lnt_done"], t - 2)
                        ln_norm(nc, dve, s, "", t - 1, x_res[:, t - 1, :], ln_out[:, (t - 1) % 2, 0:D], mv, rstd)
                    if t >= 3:
                        ln_lo(t - 3)
                    if t == 6:
                        dve_w1(dve, 0)
                ln_lo(TT - 2)
                ln_lo(TT - 1)
                dve.wait_ge(s["const_in"], 48)
                dve_rope_in(dve, 0, 0)
                for r in range(3):
                    dve_rope_lo(dve, 0, r, 0)
                    if r < 2:
                        dve_rope_in(dve, 0, r + 1)
                dve_v(dve, 0, 0)
                dve_masked(dve, 0, 0)
                dve_recip(dve, 0, 0)
                dve_group(dve, 0)
                with dve.Fori(1, GROUPS - 1) as g:
                    dve_group(dve, g)
                dve_group(dve, GROUPS - 1)
                dve_oadd(dve, HEADS * GROUPS - 1, 1, HEADS * GROUPS // 2 - 1)
                dve_o(dve, HEADS * GROUPS // 2 - 1, 1)
                for t in range(QB):
                    dve_woacc(dve, B * GROUPS - 1, B - 1, t)

            @block.gpsimd
            def _(pool):
                nc.gpsimd.memset(half[:, :], -0.5).then_inc(s["half_done"], 1)
                pool.wait_ge(s["half_done"], 1)
                for t in range(TT):
                    ln_rstd(nc, pool, s, "", t, var_eps, half, rstd)
                pool.wait_ge(s["const_in"], 48)
                for r in range(3):
                    pool_rope(pool, 0, r)
                pool_norm(pool, 0, 0)
                pool_group(pool, 0)
                with pool.Fori(1, GROUPS - 1) as g:
                    pool_group(pool, g)
                pool_group(pool, GROUPS - 1)

        attn.close()

        def st(name, shape, dt=F32):
            return stack.enter_context(nc.sbuf_tensor(name, shape, dt))

        ctx_raw = st("ctx_raw", [P, B, D])
        ctx_hi = st("ctx_hi", [P, B, D], F32R)
        ctx_lo = st("ctx_lo", [P, B, D], F32R)
        ctx_t = st("ctx_t", [P, B, DC, MEM])
        mask_u8 = st("mask_u8", [P, B * MEM], U8)
        mask_f = st("mask_f", [P, B, MEM])
        mask_scale = st("mask_scale", [P, B, MEM])
        mask_add = st("mask_add", [P, B, MEM])
        valid = st("valid", [P, B])
        ln_t = st("ln_t", [P, 2, D])
        ln_h = st("ln_h", [P, 2, D])
        xt = st("xt", [P, DC, P])
        mv_h = st("mv_h", [P, 2, 2])
        var_eps_h = st("var_eps_h", [P, 2])
        rstd_h = st("rstd_h", [P, 2])
        stats_h = st("stats_h", [P, 2, 6])
        m_sc = st("m_sc", [P, MEM])
        m_neg = st("m_neg", [P, 3])
        m_inv = st("m_inv", [P, 2])
        a_st = st("a_st", [P, P], F32R)
        rw_raw = st("rw_raw", [E, D])
        rw_t = st("rw_t", [P, DC, 2 * E], F32R)
        rb = st("rb", [P, E])
        iota = st("iota", [P, E])
        logits = st("logits", [P, 2, E])
        top = st("top", [P, 8])
        top_at = st("top_at", [P, 8], U32)
        top_f = st("top_f", [P, 2])
        gate2 = st("gate2", [P, 6])
        pick = st("pick", [P, 2, E])
        share = st("share", [P, TT, E])
        share_e = st("share_e", [P, TT, 1])
        share_t = st("share_t", [E, P])
        down_bias = st("down_bias", [E, D])
        gu_raw = st("gu_raw", [P, 2, DC, 2 * P])
        dn_raw = st("dn_raw", [P, 2, D])
        bias_raw = st("bias_raw", [P, 2, 2])
        gu = [st("gu_hi", [P, 2, DC, 2, P], F32R), st("gu_lo", [P, 2, DC, 2, P], F32R)]
        dn = [st("dn_hi", [P, 2, D], F32R), st("dn_lo", [P, 2, D], F32R)]
        bias = st("bias", [P, 2, 2])
        gate = st("gate", [P, 2, L])
        up = st("up", [P, 2, L])
        sig = st("sig", [P, 2, L])
        act_st = [st("act_hi", [P, 2, L], F32R), st("act_lo", [P, 2, L], F32R)]

        names2 = []
        for pre in ("m_", "h_"):
            names2 += [pre + e for e in ("stat_done", "aggr_done", "eps_done", "rstd_done", "norm_done")]
        names2 += ["mem_in", "mask_in", "rw_in", "small_in", "bd_in", "ctx_hi_done", "ctx_lo_done", "ctx_tr", "ctx_t_done",
                   "mask_f_done", "mask_tab", "rw_tr", "rw_hi_done", "rw_lo_done",
                   "mt_tr", "mt_done", "msc_done", "m1", "m2", "m3", "mexp_done", "msum_inv", "m_inv_done", "at_tr", "at_hi", "at_lo",
                   "read_done", "x_mem", "ht_tr", "ht_hi", "ht_lo", "log_done", "l1", "l2", "top_done", "topi_done", "diff_done",
                   "gexp_done", "g1", "g2", "g3", "topf_done", "p1", "share_done", "st_tr", "st_done", "bias_mm", "x_bias",
                   "share_e_done",
                   "gu_in0", "gu_in1", "gu_hi_done", "gu_lo_done", "dn_hi_done", "dn_lo_done", "bias_done", "gu_mm", "gate_done", "up_done",
                   "sig_done", "glu_done", "act_done", "ah_done", "al_done", "dn_mm", "x_moe", "out_done"]
        z = {name: sem("z_" + name) for name in names2}
        UNITS_E = E * IB
        STEPS = IB * B

        def pe_setup2(pe):
            pe.wait_ge(z["mem_in"], 32)
            for b in range(B):
                for c in range(DC):
                    last = nc.tensor.transpose(bank[b % 2][:, 2 * P * (b // 2) + c * MEM:2 * P * (b // 2) + (c + 1) * MEM],
                                               ctx_raw[0:MEM, b, c * P:(c + 1) * P], ident[0:MEM, 0:MEM])
            last.then_inc(z["ctx_tr"], 1)
            pe.wait_ge(z["rw_in"], 16)
            for c in range(DC):
                last = nc.tensor.transpose(bank[2][:, c * E:(c + 1) * E], rw_raw[:, c * P:(c + 1) * P], ident[0:E, 0:E])
            last.then_inc(z["rw_tr"], 1)

        M_TR, M_SC, A_TR, A_OUT, H_TR, H_LOG, S_TR, S_OUT = bank

        def pe_a(pe, t):
            b = t // QB
            pe.wait_ge(z["m_norm_done"], t + 1)
            wait(pe, z["mt_done"], t)
            for c in range(DC):
                last = nc.tensor.transpose(M_TR[:, c * P:(c + 1) * P], ln_t[:, t % 2, c * P:(c + 1) * P], ident[:, :])
            last.then_inc(z["mt_tr"], 1)
            pe.wait_ge(z["mt_done"], t + 1)
            wait(pe, z["m1"], t)
            for c in range(DC):
                last = nc.tensor.matmul(M_SC[:, 0:MEM], xt[:, c, :], ctx_t[:, b, c, :], start=(c == 0), stop=(c == DC - 1))
            last.then_inc(z["msc_done"], 1)

        def pe_b(pe, t):
            b = t // QB
            pe.wait_ge(z["mexp_done"], t + 1)
            wait(pe, z["at_lo"], t)
            nc.tensor.transpose(A_TR[0:MEM, 0:P], m_sc[:, :], ident[:, :]).then_inc(z["at_tr"], 1)
            pe.wait_ge(z["at_lo"], t + 1)
            wait(pe, z["x_mem"], t)
            nc.tensor.matmul(A_OUT[:, :], a_st[:, :], ctx_hi[:, b, :], start=True, stop=False)
            nc.tensor.matmul(A_OUT[:, :], a_st[:, :], ctx_lo[:, b, :], start=False, stop=True).then_inc(z["read_done"], 1)

        def pe_c(pe, t):
            pe.wait_ge(z["h_norm_done"], t + 1)
            wait(pe, z["ht_lo"], t)
            for c in range(DC):
                last = nc.tensor.transpose(H_TR[:, c * P:(c + 1) * P], ln_h[:, t % 2, c * P:(c + 1) * P], ident[:, :])
            last.then_inc(z["ht_tr"], 1)
            pe.wait_ge(z["ht_lo"], t + 1)
            wait(pe, z["l2"], t)
            for a in range(2):
                for c in range(DC):
                    last = nc.tensor.matmul(H_LOG[:, 0:2 * E], xn[a][:, c, t * P:(t + 1) * P], rw_t[:, c, :],
                                            start=(a == 0 and c == 0), stop=(a == 1 and c == DC - 1))
            last.then_inc(z["log_done"], 1)

        def pe_d(pe, t):
            pe.wait_ge(z["share_done"], t + 1)
            wait(pe, z["st_done"], t)
            nc.tensor.transpose(S_TR[0:E, 0:P], share[:, t, :], ident[:, :]).then_inc(z["st_tr"], 1)
            pe.wait_ge(z["st_done"], t + 1)
            wait(pe, z["x_bias"], t)
            nc.tensor.matmul(S_OUT[:, :], share_t[:, :], down_bias[:, :], start=True, stop=True).then_inc(z["bias_mm"], 1)

        def act_a(act, t):
            act.wait_ge(z["mt_tr"], t + 1)
            wait(act, z["msc_done"], t)
            nc.scalar.activation(xt[:, :, :], M_TR[:, :].rearrange("p (c n) -> p c n", c=DC), ACT.Copy).then_inc(z["mt_done"], 1)

        def act_b(act, t):
            act.wait_ge(z["m3"], t + 1)
            nc.scalar.activation(m_sc[:, :], m_sc[:, :], ACT.Exp, bias=m_neg[:, 1:2], accum_out=m_neg[:, 2:3]).then_inc(z["mexp_done"], 1)
            act.wait_ge(z["at_tr"], t + 1)
            wait(act, z["read_done"], t)
            act_split(a_st[0:MEM, :], A_TR[0:MEM, 0:P], z["at_hi"])

        def act_c(act, t):
            act.wait_ge(z["ht_tr"], t + 1)
            act_split(xn[0][:, :, t * P:(t + 1) * P], H_TR[:, :].rearrange("p (c n) -> p c n", c=DC), z["ht_hi"])
            act.wait_ge(z["diff_done"], t + 1)
            nc.scalar.activation(gate2[:, 1:2], gate2[:, 0:1], ACT.Exp).then_inc(z["gexp_done"], 1)

        def act_d(act, t):
            act.wait_ge(z["st_tr"], t + 1)
            wait(act, z["bias_mm"], t)
            nc.scalar.activation(share_t[:, :], S_TR[0:E, 0:P], ACT.Copy).then_inc(z["st_done"], 1)

        def dve_b1(dve, t):
            b = t // QB
            dve.wait_ge(z["msc_done"], t + 1)
            wait(dve, z["at_tr"], t)
            nc.vector.tensor_tensor(m_sc[:, :], M_SC[:, 0:MEM], mask_scale[:, b, :], ALU.mult).then_inc(z["m1"], 1)
            dve.wait_ge(z["m1"], t + 1)
            nc.vector.tensor_tensor_reduce(out=m_sc[:, :], in0=m_sc[:, :], in1=mask_add[:, b, :], scale=1.0, scalar=NEG,
                                           op0=ALU.add, op1=ALU.max, accum_out=m_neg[:, 0:1]).then_inc(z["m2"], 1)
            dve.wait_ge(z["m2"], t + 1)
            nc.vector.tensor_scalar(m_neg[:, 1:2], m_neg[:, 0:1], -1.0, None, ALU.mult).then_inc(z["m3"], 1)

        def dve_b2(dve, t):
            b = t // QB
            dve.wait_ge(z["mexp_done"], t + 1)
            nc.vector.reciprocal(m_inv[:, 0:1], m_neg[:, 2:3]).then_inc(z["msum_inv"], 1)
            dve.wait_ge(z["msum_inv"], t + 1)
            nc.vector.tensor_tensor(m_inv[:, 1:2], m_inv[:, 0:1], valid[:, b:b + 1], ALU.mult).then_inc(z["m_inv_done"], 1)
            dve.wait_ge(z["at_hi"], t + 1)
            nc.vector.tensor_tensor(a_st[MEM:P, :], A_TR[0:MEM, 0:P], a_st[0:MEM, :].bitcast(F32), ALU.subtract).then_inc(z["at_lo"], 1)

        def dve_b3(dve, t):
            dve.wait_ge(z["read_done"], t + 1)
            dve.wait_ge(z["m_inv_done"], t + 1)
            nc.vector.scalar_tensor_tensor(out=x_res[:, t, :], in0=A_OUT[:, :], scalar=m_inv[:, 1:2], in1=x_res[:, t, :],
                                           op0=ALU.mult, op1=ALU.add).then_inc(z["x_mem"], 1)

        def dve_c1(dve, t):
            dve.wait_ge(z["ht_hi"], t + 1)
            dve_lo(xn[1][:, :, t * P:(t + 1) * P], H_TR[:, :].rearrange("p (c n) -> p c n", c=DC), xn[0][:, :, t * P:(t + 1) * P], z["ht_lo"])

        def dve_c2(dve, t):
            dve.wait_ge(z["log_done"], t + 1)
            nc.vector.tensor_tensor(logits[:, 0, :], H_LOG[:, 0:E], rb[:, :], ALU.add).then_inc(z["l1"], 1)
            dve.wait_ge(z["l1"], t + 1)
            nc.vector.tensor_tensor(logits[:, 1, :], H_LOG[:, E:2 * E], logits[:, 0, :], ALU.add).then_inc(z["l2"], 1)
            dve.wait_ge(z["l2"], t + 1)
            nc.vector.max(top[:, :], logits[:, 1, :]).then_inc(z["top_done"], 1)
            dve.wait_ge(z["top_done"], t + 1)
            nc.vector.tensor_tensor(gate2[:, 0:1], top[:, 1:2], top[:, 0:1], ALU.subtract).then_inc(z["diff_done"], 1)
            nc.vector.max_index(top_at[:, :], top[:, :], logits[:, 1, :]).then_inc(z["topi_done"], 1)
            dve.wait_ge(z["topi_done"], t + 1)
            nc.vector.tensor_copy(top_f[:, :], top_at[:, 0:2]).then_inc(z["topf_done"], 1)
            dve.wait_ge(z["gexp_done"], t + 1)
            nc.vector.tensor_scalar(gate2[:, 2:3], gate2[:, 1:2], 1.0, None, ALU.add).then_inc(z["g1"], 1)
            dve.wait_ge(z["g1"], t + 1)
            nc.vector.reciprocal(gate2[:, 3:4], gate2[:, 2:3]).then_inc(z["g2"], 1)
            dve.wait_ge(z["g2"], t + 1)
            nc.vector.tensor_tensor(gate2[:, 4:5], gate2[:, 3:4], gate2[:, 1:2], ALU.mult).then_inc(z["g3"], 1)
            dve.wait_ge(z["topf_done"], t + 1)
            dve.wait_ge(z["g3"], t + 1)
            for k in range(2):
                nc.vector.tensor_scalar(pick[:, k, :], iota[:, :], top_f[:, k:k + 1], gate2[:, 3 + k:4 + k], ALU.is_equal, ALU.mult).then_inc(z["p1"], 1)
            dve.wait_ge(z["p1"], 2 * t + 2)
            nc.vector.tensor_tensor(share[:, t, :], pick[:, 0, :], pick[:, 1, :], ALU.add).then_inc(z["share_done"], 1)

        def dve_d(dve, t):
            dve.wait_ge(z["bias_mm"], t + 1)
            nc.vector.tensor_tensor(x_res[:, t, :], S_OUT[:, :], x_res[:, t, :], ALU.add).then_inc(z["x_bias"], 1)

        def sp_weights(sp, e, ib):
            k, u = ib % 2, IB * e + ib
            wait(sp, z["gu_lo_done"], u - 1)
            wait(sp, z["gu_hi_done"], u - 1)
            wait(sp, z["dn_lo_done"], u - 1)
            wait(sp, z["bias_done"], 2 * u - 2)
            if not isinstance(e, int):
                settled(sp)
            gu_rows = gu_w.rearrange("e h j -> (e h) j")[bass.ds(e * D, D), 2 * P * ib:2 * P * (ib + 1)]
            sp.dma_start(gu_raw[:, k, :, :], gu_rows.rearrange("(c p) j -> p c j", p=P)).then_inc(z[f"gu_in{k}"], 16)
            sp.dma_start(dn_raw[:, k, :], down_w.rearrange("e i h -> (e i) h")[bass.ds(e * I + ib * P, P), :]).then_inc(z[f"gu_in{k}"], 16)
            sp.dma_start(bias_raw[:, k, :], gu_b.rearrange("e (q s) -> (e q) s", s=2)[bass.ds(e * I + ib * P, P), :]).then_inc(z[f"gu_in{k}"], 16)

        def raw_in(ib, e):
            return 96 * e + 48 * (ib // 2) + 48

        def act_weights(act, e, ib):
            k, u = ib % 2, IB * e + ib
            act.wait_ge(z[f"gu_in{k}"], raw_in(ib, e))
            wait(act, z["dn_mm"], 4 * B * (u - 1))
            act_split(gu[0][:, k, :, :, :].rearrange("p c s i -> p c i s"), gu_raw[:, k, :, :].rearrange("p c (i s) -> p c i s", s=2), z["gu_hi_done"])
            act_split(dn[0][:, k, :], dn_raw[:, k, :], z["dn_hi_done"])

        def pool_weights(pool, e, ib):
            k, u = ib % 2, IB * e + ib
            pool.wait_ge(z[f"gu_in{k}"], raw_in(ib, e))
            pool.wait_ge(z["gu_hi_done"], u + 1)
            nc.gpsimd.tensor_tensor(gu[1][:, k, :, :, :].rearrange("p c s i -> p c i s"), gu_raw[:, k, :, :].rearrange("p c (i s) -> p c i s", s=2),
                                    gu[0][:, k, :, :, :].rearrange("p c s i -> p c i s").bitcast(F32), ALU.subtract).then_inc(z["gu_lo_done"], 1)
            pool.wait_ge(z["dn_hi_done"], u + 1)
            nc.gpsimd.tensor_tensor(dn[1][:, k, :], dn_raw[:, k, :], dn[0][:, k, :].bitcast(F32), ALU.subtract).then_inc(z["dn_lo_done"], 1)

        def dve_bias(dve, e, ib):
            k, u = ib % 2, IB * e + ib
            dve.wait_ge(z[f"gu_in{k}"], raw_in(ib, e))
            wait(dve, z["up_done"], B * (u - 1))
            nc.vector.tensor_scalar(bias[:, k, 0:1], bias_raw[:, k, 0:1], 0.0, None, ALU.add).then_inc(z["bias_done"], 1)
            nc.vector.tensor_scalar(bias[:, k, 1:2], bias_raw[:, k, 1:2], 1.0, None, ALU.add).then_inc(z["bias_done"], 1)

        def pe_gu(pe, e, st_):
            ib, b = divmod(st_, B)
            k, i = ib % 2, STEPS * e + st_
            pe.wait_ge(z["gu_lo_done"], IB * e + ib + 1)
            wait(pe, z["up_done"], i - 1)
            for side in range(2):
                first = True
                for c in range(DC):
                    for sp_, mp in PASSES:
                        last = nc.tensor.matmul(bank[2 * (st_ % 2) + side][:, :], gu[sp_][:, k, c, side, :], xn[mp][:, c, b * L:(b + 1) * L],
                                                start=first, stop=(c == DC - 1 and (sp_, mp) == PASSES[-1]))
                        first = False
                last.then_inc(z["gu_mm"], 1)


        def pe_dn(pe, e, st_):
            ib, b = divmod(st_, B)
            k, i = ib % 2, STEPS * e + st_
            pe.wait_ge(z["al_done"], i + 1)
            pe.wait_ge(z["dn_lo_done"], IB * e + ib + 1)
            for t in range(QB):
                wait(pe, z["x_moe"], QB * i - QB + t + 1)
                for sp_, mp in PASSES:
                    last = nc.tensor.matmul(bank[4 + t][:, :], act_st[sp_][:, st_ % 2, t * P:(t + 1) * P], dn[mp][:, k, :],
                                            start=((sp_, mp) == PASSES[0]), stop=((sp_, mp) == PASSES[-1]))
                last.then_inc(z["dn_mm"], 1)

        def dve_gu(dve, e, st_):
            ib = st_ // B
            k, i, w = ib % 2, STEPS * e + st_, st_ % 2
            dve.wait_ge(z["bias_done"], 2 * (IB * e + ib) + 2)
            dve.wait_ge(z["gu_mm"], 2 * i + 1)
            nc.vector.tensor_scalar(gate[:, w, :], bank[2 * w][:, :], bias[:, k, 0:1], LIMIT, ALU.add, ALU.min).then_inc(z["gate_done"], 1)
            dve.wait_ge(z["gu_mm"], 2 * i + 2)
            wait(dve, z["ah_done"], i - 1)
            nc.vector.tensor_scalar(up[:, w, :], bank[2 * w + 1][:, :], bias[:, k, 1:2], LIMIT + 1.0, ALU.add, ALU.min).then_inc(z["up_done"], 1)

        def dve_act(dve, e, st_):
            i, w = STEPS * e + st_, st_ % 2
            dve.wait_ge(z["sig_done"], i + 1)
            nc.vector.tensor_tensor(sig[:, w, :], sig[:, w, :], gate[:, w, :], ALU.mult).then_inc(z["glu_done"], 1)
            dve.wait_ge(z["glu_done"], i + 1)
            nc.vector.scalar_tensor_tensor(out=up[:, w, :], in0=up[:, w, :], scalar=1.0 - LIMIT, in1=sig[:, w, :],
                                           op0=ALU.max, op1=ALU.mult).then_inc(z["act_done"], 1)

        def dve_al(dve, e, st_):
            i, w = STEPS * e + st_, st_ % 2
            dve.wait_ge(z["ah_done"], i + 1)
            dve_lo(act_st[1][:, w, :], up[:, w, :], act_st[0][:, w, :], z["al_done"])

        def dve_moe(dve, e, st_, t):
            b = st_ % B
            i = STEPS * e + st_
            tt = b * QB + t
            dve.wait_ge(z["dn_mm"], QB * i + t + 1)
            wait(dve, z["x_moe"], QB * i + t - STEPS)
            nc.vector.scalar_tensor_tensor(out=x_res[:, tt, :], in0=bank[4 + t][:, :], scalar=share_e[:, tt, :], in1=x_res[:, tt, :],
                                           op0=ALU.mult, op1=ALU.add).then_inc(z["x_moe"], 1)

        def act_step(act, e, st_):
            i, w = STEPS * e + st_, st_ % 2
            act.wait_ge(z["gate_done"], i + 1)
            wait(act, z["act_done"], i - 1)
            nc.scalar.activation(sig[:, w, :], gate[:, w, :], ACT.Sigmoid, scale=ALPHA).then_inc(z["sig_done"], 1)
            act.wait_ge(z["act_done"], i + 1)
            wait(act, z["dn_mm"], QB * (i - 1))
            act_split(act_st[0][:, w, :], up[:, w, :], z["ah_done"])

        def next_unit(e, ib):
            return (e, ib + 1) if ib + 1 < IB else (e + 1, 0)

        def pe_expert(pe, e, final):
            for st_ in range(STEPS):
                if st_ + 1 < STEPS:
                    pe_gu(pe, e, st_ + 1)
                elif not final:
                    pe_gu(pe, e + 1, 0)
                pe_dn(pe, e, st_)

        def act_expert(act, e, final):
            for st_ in range(STEPS):
                if st_ + 1 < STEPS:
                    act_step(act, e, st_ + 1)
                elif not final:
                    act_step(act, e + 1, 0)
                if st_ % B == 1 and not (final and st_ // B == IB - 1):
                    act_weights(act, *next_unit(e, st_ // B))

        def dve_expert(dve, e, final):
            wait(dve, z["x_moe"], QB * STEPS * e)
            nc.vector.tensor_copy(share_e[:, :, :], share_of(e)).then_inc(z["share_e_done"], 1)
            dve.wait_ge(z["share_e_done"], e + 1)
            for st_ in range(STEPS):
                ne, ns = (e, st_ + 1) if st_ + 1 < STEPS else (e + 1, 0)
                more = not (final and st_ + 1 == STEPS)
                if more:
                    dve_gu(dve, ne, ns)
                dve_moe(dve, e, st_, 0)
                if more:
                    dve_act(dve, ne, ns)
                dve_moe(dve, e, st_, 1)
                if more:
                    dve_al(dve, ne, ns)
                dve_moe(dve, e, st_, 2)
                dve_moe(dve, e, st_, 3)
                if st_ % B == 1 and not (final and st_ // B == IB - 1):
                    dve_bias(dve, *next_unit(e, st_ // B))

        def share_of(e):
            return share[:, :, bass.ds(e, 1)]

        def pool_expert(pool, e, final):
            for ib in range(IB):
                if not (final and ib == IB - 1):
                    pool_weights(pool, *next_unit(e, ib))

        with nc.Block() as block:

            @block.sync
            def _(sp):
                ctx_dup = ctx.rearrange("b m d -> m b d")
                sp.dma_start(ctx_raw[0:MEM, :, :], ctx_dup).then_inc(z["mem_in"], 16)
                sp.dma_start(ctx_raw[MEM:P, :, :], ctx_dup).then_inc(z["mem_in"], 16)
                sp.dma_start(mask_u8[:, :], mem_mask.rearrange("(o b) m -> o (b m)", o=1).partition_broadcast(P)).then_inc(z["mask_in"], 16)
                sp.dma_start(rw_raw[:, :], router_w).then_inc(z["rw_in"], 16)
                sp.dma_start(rb[:, :], router_b.rearrange("(o e) -> o e", o=1).partition_broadcast(P)).then_inc(z["small_in"], 16)
                sp.dma_start(iota[:, :], iota_t).then_inc(z["small_in"], 16)
                sp.dma_start(down_bias[:, :], down_b).then_inc(z["bd_in"], 16)
                for ib in range(IB):
                    sp_weights(sp, 0, ib)
                with sp.Fori(1, E) as e:
                    for ib in range(IB):
                        sp_weights(sp, e, ib)
                for b in range(B):
                    sp.wait_ge(z["x_moe"], QB * (E * STEPS - B + b + 1))
                    sp.dma_start(outr[:, b * QB:(b + 1) * QB, :], x_res[:, b * QB:(b + 1) * QB, :]).then_inc(z["out_done"], 16)
                sp.wait_ge(z["out_done"], 16 * B)

            @block.tensor
            def _(pe):
                pe_setup2(pe)
                pe.wait_ge(z["ctx_t_done"], 2)
                pe.wait_ge(z["ctx_lo_done"], 1)
                pe.wait_ge(z["rw_lo_done"], 1)
                pe.wait_ge(z["bd_in"], 16)
                for t in range(TT + 3):
                    if t < TT:
                        pe_a(pe, t)
                    if 1 <= t < TT + 1:
                        pe_b(pe, t - 1)
                    if 2 <= t < TT + 2:
                        pe_c(pe, t - 2)
                    if t >= 3:
                        pe_d(pe, t - 3)
                pe.wait_ge(z["x_bias"], TT)
                pe_gu(pe, 0, 0)
                pe_expert(pe, 0, False)
                with pe.Fori(1, E - 1) as e:
                    pe_expert(pe, e, False)
                pe_expert(pe, E - 1, True)

            @block.scalar
            def _(act):
                act.wait_ge(z["mem_in"], 32)
                act_split(ctx_hi[:, :, :], ctx_raw[:, :, :], z["ctx_hi_done"])
                act.wait_ge(z["ctx_tr"], 1)
                for k in range(2):
                    for half_ in range(2):
                        done = nc.scalar.activation(ctx_t[:, k + 2 * half_, :, :], bank[k][:, 2 * P * half_:2 * P * (half_ + 1)].rearrange("p (c m) -> p c m", c=DC), ACT.Copy)
                    done.then_inc(z["ctx_t_done"], 1)
                act.wait_ge(z["rw_tr"], 1)
                act_split(rw_t[:, :, 0:E], bank[2][:, 0:DC * E].rearrange("p (c e) -> p c e", c=DC), z["rw_hi_done"])
                for t in range(TT + 3):
                    if t < TT:
                        act_a(act, t)
                    if 1 <= t < TT + 1:
                        act_b(act, t - 1)
                    if 2 <= t < TT + 2:
                        act_c(act, t - 2)
                    if t >= 3:
                        act_d(act, t - 3)
                act_weights(act, 0, 0)
                act_step(act, 0, 0)
                act_expert(act, 0, False)
                with act.Fori(1, E - 1) as e:
                    act_expert(act, e, False)
                act_expert(act, E - 1, True)

            @block.vector
            def _(dve):
                dve.wait_ge(z["mask_in"], 16)
                nc.vector.tensor_copy(mask_f[:, :, :], mask_u8[:, :].rearrange("p (b m) -> p b m", b=B)).then_inc(z["mask_f_done"], 1)
                dve.wait_ge(z["mask_f_done"], 1)
                nc.vector.tensor_scalar(mask_scale[:, :, :], mask_f[:, :, :], float(np.float32(1.0) / np.sqrt(np.float32(D))), None, ALU.mult).then_inc(z["mask_tab"], 1)
                nc.vector.tensor_scalar(mask_add[:, :, :], mask_f[:, :, :], -1.0, -MASKED, ALU.add, ALU.mult).then_inc(z["mask_tab"], 1)
                nc.vector.reduce_max(valid[:, :], mask_f[:, :, :], AX.X).then_inc(z["mask_tab"], 1)
                dve.wait_ge(z["ctx_hi_done"], 1)
                dve_lo(ctx_lo[:, :, :], ctx_raw[:, :, :], ctx_hi[:, :, :], z["ctx_lo_done"])
                dve.wait_ge(z["rw_hi_done"], 1)
                dve_lo(rw_t[:, :, E:2 * E], bank[2][:, 0:DC * E].rearrange("p (c e) -> p c e", c=DC), rw_t[:, :, 0:E], z["rw_lo_done"])
                dve.wait_ge(z["mask_tab"], 3)
                dve.wait_ge(z["small_in"], 32)
                for t in range(TT + 3):
                    a, b_, c_, d_ = t < TT, 1 <= t < TT + 1, 2 <= t < TT + 2, t >= 3
                    if a:
                        ln_stats(nc, dve, z, "m_", t, x_res[:, t, :], stats, mv, var_eps)
                    if c_:
                        ln_stats(nc, dve, z, "h_", t - 2, x_res[:, t - 2, :], stats_h, mv_h, var_eps_h)
                    if b_:
                        dve_b1(dve, t - 1)
                    if a:
                        wait(dve, z["mt_tr"], t - 1)
                        ln_norm(nc, dve, z, "m_", t, x_res[:, t, :], ln_t[:, t % 2, :], mv, rstd)
                    if c_:
                        wait(dve, z["ht_tr"], t - 3)
                        ln_norm(nc, dve, z, "h_", t - 2, x_res[:, t - 2, :], ln_h[:, t % 2, :], mv_h, rstd_h)
                    if b_:
                        dve_b2(dve, t - 1)
                    if c_:
                        dve_c1(dve, t - 2)
                    if b_:
                        dve_b3(dve, t - 1)
                        dve.wait_ge(z["x_mem"], t)
                    if c_:
                        dve_c2(dve, t - 2)
                    if d_:
                        dve_d(dve, t - 3)
                dve.wait_ge(z["share_done"], TT)
                dve_bias(dve, 0, 0)
                dve_gu(dve, 0, 0)
                dve_act(dve, 0, 0)
                dve_al(dve, 0, 0)
                dve_expert(dve, 0, False)
                with dve.Fori(1, E - 1) as e:
                    dve_expert(dve, e, False)
                dve_expert(dve, E - 1, True)

            @block.gpsimd
            def _(pool):
                for t in range(TT + 2):
                    if t < TT:
                        ln_rstd(nc, pool, z, "m_", t, var_eps, half, rstd)
                    if t >= 2:
                        ln_rstd(nc, pool, z, "h_", t - 2, var_eps_h, half, rstd_h)
                pool_weights(pool, 0, 0)
                pool_expert(pool, 0, False)
                with pool.Fori(1, E - 1) as e:
                    pool_expert(pool, e, False)
                pool_expert(pool, E - 1, True)



_INS = ["x", "ctx_2048", "mask_BxS2_bk0", "L0_attn_Wq", "L0_attn_Wk", "L0_attn_Wv", "L0_attn_Wo",
        "L0_ffn_router_weight", "L0_ffn_router_bias", "L0_ffn_gate_up_proj", "L0_ffn_gate_up_proj_bias",
        "L0_ffn_down_proj", "L0_ffn_down_proj_bias"]


def _constants():
    inv = (1.0 / 10000.0 ** (np.arange(0, HD, 2, dtype=np.float32) / HD)).astype(np.float32)
    angle = (np.arange(L, dtype=np.float32)[:, None] * inv[None, :]).astype(np.float32)
    row = (np.arange(P) % HD) // 2
    sign = np.where(np.arange(P) % 2 == 0, -1.0, 1.0)[:, None]
    cos = np.cos(angle.astype(np.float64)).T[row].astype(np.float32)
    sin = (np.sin(angle.astype(np.float64)).T[row] * sign).astype(np.float32)
    causal = np.where(np.arange(L)[None, :] - (L - P) <= np.arange(P)[:, None], 0.0, NEG).astype(np.float32)
    iota = np.broadcast_to(np.arange(E, dtype=np.float32), (P, E)).copy()
    return {"cos": cos, "sin": sin, "causal": causal, "ident": np.eye(P, dtype=np.float32), "iota": iota}


def kernel(**inputs):
    import concourse.bacc as bacc
    from concourse.bass_utils import run_bass_kernel_spmd

    nc = bacc.Bacc("TRN2", target_bir_lowering=False, num_devices=1)
    arrays, args = {}, []
    for name in _INS:
        a = np.ascontiguousarray(inputs[name])
        arrays[f"in_{name}"] = a
    for name, a in _constants().items():
        arrays[f"const_{name}"] = a
    for name, a in arrays.items():
        args.append(nc.dram_tensor(name, a.shape, mybir.dt.from_np(a.dtype), kind="ExternalInput").ap())
    out = nc.dram_tensor("out", (B, L, D), F32, kind="ExternalOutput").ap()
    decoder_layer(nc, *args, out)
    r = run_bass_kernel_spmd(nc, [arrays], core_ids=[0])
    return r.results[0]["out"]
```

```python
from contextlib import ExitStack

import numpy as np

import concourse.bass as bass
from concourse import mybir

F32 = mybir.dt.float32
F32R = mybir.dt.float32r
U32 = mybir.dt.uint32
U8 = mybir.dt.uint8
ALU = mybir.AluOpType
ACT = mybir.ActivationFunctionType
AX = mybir.AxisListType

P = 128
B, L, D = 4, 512, 512
T = B * L
TT = T // P
DC = D // P
HQ, HKV, HD = 32, 8, 64
G = HQ // HKV
QB = L // P
MEM = 64
E, I = 8, 512
IB = I // P
EPS = 1e-5
NEG = -3.0e38
MASKED = -1e30
ALPHA, LIMIT = 1.702, 7.0
GROUPS = HKV
HEADS = B * G
PASSES = ((0, 0), (0, 1), (1, 0))

P_AT = [0, P, 3 * P, 6 * P]
P_LEN = 10 * P
PT_ZERO = 4 * P
PT_AT = [0, 5 * P, 9 * P, 8 * P]
PT_LEN = 12 * P
UNITS = [[(0, 0), (0, 1), (0, 2), (0, 3)], [(1, 1), (1, 2), (1, 3), (3, 3)], [(2, 2), (2, 3)]]
UNIT_PT = [0, PT_AT[1], PT_AT[2]]


def wait(eng, sem, value):
    if isinstance(value, int) and value <= 0:
        return
    eng.wait_ge(sem, value)


def ln_stats(nc, dve, s, pre, t, src, stats, mv, var_eps):
    k = t % 2
    nc.vector.bn_stats(stats[:, k, :], src).then_inc(s[pre + "stat_done"], 1)
    dve.wait_ge(s[pre + "stat_done"], t + 1)
    wait(dve, s[pre + "norm_done"], t - 1)
    nc.vector.bn_aggr(mv[:, k, :], stats[:, k, :]).then_inc(s[pre + "aggr_done"], 1)
    dve.wait_ge(s[pre + "aggr_done"], t + 1)
    nc.vector.tensor_scalar(var_eps[:, k:k + 1], mv[:, k, 1:2], EPS, None, ALU.add).then_inc(s[pre + "eps_done"], 1)


def ln_rstd(nc, pool, s, pre, t, var_eps, half, rstd):
    k = t % 2
    pool.wait_ge(s[pre + "eps_done"], t + 1)
    nc.gpsimd.tensor_tensor(rstd[:, k:k + 1], var_eps[:, k:k + 1], half[:, :], ALU.pow).then_inc(s[pre + "rstd_done"], 1)


def ln_norm(nc, dve, s, pre, t, src, dst, mv, rstd):
    k = t % 2
    dve.wait_ge(s[pre + "rstd_done"], t + 1)
    nc.vector.tensor_scalar(dst, src, mv[:, k, 0:1], rstd[:, k:k + 1], ALU.subtract, ALU.mult).then_inc(s[pre + "norm_done"], 1)


def decoder_layer(nc, x, ctx, mem_mask, wq, wk, wv, wo, router_w, router_b, gu_w, gu_b, down_w, down_b,
                  cos_t, sin_t, causal_t, ident_t, iota_t, out):
    stack = ExitStack()
    with stack:
        def sb(name, shape, dt=F32):
            return stack.enter_context(nc.sbuf_tensor(name, shape, dt))

        def sem(name):
            return stack.enter_context(nc.semaphore(name))

        x_res = sb("x_res", [P, TT, D])
        xn = [sb("xn_hi", [P, DC, T], F32R), sb("xn_lo", [P, DC, T], F32R)]
        ident = sb("ident", [P, P])
        stats = sb("stats", [P, 2, 6])
        mv = sb("mv", [P, 2, 2])
        var_eps = sb("var_eps", [P, 2])
        half = sb("half", [P, 1])
        rstd = sb("rstd", [P, 2])

        bank = [stack.enter_context(nc.psum_tensor(f"bank{i}", [P, 512], F32)) for i in range(8)]
        xr = x.rearrange("b (t p) d -> p (b t) d", p=P)
        outr = out.rearrange("b (t p) d -> p (b t) d", p=P)

        attn = ExitStack()

        def sa(name, shape, dt=F32):
            return attn.enter_context(nc.sbuf_tensor(name, shape, dt))

        w1_raw = sa("w1_raw", [P, 3, D])
        w2_raw = sa("w2_raw", [P, DC, G * HD])
        w1 = [sa("w1_hi", [P, DC, 3 * P], F32R), sa("w1_lo", [P, DC, 3 * P], F32R)]
        w2 = [sa("w2_hi", [P, 2, D], F32R), sa("w2_lo", [P, 2, D], F32R)]
        cos = sa("cos", [P, L])
        sin = sa("sin", [P, L])
        causal = sa("causal", [P, L])
        probs = sa("probs", [P, 2, P_LEN])
        pt = [[sa(f"pt{b}_hi", [P, PT_LEN], F32R), sa(f"pt{b}_lo", [P, PT_LEN], F32R)] for b in range(2)]
        q_st = sa("q_st", [P, G, L], F32R)
        k_hi = sa("k_hi", [P, 2, L], F32R)
        k_lo = sa("k_lo", [P, 2, L], F32R)
        v_t = sa("v_t", [HD, L])
        v_st = sa("v_st", [P, 2, QB, P], F32R)
        rot = sa("rot", [P, L])
        rope = sa("rope", [P, 2, L])
        wo_out = sa("wo_out", [P, QB, D])
        o_part = sa("o_part", [HD, L])
        o_f = sa("o_f", [P, L])
        o_st = [sa("o_hi", [P, 4, L], F32R), sa("o_lo", [P, 4, L], F32R)]
        neg_max = sa("neg_max", [P, 2, QB])
        row_sum = sa("row_sum", [P, 2, QB])
        row_inv = sa("row_inv", [P, 2, QB])
        ln_out = probs

        S_BANK, T_BANK, O_BANK, PJ_BANK, WO_BANK = bank[0:3], bank[3:5], bank[5], bank[6], bank[7]

        s = {name: sem(name) for name in (
            "const_in", "ident_in", "x_in0", "x_in1", "x_in2", "x_in3", "zero_done", "stat_done", "aggr_done", "eps_done", "half_done", "rstd_done", "norm_done", "lnt_done",
            "ln_hi", "ln_lo", "w1_in", "w2_in", "w1_tr", "w1_hi_done", "w1_lo_done", "w2_tr", "w2_hi_done",
            "w2_lo_done", "proj_done", "vt_done", "rope_in", "rot_sin", "rope_sum", "rope_hi", "k_lo_done", "q_lo_done",
            "v_tr", "v_hi_done", "v_lo_done", "scores_done", "masked_done", "exp_done",
            "recip_done", "pnorm_done", "ptrans_done", "pt_hi_done", "pt_lo_done", "pv_done", "opart_done",
            "oadd_done", "o_hi_done", "o_lo_done", "wo_done", "wo_out_done", "woacc_done")}

        def settled(eng):
            eng.nop(nofuse=True)

        def pe_ln(pe, t):
            pe.wait_ge(s["norm_done"], t + 1)
            wait(pe, s["ln_lo"], t - 3)
            for c in range(DC):
                last = nc.tensor.transpose(bank[t % 4][:, c * P:(c + 1) * P], ln_out[:, t % 2, c * P:(c + 1) * P], ident[:, :])
            last.then_inc(s["lnt_done"], 1)

        def pe_w1(pe, g, bank_free):
            pe.wait_ge(s["w1_in"], 48 * g + 48)
            for r in range(3):
                if bank_free[r]:
                    wait(pe, *bank_free[r])
                else:
                    pe.wait_ge(s["w1_lo_done"], 3 * g + r - 1)
                for c in range(DC):
                    last = nc.tensor.transpose((PJ_BANK, WO_BANK)[r % 2][:, c * P:(c + 1) * P], w1_raw[:, r, c * P:(c + 1) * P], ident[:, :])
                last.then_inc(s["w1_tr"], 1)

        def pe_w2(pe, g, bank_free):
            pe.wait_ge(s["w2_in"], 16 * g + 16)
            for k in range(2):
                wait(pe, *bank_free[k])
                for c in range(DC):
                    last = nc.tensor.transpose((PJ_BANK, WO_BANK)[k][:, c * P:(c + 1) * P], w2_raw[:, c, k * P:(k + 1) * P], ident[:, :])
                last.then_inc(s["w2_tr"], 1)

        def pe_proj(pe, b, r):
            first = True
            for c in range(DC):
                for sp, mp in PASSES:
                    last = nc.tensor.matmul(PJ_BANK[:, :], w1[sp][:, c, r * P:(r + 1) * P], xn[mp][:, c, b * L:(b + 1) * L],
                                            start=first, stop=(c == DC - 1 and (sp, mp) == PASSES[-1]))
                    first = False
            last.then_inc(s["proj_done"], 1)

        def pe_vt(pe, m):
            pe.wait_ge(s["vt_done"], m + 1)
            settled(pe)
            for j in range(QB):
                last = nc.tensor.transpose(PJ_BANK[:, j * HD:(j + 1) * HD], v_t[:, j * P:(j + 1) * P], ident[0:HD, 0:HD])
            last.then_inc(s["v_tr"], 1)

        def pe_scores(pe, n, m, h, kb):
            pe.wait_ge(s["k_lo_done"], 2 * m + 2)
            pe.wait_ge(s["q_lo_done"], 2 * m + 1 + (h >= 2))
            for k, blocks in enumerate(((3,), (2,), (1, 0))):
                wait(pe, s["masked_done"], 4 * n - (3, 2, 0)[k])
                for i in blocks:
                    cols = P * (i + 1) if i else 2 * P
                    at = 2 * P if i == 0 else 0
                    for a, kk in enumerate((k_hi, k_lo)):
                        last = nc.tensor.matmul(S_BANK[k][:, at:at + cols], q_st[:, h, i * P:(i + 1) * P], kk[:, kb, 0:cols],
                                                start=(a == 0), stop=(a == 1))
                last.then_inc(s["scores_done"], 1)

        def pe_ptrans(pe, n, hb, u):
            if u == 0:
                pe.wait_ge(s["pnorm_done"], 4 * n + 4)
            wait(pe, s["pt_lo_done"], 3 * n + (0, 0, 1)[u])
            for k, (j, i) in enumerate(UNITS[u]):
                last = nc.tensor.transpose(T_BANK[u % 2][:, k * P:(k + 1) * P],
                                           probs[:, hb, P_AT[i] + j * P:P_AT[i] + (j + 1) * P], ident[:, :])
            last.then_inc(s["ptrans_done"], 1)

        def pe_pv(pe, n, m, hb, vb):
            pe.wait_ge(s["pt_lo_done"], 3 * n + 3)
            pe.wait_ge(s["v_lo_done"], m + 1)
            wait(pe, s["oadd_done"], n)
            for j in range(QB):
                for a in range(2):
                    if j == 3:
                        rhs = pt[hb][a][:, PT_ZERO:PT_ZERO + 8 * P].rearrange("p (z c) -> p z c", z=2)[:, :, 0:P]
                        dst = O_BANK[:, 2 * P:4 * P].rearrange("p (z c) -> p z c", z=2)
                    else:
                        rhs = pt[hb][a][:, PT_AT[j]:PT_AT[j] + (QB - j) * P]
                        dst = O_BANK[:, j * P:4 * P]
                    last = nc.tensor.matmul(dst, v_st[:, vb, j, :], rhs, start=(j == 0 and a == 0), stop=(j == QB - 1 and a == 1))
            last.then_inc(s["pv_done"], 1)

        def pe_wo(pe, m, mb, t):
            pe.wait_ge(s["o_lo_done"], 2 * m + 2)
            wait(pe, s["wo_out_done"], 4 * m + t)
            first = True
            for k in range(2):
                for sp, mp in PASSES:
                    last = nc.tensor.matmul(WO_BANK[:, :], o_st[sp][:, 2 * mb + k, t * P:(t + 1) * P], w2[mp][:, k, :],
                                            start=first, stop=(k == 1 and (sp, mp) == PASSES[-1]))
                    first = False
            last.then_inc(s["wo_done"], 1)

        def pe_group(pe, g):
            for c in range(HEADS):
                b, h = divmod(c, G)
                n, m = HEADS * g + c, B * g + b
                begun = not (isinstance(g, int) and g == 0 and c == 0)
                more = not (isinstance(g, int) and g == GROUPS - 1 and c == HEADS - 1)
                next_batch = not (isinstance(g, int) and g == GROUPS - 1 and b == B - 1)
                last_batch = not (isinstance(g, int) and g == 0 and b == 0)
                next_group = not (isinstance(g, int) and g == GROUPS - 1)
                batch_before_last = not (isinstance(g, int) and g == 0 and b < 2)
                if begun:
                    pe_ptrans(pe, n - 1, (c + 1) % 2, 2)
                if more:
                    pe_scores(pe, n + 1, m if h < G - 1 else m + 1, (h + 1) % G, (b + (h == G - 1)) % 2)
                if h == 0 and next_batch:
                    if b == 3:
                        pe.wait_ge(s["w1_lo_done"], 3 * g + 6)
                    else:
                        pe.wait_ge(s["v_lo_done"], m + 1)
                    pe_proj(pe, (b + 1) % B, 2)
                if h == 1 and next_batch:
                    if b == 1:
                        pe.wait_ge(s["w2_lo_done"], 2 * g + 1)
                    else:
                        pe.wait_ge(s["rope_in"], 3 * m + 4)
                        pe.wait_ge(s["vt_done"], m + 2)
                    pe_proj(pe, (b + 1) % B, 0)
                if h == 2 and next_batch:
                    pe.wait_ge(s["rope_in"], 3 * m + 5)
                    pe_proj(pe, (b + 1) % B, 1)
                if h == 3 and next_batch:
                    pe.wait_ge(s["rope_in"], 3 * m + 6)
                    pe_vt(pe, m + 1)
                pe_ptrans(pe, n, c % 2, 0)
                pe_ptrans(pe, n, c % 2, 1)
                if begun:
                    pe_pv(pe, n - 1, m if h else m - 1, (c + 1) % 2, (b if h else b + 1) % 2)
                if h and last_batch:
                    if h == 1 and b == 1:
                        pe.wait_ge(s["w2_lo_done"], 2 * g + 2)
                    pe_wo(pe, m - 1, (b - 1) % 2, h - 1)
                if h == 0 and batch_before_last:
                    if b == 3 and next_group:
                        pe.wait_ge(s["w1_lo_done"], 3 * g + 5)
                    pe_wo(pe, m - 2, b % 2, 3)
                if h == 0 and b == 1:
                    pe.wait_ge(s["vt_done"], m + 2)
                    pe_w2(pe, g, ((s["rope_in"], 3 * m + 4), (s["wo_out_done"], 4 * m - 4)))
                if h == 3 and b == 2 and next_group:
                    pe_w1(pe, g + 1, ((s["v_lo_done"], m + 2), (s["wo_out_done"], 4 * m - 1), None))

        def act_split(dst, src, sem_):
            nc.scalar.activation(dst, src, ACT.Copy).then_inc(sem_, 1)

        def act_exp(act, n, hb):
            for i in (3, 2, 1, 0):
                act.wait_ge(s["masked_done"], 4 * n + 4 - i)
                row = probs[:, hb, P_AT[i]:P_AT[i] + (i + 1) * P]
                nc.scalar.activation(row, row, ACT.Exp, bias=neg_max[:, hb, i:i + 1], scale=-1.0,
                                     accum_out=row_sum[:, hb, i:i + 1]).then_inc(s["exp_done"], 1)

        def act_rope(act, m, r, mb):
            act.wait_ge(s["rope_sum"], 3 * m + r + 1)
            if r == 0:
                wait(act, s["scores_done"], 12 * m - 12)
                act_split(k_hi[0:HD, mb, :], rope[0:HD, mb, :], s["rope_hi"])
                act_split(k_hi[HD:P, mb, :], rope[0:HD, mb, :], s["rope_hi"])
            else:
                wait(act, s["scores_done"], 12 * m - 12 + 6 * r)
                act_split(q_st[0:HD, 2 * r - 2, :], rope[0:HD, (mb + r) % 2, :], s["rope_hi"])
                act_split(q_st[HD:P, 2 * r - 1, :], rope[HD:P, (mb + r) % 2, :], s["rope_hi"])

        def act_vt(act, m, r_sem_value):
            act.wait_ge(s["proj_done"], r_sem_value)
            wait(act, s["v_tr"], m)
            act_split(v_t[:, :], PJ_BANK[HD:P, :], s["vt_done"])

        def act_v(act, m, vb):
            act.wait_ge(s["v_tr"], m + 1)
            wait(act, s["pv_done"], 4 * m - 4)
            act_split(v_st[:, vb, :, 0:HD], PJ_BANK[:, 0:QB * HD].rearrange("p (j d) -> p j d", j=QB), s["v_hi_done"])

        def act_w1(act, g):
            wait(act, s["proj_done"], 12 * g)
            for r in range(3):
                act.wait_ge(s["w1_tr"], 3 * g + r + 1)
                act_split(w1[0][:, :, r * P:(r + 1) * P], (PJ_BANK, WO_BANK)[r % 2][:, :].rearrange("p (c n) -> p c n", c=DC), s["w1_hi_done"])

        def act_w2(act, g):
            wait(act, s["wo_done"], 16 * g)
            for k in range(2):
                act.wait_ge(s["w2_tr"], 2 * g + k + 1)
                act_split(w2[0][:, k, :], (PJ_BANK, WO_BANK)[k][:, :], s["w2_hi_done"])

        def act_pt(act, n, hb, u):
            act.wait_ge(s["ptrans_done"], 3 * n + u + 1)
            if u == 0:
                wait(act, s["pv_done"], n - 1)
            w = P * len(UNITS[u])
            act_split(pt[hb][0][:, UNIT_PT[u]:UNIT_PT[u] + w], T_BANK[u % 2][:, 0:w], s["pt_hi_done"])

        def act_opart(act, n):
            act.wait_ge(s["pv_done"], n + 1)
            wait(act, s["oadd_done"], n)
            act_split(o_part[:, :], O_BANK[HD:P, :], s["opart_done"])

        def act_o(act, n, m, k):
            act.wait_ge(s["oadd_done"], n + 1)
            wait(act, s["wo_done"], 4 * m - 4)
            act_split(o_st[0][:, k, :], o_f[:, :], s["o_hi_done"])

        def act_wo(act, m, t):
            act.wait_ge(s["wo_done"], 4 * m + t + 1)
            wait(act, s["woacc_done"], 4 * m + t - 3)
            nc.scalar.activation(wo_out[:, t, :], WO_BANK[:, :], ACT.Copy).then_inc(s["wo_out_done"], 1)

        def act_group(act, g):
            for c in range(HEADS):
                b, h = divmod(c, G)
                n, m = HEADS * g + c, B * g + b
                begun = not (isinstance(g, int) and g == 0 and c == 0)
                more = not (isinstance(g, int) and g == GROUPS - 1 and c == HEADS - 1)
                last_batch = not (isinstance(g, int) and g == 0 and b == 0)
                next_batch = not (isinstance(g, int) and g == GROUPS - 1 and b == B - 1)
                if begun:
                    act_pt(act, n - 1, (c + 1) % 2, 2)
                if h and next_batch:
                    act_rope(act, m + 1, h - 1, (b + 1) % 2)
                if more:
                    act_exp(act, n + 1, (c + 1) % 2)
                if h == 0 and next_batch:
                    act_vt(act, m + 1, 3 * m + 4)
                if h == 3 and next_batch:
                    act_v(act, m + 1, (b + 1) % 2)
                act_pt(act, n, c % 2, 0)
                act_pt(act, n, c % 2, 1)
                if begun:
                    act_opart(act, n - 1)
                if h and last_batch:
                    act_wo(act, m - 1, h - 1)
                if h == 0 and not (isinstance(g, int) and g == 0 and b < 2):
                    act_wo(act, m - 2, 3)
                if begun and h % 2 == 0:
                    act_o(act, n - 1, m if h else m - 1, (c // 2 - 1) % 4)
                if h == 0 and b == 1:
                    act_w2(act, g)
                if h == 3 and b == 2 and not (isinstance(g, int) and g == GROUPS - 1):
                    act_w1(act, g + 1)

        def dve_lo(dst, src, hi, sem_):
            nc.vector.tensor_tensor(dst, src, hi.bitcast(F32), ALU.subtract).then_inc(sem_, 1)

        def dve_masked(dve, n, hb):
            wait(dve, s["ptrans_done"], 3 * n - 3)
            for i in (3, 2, 1, 0):
                k = (2, 2, 1, 0)[i]
                if i:
                    dve.wait_ge(s["scores_done"], 3 * n + k + 1)
                    settled(dve)
                at = 2 * P if i == 0 else 0
                nc.vector.tensor_tensor_reduce(
                    out=probs[:, hb, P_AT[i]:P_AT[i] + (i + 1) * P], in0=S_BANK[k][:, at:at + (i + 1) * P],
                    in1=causal[:, (QB - 1 - i) * P:L], scale=-HD ** -0.5, scalar=-NEG, op0=ALU.add, op1=ALU.min,
                    accum_out=neg_max[:, hb, i:i + 1]).then_inc(s["masked_done"], 1)

        def dve_recip(dve, n, hb):
            dve.wait_ge(s["exp_done"], 4 * n + 4)
            nc.vector.reciprocal(row_inv[:, hb, :], row_sum[:, hb, :]).then_inc(s["recip_done"], 1)

        def dve_rope_in(dve, m, r, mb):
            dve.wait_ge(s["proj_done"], 3 * m + r + 1)
            wait(dve, s["rope_sum"], 3 * m + r)
            if r == 2:
                dve.wait_ge(s["k_lo_done"], 2 * m + 2)
            else:
                wait(dve, s["q_lo_done"], 2 * m + r - 1)
            rows = HD if r == 0 else P
            nc.vector.tensor_tensor(rope[0:rows, (mb + r) % 2, :], PJ_BANK[0:rows, :], cos[0:rows, :], ALU.mult)
            nc.vector.stream_shuffle(rot[0:rows, :], PJ_BANK[0:rows, :], [p ^ 1 for p in range(32)]).then_inc(s["rope_in"], 1)

        def dve_q_lo(dve, m, r, mb):
            dve.wait_ge(s["rope_hi"], 6 * m + 2 * r + 2)
            a, c = 2 * r - 2, 2 * r - 1
            nc.vector.tensor_tensor(q_st[HD:P, a, :], rope[0:HD, (mb + r) % 2, :], q_st[0:HD, a, :].bitcast(F32), ALU.subtract)
            nc.vector.tensor_tensor(q_st[0:HD, c, :], rope[HD:P, (mb + r) % 2, :], q_st[HD:P, c, :].bitcast(F32), ALU.subtract).then_inc(s["q_lo_done"], 1)

        def dve_v(dve, m, vb):
            dve.wait_ge(s["v_hi_done"], m + 1)
            dve_lo(v_st[:, vb, :, HD:P], PJ_BANK[:, 0:QB * HD].rearrange("p (j d) -> p j d", j=QB), v_st[:, vb, :, 0:HD], s["v_lo_done"])

        def dve_w1(dve, g):
            for r in range(3):
                dve.wait_ge(s["w1_hi_done"], 3 * g + r + 1)
                dve_lo(w1[1][:, :, r * P:(r + 1) * P], (PJ_BANK, WO_BANK)[r % 2][:, :].rearrange("p (c n) -> p c n", c=DC),
                       w1[0][:, :, r * P:(r + 1) * P], s["w1_lo_done"])

        def dve_w2(dve, g):
            for k in range(2):
                dve.wait_ge(s["w2_hi_done"], 2 * g + k + 1)
                dve_lo(w2[1][:, k, :], (PJ_BANK, WO_BANK)[k][:, :], w2[0][:, k, :], s["w2_lo_done"])

        def dve_pt(dve, n, hb, u):
            dve.wait_ge(s["pt_hi_done"], 3 * n + u + 1)
            w = P * len(UNITS[u])
            dve_lo(pt[hb][1][:, UNIT_PT[u]:UNIT_PT[u] + w], T_BANK[u % 2][:, 0:w], pt[hb][0][:, UNIT_PT[u]:UNIT_PT[u] + w], s["pt_lo_done"])

        def dve_oadd(dve, n, odd, pairs_before):
            dve.wait_ge(s["opart_done"], n + 1)
            wait(dve, s["o_lo_done"], pairs_before)
            r = HD if odd else 0
            nc.vector.tensor_tensor(o_f[r:r + HD, :], O_BANK[0:HD, :], o_part[:, :], ALU.add).then_inc(s["oadd_done"], 1)

        def dve_o(dve, pair, k):
            dve.wait_ge(s["o_hi_done"], pair + 1)
            dve_lo(o_st[1][:, k, :], o_f[:, :], o_st[0][:, k, :], s["o_lo_done"])

        def dve_group(dve, g):
            for c in range(HEADS):
                b, h = divmod(c, G)
                n, m = HEADS * g + c, B * g + b
                begun = not (isinstance(g, int) and g == 0 and c == 0)
                more = not (isinstance(g, int) and g == GROUPS - 1 and c == HEADS - 1)
                next_batch = not (isinstance(g, int) and g == GROUPS - 1 and b == B - 1)
                if more:
                    dve_masked(dve, n + 1, (c + 1) % 2)
                if begun:
                    dve_pt(dve, n - 1, (c + 1) % 2, 2)
                if begun and h % 2 == 1 and c > 0 and not (isinstance(g, int) and g == 0 and c == 1):
                    dve_o(dve, HEADS // 2 * g + (c - 1) // 2 - 1, ((c - 1) // 2 - 1) % 4)
                if h > 1 and next_batch:
                    dve_q_lo(dve, m + 1, h - 1, (b + 1) % 2)
                if h < 3 and next_batch:
                    dve_rope_in(dve, m + 1, h, (b + 1) % 2)
                if h == 3 and next_batch:
                    dve_v(dve, m + 1, (b + 1) % 2)
                if more:
                    dve_recip(dve, n + 1, (c + 1) % 2)
                dve_pt(dve, n, c % 2, 0)
                dve_pt(dve, n, c % 2, 1)
                if begun:
                    dve_oadd(dve, n - 1, (c - 1) % 2, HEADS // 2 * g + ((c - 1) // 2 if c else -1))
                if h == 0 and b == 1:
                    dve_w2(dve, g)
                if h == 3 and b == 2 and not (isinstance(g, int) and g == GROUPS - 1):
                    dve_w1(dve, g + 1)

        def pool_rope(pool, m, r, mb):
            pool.wait_ge(s["rope_in"], 3 * m + r + 1)
            rows = HD if r == 0 else P
            nc.gpsimd.tensor_tensor(rot[0:rows, :], rot[0:rows, :], sin[0:rows, :], ALU.mult).then_inc(s["rot_sin"], 1)
            pool.wait_ge(s["rot_sin"], 3 * m + r + 1)
            nc.gpsimd.tensor_tensor(rope[0:rows, (mb + r) % 2, :], rope[0:rows, (mb + r) % 2, :], rot[0:rows, :], ALU.add).then_inc(s["rope_sum"], 1)

        def pool_norm(pool, n, hb):
            pool.wait_ge(s["recip_done"], n + 1)
            settled(pool)
            for i in (3, 2, 1, 0):
                row = probs[:, hb, P_AT[i]:P_AT[i] + (i + 1) * P]
                nc.gpsimd.tensor_scalar(row, row, row_inv[:, hb, i:i + 1], 0.0, ALU.mult, ALU.add).then_inc(s["pnorm_done"], 1)

        def pool_k_lo(pool, m, mb):
            pool.wait_ge(s["rope_hi"], 6 * m + 2)
            wait(pool, s["pnorm_done"], 16 * m - 8)
            wait(pool, s["woacc_done"], 4 * m - 8)
            for half_ in range(2):
                nc.gpsimd.tensor_tensor(k_lo[half_ * HD:(half_ + 1) * HD, mb, :], rope[0:HD, mb, :], k_hi[0:HD, mb, :].bitcast(F32),
                                        ALU.subtract).then_inc(s["k_lo_done"], 1)
            pool.wait_ge(s["k_lo_done"], 2 * m + 2)

        def pool_woacc(pool, m, b, t):
            pool.wait_ge(s["wo_out_done"], 4 * m + t + 1)
            tile = x_res[:, b * QB + t, :]
            nc.gpsimd.tensor_tensor(tile, wo_out[:, t, :], tile, ALU.add).then_inc(s["woacc_done"], 1)

        def pool_group(pool, g):
            for c in range(HEADS):
                b, h = divmod(c, G)
                n, m = HEADS * g + c, B * g + b
                next_batch = not (isinstance(g, int) and g == GROUPS - 1 and b == B - 1)
                last_batch = not (isinstance(g, int) and g == 0 and b == 0)
                if h == 1 and next_batch:
                    pool_k_lo(pool, m + 1, (b + 1) % 2)
                if h < 3 and next_batch:
                    pool_rope(pool, m + 1, h, (b + 1) % 2)
                if not (isinstance(g, int) and g == GROUPS - 1 and c == HEADS - 1):
                    pool_norm(pool, n + 1, (c + 1) % 2)
                if h and last_batch:
                    pool_woacc(pool, m - 1, (b - 1) % B, h - 1)
                if h == 0 and not (isinstance(g, int) and g == 0 and b < 2):
                    pool_woacc(pool, m - 2, (b - 2) % B, 3)

        def sp_w1(sp, g):
            wait(sp, s["w1_tr"], 3 * g)
            if not isinstance(g, int):
                settled(sp)
            sp.dma_start(w1_raw[:, 0:2, :], wq[bass.ds(g * G * HD, G * HD), :].rearrange("(r p) d -> p r d", p=P)).then_inc(s["w1_in"], 16)
            sp.dma_start(w1_raw[0:HD, 2, :], wk[bass.ds(g * HD, HD), :]).then_inc(s["w1_in"], 16)
            sp.dma_start(w1_raw[HD:P, 2, :], wv[bass.ds(g * HD, HD), :]).then_inc(s["w1_in"], 16)

        def sp_w2(sp, g):
            wait(sp, s["w2_tr"], 2 * g)
            if not isinstance(g, int):
                settled(sp)
            sp.dma_start(w2_raw[:, :, :], wo[:, bass.ds(g * G * HD, G * HD)].rearrange("(c p) n -> p c n", p=P)).then_inc(s["w2_in"], 16)

        with nc.Block() as block:

            @block.sync
            def _(sp):
                for b in range(B):
                    sp.dma_start(x_res[:, b * QB:(b + 1) * QB, :], xr[:, b * QB:(b + 1) * QB, :]).then_inc(s[f"x_in{b}"], 16)
                    if b == 0:
                        sp_w1(sp, 0)
                        sp.dma_start(cos[:, :], cos_t).then_inc(s["const_in"], 16)
                        sp.dma_start(sin[:, :], sin_t).then_inc(s["const_in"], 16)
                        sp.dma_start(causal[:, :], causal_t).then_inc(s["const_in"], 16)
                sp_w2(sp, 0)
                with sp.Fori(1, GROUPS) as g:
                    sp_w1(sp, g)
                    sp_w2(sp, g)

            @block.tensor
            def _(pe):
                pe.wait_ge(s["ident_in"], 16)
                pe.wait_ge(s["zero_done"], 4)
                for t in range(4):
                    pe_ln(pe, t)
                pe_w1(pe, 0, ((s["w1_lo_done"], 0), (s["w1_lo_done"], 0), None))
                for t in range(4, TT):
                    pe_ln(pe, t)
                pe.wait_ge(s["w1_lo_done"], 3)
                pe.wait_ge(s["ln_lo"], TT)
                pe_proj(pe, 0, 2)
                for r in range(2):
                    pe.wait_ge(s["rope_in"], r + 1)
                    pe.wait_ge(s["vt_done"], 1)
                    pe_proj(pe, 0, r)
                pe.wait_ge(s["rope_in"], 3)
                pe_vt(pe, 0)
                pe_scores(pe, 0, 0, 0, 0)
                pe_group(pe, 0)
                with pe.Fori(1, GROUPS - 1) as g:
                    pe_group(pe, g)
                pe_group(pe, GROUPS - 1)
                pe_ptrans(pe, HEADS * GROUPS - 1, 1, 2)
                pe_pv(pe, HEADS * GROUPS - 1, B * GROUPS - 1, 1, 1)
                pe_wo(pe, B * GROUPS - 2, 0, 3)
                for t in range(QB):
                    pe_wo(pe, B * GROUPS - 1, 1, t)

            @block.scalar
            def _(act):
                act.dma_start(ident[:, :], ident_t).then_inc(s["ident_in"], 16)

                def ln_hi(t):
                    act.wait_ge(s["lnt_done"], t + 1)
                    act_split(xn[0][:, :, t * P:(t + 1) * P], bank[t % 4][:, :].rearrange("p (c n) -> p c n", c=DC), s["ln_hi"])

                for t in range(4):
                    ln_hi(t)
                act_w1(act, 0)
                for t in range(4, TT):
                    ln_hi(t)
                act_vt(act, 0, 1)
                for r in range(3):
                    act_rope(act, 0, r, 0)
                act_v(act, 0, 0)
                act_exp(act, 0, 0)
                act_group(act, 0)
                with act.Fori(1, GROUPS - 1) as g:
                    act_group(act, g)
                act_group(act, GROUPS - 1)
                act_pt(act, HEADS * GROUPS - 1, 1, 2)
                act_opart(act, HEADS * GROUPS - 1)
                act_o(act, HEADS * GROUPS - 1, B * GROUPS - 1, 3)
                act_wo(act, B * GROUPS - 2, 3)
                for t in range(QB):
                    act_wo(act, B * GROUPS - 1, t)

            @block.vector
            def _(dve):
                for hb in range(2):
                    for a in range(2):
                        nc.vector.memset(pt[hb][a][:, PT_ZERO:PT_ZERO + P].bitcast(F32), 0.0).then_inc(s["zero_done"], 1)

                def ln_lo(t):
                    dve.wait_ge(s["ln_hi"], t + 1)
                    dve_lo(xn[1][:, :, t * P:(t + 1) * P], bank[t % 4][:, :].rearrange("p (c n) -> p c n", c=DC),
                           xn[0][:, :, t * P:(t + 1) * P], s["ln_lo"])

                for t in range(TT + 1):
                    if t < TT:
                        dve.wait_ge(s[f"x_in{t // QB}"], 16)
                        ln_stats(nc, dve, s, "", t, x_res[:, t, :], stats, mv, var_eps)
                    if t >= 1:
                        wait(dve, s["lnt_done"], t - 2)
                        ln_norm(nc, dve, s, "", t - 1, x_res[:, t - 1, :], ln_out[:, (t - 1) % 2, 0:D], mv, rstd)
                    if t >= 3:
                        ln_lo(t - 3)
                    if t == 6:
                        dve_w1(dve, 0)
                ln_lo(TT - 2)
                ln_lo(TT - 1)
                dve.wait_ge(s["const_in"], 48)
                dve_rope_in(dve, 0, 0, 0)
                for r in range(3):
                    if r:
                        dve_q_lo(dve, 0, r, 0)
                    if r < 2:
                        dve_rope_in(dve, 0, r + 1, 0)
                dve_v(dve, 0, 0)
                dve_masked(dve, 0, 0)
                dve_recip(dve, 0, 0)
                dve_group(dve, 0)
                with dve.Fori(1, GROUPS - 1) as g:
                    dve_group(dve, g)
                dve_group(dve, GROUPS - 1)
                dve_pt(dve, HEADS * GROUPS - 1, 1, 2)
                dve_oadd(dve, HEADS * GROUPS - 1, 1, HEADS * GROUPS // 2 - 1)
                dve_o(dve, HEADS * GROUPS // 2 - 1, 3)

            @block.gpsimd
            def _(pool):
                nc.gpsimd.memset(half[:, :], -0.5).then_inc(s["half_done"], 1)
                pool.wait_ge(s["half_done"], 1)
                for t in range(TT):
                    ln_rstd(nc, pool, s, "", t, var_eps, half, rstd)
                pool.wait_ge(s["const_in"], 48)
                for r in range(3):
                    pool_rope(pool, 0, r, 0)
                    if r == 0:
                        pool_k_lo(pool, 0, 0)
                pool_norm(pool, 0, 0)
                pool_group(pool, 0)
                with pool.Fori(1, GROUPS - 1) as g:
                    pool_group(pool, g)
                pool_group(pool, GROUPS - 1)
                pool_woacc(pool, B * GROUPS - 2, B - 2, 3)
                for t in range(QB):
                    pool_woacc(pool, B * GROUPS - 1, B - 1, t)

        attn.close()

        def st(name, shape, dt=F32):
            return stack.enter_context(nc.sbuf_tensor(name, shape, dt))

        ctx_raw = st("ctx_raw", [P, B, D])
        ctx_hi = st("ctx_hi", [P, B, D], F32R)
        ctx_lo = st("ctx_lo", [P, B, D], F32R)
        ctx_t = st("ctx_t", [P, B, DC, MEM])
        mask_u8 = st("mask_u8", [P, B * MEM], U8)
        mask_f = st("mask_f", [P, B, MEM])
        mask_scale = st("mask_scale", [P, B, MEM])
        mask_add = st("mask_add", [P, B, MEM])
        valid = st("valid", [P, B])
        ln_t = st("ln_t", [P, 2, D])
        ln_h = st("ln_h", [P, 2, D])
        xt = st("xt", [P, DC, P])
        mv_h = st("mv_h", [P, 2, 2])
        var_eps_h = st("var_eps_h", [P, 2])
        rstd_h = st("rstd_h", [P, 2])
        stats_h = st("stats_h", [P, 2, 6])
        m_sc = st("m_sc", [P, MEM])
        m_neg = st("m_neg", [P, 3])
        m_inv = st("m_inv", [P, 2])
        a_st = st("a_st", [P, P], F32R)
        rw_raw = st("rw_raw", [E, D])
        rw_t = st("rw_t", [P, DC, 2 * E], F32R)
        rb = st("rb", [P, E])
        iota = st("iota", [P, E])
        logits = st("logits", [P, 2, E])
        top = st("top", [P, 8])
        top_at = st("top_at", [P, 8], U32)
        top_f = st("top_f", [P, 2])
        gate2 = st("gate2", [P, 6])
        pick = st("pick", [P, 2, E])
        share = st("share", [P, TT, E])
        share_e = st("share_e", [P, TT, 1])
        share_t = st("share_t", [E, P])
        down_bias = st("down_bias", [E, D])
        gu_raw = st("gu_raw", [P, 2, DC, 2 * P])
        dn_raw = st("dn_raw", [P, 2, D])
        bias_raw = st("bias_raw", [P, 2, 2])
        gu = [st("gu_hi", [P, 2, DC, 2, P], F32R), st("gu_lo", [P, 2, DC, 2, P], F32R)]
        dn = [st("dn_hi", [P, 2, D], F32R), st("dn_lo", [P, 2, D], F32R)]
        bias = st("bias", [P, 2, 2])
        gate = st("gate", [P, 2, L])
        up = st("up", [P, 2, L])
        sig = st("sig", [P, 2, L])
        act_st = [st("act_hi", [P, 2, L], F32R), st("act_lo", [P, 2, L], F32R)]

        names2 = []
        for pre in ("m_", "h_"):
            names2 += [pre + e for e in ("stat_done", "aggr_done", "eps_done", "rstd_done", "norm_done")]
        names2 += ["mem_in", "mask_in", "rw_in", "small_in", "bd_in", "ctx_hi_done", "ctx_lo_done", "ctx_tr", "ctx_t_done",
                   "mask_f_done", "mask_tab", "rw_tr", "rw_hi_done", "rw_lo_done",
                   "mt_tr", "mt_done", "msc_done", "m1", "m2", "m3", "mexp_done", "msum_inv", "m_inv_done", "at_tr", "at_hi", "at_lo",
                   "read_done", "x_mem", "ht_tr", "ht_hi", "ht_lo", "log_done", "l1", "l2", "top_done", "topi_done", "diff_done",
                   "gexp_done", "g1", "g2", "g3", "topf_done", "p1", "share_done", "st_tr", "st_done", "bias_mm", "x_bias",
                   "share_e_done",
                   "gu_in0", "gu_in1", "gu_hi_done", "gu_lo_done", "dn_hi_done", "dn_lo_done", "bias_done", "gu_mm", "gate_done", "up_done",
                   "sig_done", "glu_done", "act_done", "ah_done", "al_done", "dn_mm", "x_moe", "out_done"]
        z = {name: sem("z_" + name) for name in names2}
        UNITS_E = E * IB
        STEPS = IB * B

        def pe_setup2(pe):
            pe.wait_ge(z["mem_in"], 32)
            for b in range(B):
                for c in range(DC):
                    last = nc.tensor.transpose(bank[b % 2][:, 2 * P * (b // 2) + c * MEM:2 * P * (b // 2) + (c + 1) * MEM],
                                               ctx_raw[0:MEM, b, c * P:(c + 1) * P], ident[0:MEM, 0:MEM])
            last.then_inc(z["ctx_tr"], 1)
            pe.wait_ge(z["rw_in"], 16)
            for c in range(DC):
                last = nc.tensor.transpose(bank[2][:, c * E:(c + 1) * E], rw_raw[:, c * P:(c + 1) * P], ident[0:E, 0:E])
            last.then_inc(z["rw_tr"], 1)

        M_TR, M_SC, A_TR, A_OUT, H_TR, H_LOG, S_TR, S_OUT = bank

        def pe_a(pe, t):
            b = t // QB
            pe.wait_ge(z["m_norm_done"], t + 1)
            wait(pe, z["mt_done"], t)
            for c in range(DC):
                last = nc.tensor.transpose(M_TR[:, c * P:(c + 1) * P], ln_t[:, t % 2, c * P:(c + 1) * P], ident[:, :])
            last.then_inc(z["mt_tr"], 1)
            pe.wait_ge(z["mt_done"], t + 1)
            wait(pe, z["m1"], t)
            for c in range(DC):
                last = nc.tensor.matmul(M_SC[:, 0:MEM], xt[:, c, :], ctx_t[:, b, c, :], start=(c == 0), stop=(c == DC - 1))
            last.then_inc(z["msc_done"], 1)

        def pe_b(pe, t):
            b = t // QB
            pe.wait_ge(z["mexp_done"], t + 1)
            wait(pe, z["at_lo"], t)
            nc.tensor.transpose(A_TR[0:MEM, 0:P], m_sc[:, :], ident[:, :]).then_inc(z["at_tr"], 1)
            pe.wait_ge(z["at_lo"], t + 1)
            wait(pe, z["x_mem"], t)
            nc.tensor.matmul(A_OUT[:, :], a_st[:, :], ctx_hi[:, b, :], start=True, stop=False)
            nc.tensor.matmul(A_OUT[:, :], a_st[:, :], ctx_lo[:, b, :], start=False, stop=True).then_inc(z["read_done"], 1)

        def pe_c(pe, t):
            pe.wait_ge(z["h_norm_done"], t + 1)
            wait(pe, z["ht_lo"], t)
            for c in range(DC):
                last = nc.tensor.transpose(H_TR[:, c * P:(c + 1) * P], ln_h[:, t % 2, c * P:(c + 1) * P], ident[:, :])
            last.then_inc(z["ht_tr"], 1)
            pe.wait_ge(z["ht_lo"], t + 1)
            wait(pe, z["l2"], t)
            for a in range(2):
                for c in range(DC):
                    last = nc.tensor.matmul(H_LOG[:, 0:2 * E], xn[a][:, c, t * P:(t + 1) * P], rw_t[:, c, :],
                                            start=(a == 0 and c == 0), stop=(a == 1 and c == DC - 1))
            last.then_inc(z["log_done"], 1)

        def pe_d(pe, t):
            pe.wait_ge(z["share_done"], t + 1)
            wait(pe, z["st_done"], t)
            nc.tensor.transpose(S_TR[0:E, 0:P], share[:, t, :], ident[:, :]).then_inc(z["st_tr"], 1)
            pe.wait_ge(z["st_done"], t + 1)
            wait(pe, z["x_bias"], t)
            nc.tensor.matmul(S_OUT[:, :], share_t[:, :], down_bias[:, :], start=True, stop=True).then_inc(z["bias_mm"], 1)

        def act_a(act, t):
            act.wait_ge(z["mt_tr"], t + 1)
            wait(act, z["msc_done"], t)
            nc.scalar.activation(xt[:, :, :], M_TR[:, :].rearrange("p (c n) -> p c n", c=DC), ACT.Copy).then_inc(z["mt_done"], 1)

        def act_b(act, t):
            act.wait_ge(z["m3"], t + 1)
            nc.scalar.activation(m_sc[:, :], m_sc[:, :], ACT.Exp, bias=m_neg[:, 1:2], accum_out=m_neg[:, 2:3]).then_inc(z["mexp_done"], 1)
            act.wait_ge(z["at_tr"], t + 1)
            wait(act, z["read_done"], t)
            act_split(a_st[0:MEM, :], A_TR[0:MEM, 0:P], z["at_hi"])

        def act_c(act, t):
            act.wait_ge(z["ht_tr"], t + 1)
            act_split(xn[0][:, :, t * P:(t + 1) * P], H_TR[:, :].rearrange("p (c n) -> p c n", c=DC), z["ht_hi"])
            act.wait_ge(z["diff_done"], t + 1)
            nc.scalar.activation(gate2[:, 1:2], gate2[:, 0:1], ACT.Exp).then_inc(z["gexp_done"], 1)

        def act_d(act, t):
            act.wait_ge(z["st_tr"], t + 1)
            wait(act, z["bias_mm"], t)
            nc.scalar.activation(share_t[:, :], S_TR[0:E, 0:P], ACT.Copy).then_inc(z["st_done"], 1)

        def dve_b1(dve, t):
            b = t // QB
            dve.wait_ge(z["msc_done"], t + 1)
            wait(dve, z["at_tr"], t)
            nc.vector.tensor_tensor(m_sc[:, :], M_SC[:, 0:MEM], mask_scale[:, b, :], ALU.mult).then_inc(z["m1"], 1)
            dve.wait_ge(z["m1"], t + 1)
            nc.vector.tensor_tensor_reduce(out=m_sc[:, :], in0=m_sc[:, :], in1=mask_add[:, b, :], scale=1.0, scalar=NEG,
                                           op0=ALU.add, op1=ALU.max, accum_out=m_neg[:, 0:1]).then_inc(z["m2"], 1)
            dve.wait_ge(z["m2"], t + 1)
            nc.vector.tensor_scalar(m_neg[:, 1:2], m_neg[:, 0:1], -1.0, None, ALU.mult).then_inc(z["m3"], 1)

        def dve_b2(dve, t):
            b = t // QB
            dve.wait_ge(z["mexp_done"], t + 1)
            nc.vector.reciprocal(m_inv[:, 0:1], m_neg[:, 2:3]).then_inc(z["msum_inv"], 1)
            dve.wait_ge(z["msum_inv"], t + 1)
            nc.vector.tensor_tensor(m_inv[:, 1:2], m_inv[:, 0:1], valid[:, b:b + 1], ALU.mult).then_inc(z["m_inv_done"], 1)
            dve.wait_ge(z["at_hi"], t + 1)
            nc.vector.tensor_tensor(a_st[MEM:P, :], A_TR[0:MEM, 0:P], a_st[0:MEM, :].bitcast(F32), ALU.subtract).then_inc(z["at_lo"], 1)

        def dve_b3(dve, t):
            dve.wait_ge(z["read_done"], t + 1)
            dve.wait_ge(z["m_inv_done"], t + 1)
            nc.vector.scalar_tensor_tensor(out=x_res[:, t, :], in0=A_OUT[:, :], scalar=m_inv[:, 1:2], in1=x_res[:, t, :],
                                           op0=ALU.mult, op1=ALU.add).then_inc(z["x_mem"], 1)

        def dve_c1(dve, t):
            dve.wait_ge(z["ht_hi"], t + 1)
            dve_lo(xn[1][:, :, t * P:(t + 1) * P], H_TR[:, :].rearrange("p (c n) -> p c n", c=DC), xn[0][:, :, t * P:(t + 1) * P], z["ht_lo"])

        def dve_c2(dve, t):
            dve.wait_ge(z["log_done"], t + 1)
            nc.vector.tensor_tensor(logits[:, 0, :], H_LOG[:, 0:E], rb[:, :], ALU.add).then_inc(z["l1"], 1)
            dve.wait_ge(z["l1"], t + 1)
            nc.vector.tensor_tensor(logits[:, 1, :], H_LOG[:, E:2 * E], logits[:, 0, :], ALU.add).then_inc(z["l2"], 1)
            dve.wait_ge(z["l2"], t + 1)
            nc.vector.max(top[:, :], logits[:, 1, :]).then_inc(z["top_done"], 1)
            dve.wait_ge(z["top_done"], t + 1)
            nc.vector.tensor_tensor(gate2[:, 0:1], top[:, 1:2], top[:, 0:1], ALU.subtract).then_inc(z["diff_done"], 1)
            nc.vector.max_index(top_at[:, :], top[:, :], logits[:, 1, :]).then_inc(z["topi_done"], 1)
            dve.wait_ge(z["topi_done"], t + 1)
            nc.vector.tensor_copy(top_f[:, :], top_at[:, 0:2]).then_inc(z["topf_done"], 1)
            dve.wait_ge(z["gexp_done"], t + 1)
            nc.vector.tensor_scalar(gate2[:, 2:3], gate2[:, 1:2], 1.0, None, ALU.add).then_inc(z["g1"], 1)
            dve.wait_ge(z["g1"], t + 1)
            nc.vector.reciprocal(gate2[:, 3:4], gate2[:, 2:3]).then_inc(z["g2"], 1)
            dve.wait_ge(z["g2"], t + 1)
            nc.vector.tensor_tensor(gate2[:, 4:5], gate2[:, 3:4], gate2[:, 1:2], ALU.mult).then_inc(z["g3"], 1)
            dve.wait_ge(z["topf_done"], t + 1)
            dve.wait_ge(z["g3"], t + 1)
            for k in range(2):
                nc.vector.tensor_scalar(pick[:, k, :], iota[:, :], top_f[:, k:k + 1], gate2[:, 3 + k:4 + k], ALU.is_equal, ALU.mult).then_inc(z["p1"], 1)
            dve.wait_ge(z["p1"], 2 * t + 2)
            nc.vector.tensor_tensor(share[:, t, :], pick[:, 0, :], pick[:, 1, :], ALU.add).then_inc(z["share_done"], 1)

        def dve_d(dve, t):
            dve.wait_ge(z["bias_mm"], t + 1)
            nc.vector.tensor_tensor(x_res[:, t, :], S_OUT[:, :], x_res[:, t, :], ALU.add).then_inc(z["x_bias"], 1)

        def sp_weights(sp, e, ib):
            k, u = ib % 2, IB * e + ib
            wait(sp, z["gu_lo_done"], u - 1)
            wait(sp, z["gu_hi_done"], u - 1)
            wait(sp, z["dn_lo_done"], u - 1)
            wait(sp, z["bias_done"], 2 * u - 2)
            if not isinstance(e, int):
                settled(sp)
            gu_rows = gu_w.rearrange("e h j -> (e h) j")[bass.ds(e * D, D), 2 * P * ib:2 * P * (ib + 1)]
            sp.dma_start(gu_raw[:, k, :, :], gu_rows.rearrange("(c p) j -> p c j", p=P)).then_inc(z[f"gu_in{k}"], 16)
            sp.dma_start(dn_raw[:, k, :], down_w.rearrange("e i h -> (e i) h")[bass.ds(e * I + ib * P, P), :]).then_inc(z[f"gu_in{k}"], 16)
            sp.dma_start(bias_raw[:, k, :], gu_b.rearrange("e (q s) -> (e q) s", s=2)[bass.ds(e * I + ib * P, P), :]).then_inc(z[f"gu_in{k}"], 16)

        def raw_in(ib, e):
            return 96 * e + 48 * (ib // 2) + 48

        def act_weights(act, e, ib):
            k, u = ib % 2, IB * e + ib
            act.wait_ge(z[f"gu_in{k}"], raw_in(ib, e))
            wait(act, z["dn_mm"], 4 * B * (u - 1))
            act_split(gu[0][:, k, :, :, :].rearrange("p c s i -> p c i s"), gu_raw[:, k, :, :].rearrange("p c (i s) -> p c i s", s=2), z["gu_hi_done"])
            act_split(dn[0][:, k, :], dn_raw[:, k, :], z["dn_hi_done"])

        def pool_weights(pool, e, ib):
            k, u = ib % 2, IB * e + ib
            pool.wait_ge(z[f"gu_in{k}"], raw_in(ib, e))
            pool.wait_ge(z["gu_hi_done"], u + 1)
            nc.gpsimd.tensor_tensor(gu[1][:, k, :, :, :].rearrange("p c s i -> p c i s"), gu_raw[:, k, :, :].rearrange("p c (i s) -> p c i s", s=2),
                                    gu[0][:, k, :, :, :].rearrange("p c s i -> p c i s").bitcast(F32), ALU.subtract).then_inc(z["gu_lo_done"], 1)
            pool.wait_ge(z["dn_hi_done"], u + 1)
            nc.gpsimd.tensor_tensor(dn[1][:, k, :], dn_raw[:, k, :], dn[0][:, k, :].bitcast(F32), ALU.subtract).then_inc(z["dn_lo_done"], 1)

        def dve_bias(dve, e, ib):
            k, u = ib % 2, IB * e + ib
            dve.wait_ge(z[f"gu_in{k}"], raw_in(ib, e))
            wait(dve, z["up_done"], B * (u - 1))
            nc.vector.tensor_scalar(bias[:, k, 0:1], bias_raw[:, k, 0:1], 0.0, None, ALU.add).then_inc(z["bias_done"], 1)
            nc.vector.tensor_scalar(bias[:, k, 1:2], bias_raw[:, k, 1:2], 1.0, None, ALU.add).then_inc(z["bias_done"], 1)

        def pe_gu(pe, e, st_):
            ib, b = divmod(st_, B)
            k, i = ib % 2, STEPS * e + st_
            pe.wait_ge(z["gu_lo_done"], IB * e + ib + 1)
            wait(pe, z["up_done"], i - 1)
            for side in range(2):
                first = True
                for c in range(DC):
                    for sp_, mp in PASSES:
                        last = nc.tensor.matmul(bank[2 * (st_ % 2) + side][:, :], gu[sp_][:, k, c, side, :], xn[mp][:, c, b * L:(b + 1) * L],
                                                start=first, stop=(c == DC - 1 and (sp_, mp) == PASSES[-1]))
                        first = False
                last.then_inc(z["gu_mm"], 1)


        def pe_dn(pe, e, st_):
            ib, b = divmod(st_, B)
            k, i = ib % 2, STEPS * e + st_
            pe.wait_ge(z["al_done"], i + 1)
            pe.wait_ge(z["dn_lo_done"], IB * e + ib + 1)
            for t in range(QB):
                wait(pe, z["x_moe"], QB * i - QB + t + 1)
                for sp_, mp in PASSES:
                    last = nc.tensor.matmul(bank[4 + t][:, :], act_st[sp_][:, st_ % 2, t * P:(t + 1) * P], dn[mp][:, k, :],
                                            start=((sp_, mp) == PASSES[0]), stop=((sp_, mp) == PASSES[-1]))
                last.then_inc(z["dn_mm"], 1)

        def dve_gu(dve, e, st_):
            ib = st_ // B
            k, i, w = ib % 2, STEPS * e + st_, st_ % 2
            dve.wait_ge(z["bias_done"], 2 * (IB * e + ib) + 2)
            dve.wait_ge(z["gu_mm"], 2 * i + 1)
            nc.vector.tensor_scalar(gate[:, w, :], bank[2 * w][:, :], bias[:, k, 0:1], LIMIT, ALU.add, ALU.min).then_inc(z["gate_done"], 1)
            dve.wait_ge(z["gu_mm"], 2 * i + 2)
            wait(dve, z["ah_done"], i - 1)
            nc.vector.tensor_scalar(up[:, w, :], bank[2 * w + 1][:, :], bias[:, k, 1:2], LIMIT + 1.0, ALU.add, ALU.min).then_inc(z["up_done"], 1)

        def dve_act(dve, e, st_):
            i, w = STEPS * e + st_, st_ % 2
            dve.wait_ge(z["sig_done"], i + 1)
            nc.vector.tensor_tensor(sig[:, w, :], sig[:, w, :], gate[:, w, :], ALU.mult).then_inc(z["glu_done"], 1)
            dve.wait_ge(z["glu_done"], i + 1)
            nc.vector.scalar_tensor_tensor(out=up[:, w, :], in0=up[:, w, :], scalar=1.0 - LIMIT, in1=sig[:, w, :],
                                           op0=ALU.max, op1=ALU.mult).then_inc(z["act_done"], 1)

        def dve_al(dve, e, st_):
            i, w = STEPS * e + st_, st_ % 2
            dve.wait_ge(z["ah_done"], i + 1)
            dve_lo(act_st[1][:, w, :], up[:, w, :], act_st[0][:, w, :], z["al_done"])

        def dve_moe(dve, e, st_, t):
            b = st_ % B
            i = STEPS * e + st_
            tt = b * QB + t
            dve.wait_ge(z["dn_mm"], QB * i + t + 1)
            wait(dve, z["x_moe"], QB * i + t - STEPS)
            nc.vector.scalar_tensor_tensor(out=x_res[:, tt, :], in0=bank[4 + t][:, :], scalar=share_e[:, tt, :], in1=x_res[:, tt, :],
                                           op0=ALU.mult, op1=ALU.add).then_inc(z["x_moe"], 1)

        def act_step(act, e, st_):
            i, w = STEPS * e + st_, st_ % 2
            act.wait_ge(z["gate_done"], i + 1)
            wait(act, z["act_done"], i - 1)
            nc.scalar.activation(sig[:, w, :], gate[:, w, :], ACT.Sigmoid, scale=ALPHA).then_inc(z["sig_done"], 1)
            act.wait_ge(z["act_done"], i + 1)
            wait(act, z["dn_mm"], QB * (i - 1))
            act_split(act_st[0][:, w, :], up[:, w, :], z["ah_done"])

        def next_unit(e, ib):
            return (e, ib + 1) if ib + 1 < IB else (e + 1, 0)

        def pe_expert(pe, e, final):
            for st_ in range(STEPS):
                if st_ + 1 < STEPS:
                    pe_gu(pe, e, st_ + 1)
                elif not final:
                    pe_gu(pe, e + 1, 0)
                pe_dn(pe, e, st_)

        def act_expert(act, e, final):
            for st_ in range(STEPS):
                if st_ + 1 < STEPS:
                    act_step(act, e, st_ + 1)
                elif not final:
                    act_step(act, e + 1, 0)
                if st_ % B == 1 and not (final and st_ // B == IB - 1):
                    act_weights(act, *next_unit(e, st_ // B))

        def dve_expert(dve, e, final):
            wait(dve, z["x_moe"], QB * STEPS * e)
            nc.vector.tensor_copy(share_e[:, :, :], share_of(e)).then_inc(z["share_e_done"], 1)
            dve.wait_ge(z["share_e_done"], e + 1)
            for st_ in range(STEPS):
                ne, ns = (e, st_ + 1) if st_ + 1 < STEPS else (e + 1, 0)
                more = not (final and st_ + 1 == STEPS)
                if more:
                    dve_gu(dve, ne, ns)
                dve_moe(dve, e, st_, 0)
                if more:
                    dve_act(dve, ne, ns)
                dve_moe(dve, e, st_, 1)
                if more:
                    dve_al(dve, ne, ns)
                dve_moe(dve, e, st_, 2)
                dve_moe(dve, e, st_, 3)
                if st_ % B == 1 and not (final and st_ // B == IB - 1):
                    dve_bias(dve, *next_unit(e, st_ // B))

        def share_of(e):
            return share[:, :, bass.ds(e, 1)]

        def pool_expert(pool, e, final):
            for ib in range(IB):
                if not (final and ib == IB - 1):
                    pool_weights(pool, *next_unit(e, ib))

        with nc.Block() as block:

            @block.sync
            def _(sp):
                ctx_dup = ctx.rearrange("b m d -> m b d")
                sp.dma_start(ctx_raw[0:MEM, :, :], ctx_dup).then_inc(z["mem_in"], 16)
                sp.dma_start(ctx_raw[MEM:P, :, :], ctx_dup).then_inc(z["mem_in"], 16)
                sp.dma_start(mask_u8[:, :], mem_mask.rearrange("(o b) m -> o (b m)", o=1).partition_broadcast(P)).then_inc(z["mask_in"], 16)
                sp.dma_start(rw_raw[:, :], router_w).then_inc(z["rw_in"], 16)
                sp.dma_start(rb[:, :], router_b.rearrange("(o e) -> o e", o=1).partition_broadcast(P)).then_inc(z["small_in"], 16)
                sp.dma_start(iota[:, :], iota_t).then_inc(z["small_in"], 16)
                sp.dma_start(down_bias[:, :], down_b).then_inc(z["bd_in"], 16)
                for ib in range(IB):
                    sp_weights(sp, 0, ib)
                with sp.Fori(1, E) as e:
                    for ib in range(IB):
                        sp_weights(sp, e, ib)
                for b in range(B):
                    sp.wait_ge(z["x_moe"], QB * (E * STEPS - B + b + 1))
                    sp.dma_start(outr[:, b * QB:(b + 1) * QB, :], x_res[:, b * QB:(b + 1) * QB, :]).then_inc(z["out_done"], 16)
                sp.wait_ge(z["out_done"], 16 * B)

            @block.tensor
            def _(pe):
                pe_setup2(pe)
                pe.wait_ge(z["ctx_t_done"], 2)
                pe.wait_ge(z["ctx_lo_done"], 1)
                pe.wait_ge(z["rw_lo_done"], 1)
                pe.wait_ge(z["bd_in"], 16)
                for t in range(TT + 3):
                    if t < TT:
                        pe_a(pe, t)
                    if 1 <= t < TT + 1:
                        pe_b(pe, t - 1)
                    if 2 <= t < TT + 2:
                        pe_c(pe, t - 2)
                    if t >= 3:
                        pe_d(pe, t - 3)
                pe.wait_ge(z["x_bias"], TT)
                pe_gu(pe, 0, 0)
                pe_expert(pe, 0, False)
                with pe.Fori(1, E - 1) as e:
                    pe_expert(pe, e, False)
                pe_expert(pe, E - 1, True)

            @block.scalar
            def _(act):
                act.wait_ge(z["mem_in"], 32)
                act_split(ctx_hi[:, :, :], ctx_raw[:, :, :], z["ctx_hi_done"])
                act.wait_ge(z["ctx_tr"], 1)
                for k in range(2):
                    for half_ in range(2):
                        done = nc.scalar.activation(ctx_t[:, k + 2 * half_, :, :], bank[k][:, 2 * P * half_:2 * P * (half_ + 1)].rearrange("p (c m) -> p c m", c=DC), ACT.Copy)
                    done.then_inc(z["ctx_t_done"], 1)
                act.wait_ge(z["rw_tr"], 1)
                act_split(rw_t[:, :, 0:E], bank[2][:, 0:DC * E].rearrange("p (c e) -> p c e", c=DC), z["rw_hi_done"])
                for t in range(TT + 3):
                    if t < TT:
                        act_a(act, t)
                    if 1 <= t < TT + 1:
                        act_b(act, t - 1)
                    if 2 <= t < TT + 2:
                        act_c(act, t - 2)
                    if t >= 3:
                        act_d(act, t - 3)
                act_weights(act, 0, 0)
                act_step(act, 0, 0)
                act_expert(act, 0, False)
                with act.Fori(1, E - 1) as e:
                    act_expert(act, e, False)
                act_expert(act, E - 1, True)

            @block.vector
            def _(dve):
                dve.wait_ge(z["mask_in"], 16)
                nc.vector.tensor_copy(mask_f[:, :, :], mask_u8[:, :].rearrange("p (b m) -> p b m", b=B)).then_inc(z["mask_f_done"], 1)
                dve.wait_ge(z["mask_f_done"], 1)
                nc.vector.tensor_scalar(mask_scale[:, :, :], mask_f[:, :, :], float(np.float32(1.0) / np.sqrt(np.float32(D))), None, ALU.mult).then_inc(z["mask_tab"], 1)
                nc.vector.tensor_scalar(mask_add[:, :, :], mask_f[:, :, :], -1.0, -MASKED, ALU.add, ALU.mult).then_inc(z["mask_tab"], 1)
                nc.vector.reduce_max(valid[:, :], mask_f[:, :, :], AX.X).then_inc(z["mask_tab"], 1)
                dve.wait_ge(z["ctx_hi_done"], 1)
                dve_lo(ctx_lo[:, :, :], ctx_raw[:, :, :], ctx_hi[:, :, :], z["ctx_lo_done"])
                dve.wait_ge(z["rw_hi_done"], 1)
                dve_lo(rw_t[:, :, E:2 * E], bank[2][:, 0:DC * E].rearrange("p (c e) -> p c e", c=DC), rw_t[:, :, 0:E], z["rw_lo_done"])
                dve.wait_ge(z["mask_tab"], 3)
                dve.wait_ge(z["small_in"], 32)
                for t in range(TT + 3):
                    a, b_, c_, d_ = t < TT, 1 <= t < TT + 1, 2 <= t < TT + 2, t >= 3
                    if a:
                        ln_stats(nc, dve, z, "m_", t, x_res[:, t, :], stats, mv, var_eps)
                    if c_:
                        ln_stats(nc, dve, z, "h_", t - 2, x_res[:, t - 2, :], stats_h, mv_h, var_eps_h)
                    if b_:
                        dve_b1(dve, t - 1)
                    if a:
                        wait(dve, z["mt_tr"], t - 1)
                        ln_norm(nc, dve, z, "m_", t, x_res[:, t, :], ln_t[:, t % 2, :], mv, rstd)
                    if c_:
                        wait(dve, z["ht_tr"], t - 3)
                        ln_norm(nc, dve, z, "h_", t - 2, x_res[:, t - 2, :], ln_h[:, t % 2, :], mv_h, rstd_h)
                    if b_:
                        dve_b2(dve, t - 1)
                    if c_:
                        dve_c1(dve, t - 2)
                    if b_:
                        dve_b3(dve, t - 1)
                        dve.wait_ge(z["x_mem"], t)
                    if c_:
                        dve_c2(dve, t - 2)
                    if d_:
                        dve_d(dve, t - 3)
                dve.wait_ge(z["share_done"], TT)
                dve_bias(dve, 0, 0)
                dve_gu(dve, 0, 0)
                dve_act(dve, 0, 0)
                dve_al(dve, 0, 0)
                dve_expert(dve, 0, False)
                with dve.Fori(1, E - 1) as e:
                    dve_expert(dve, e, False)
                dve_expert(dve, E - 1, True)

            @block.gpsimd
            def _(pool):
                for t in range(TT + 2):
                    if t < TT:
                        ln_rstd(nc, pool, z, "m_", t, var_eps, half, rstd)
                    if t >= 2:
                        ln_rstd(nc, pool, z, "h_", t - 2, var_eps_h, half, rstd_h)
                pool_weights(pool, 0, 0)
                pool_expert(pool, 0, False)
                with pool.Fori(1, E - 1) as e:
                    pool_expert(pool, e, False)
                pool_expert(pool, E - 1, True)



_INS = ["x", "ctx_2048", "mask_BxS2_bk0", "L0_attn_Wq", "L0_attn_Wk", "L0_attn_Wv", "L0_attn_Wo",
        "L0_ffn_router_weight", "L0_ffn_router_bias", "L0_ffn_gate_up_proj", "L0_ffn_gate_up_proj_bias",
        "L0_ffn_down_proj", "L0_ffn_down_proj_bias"]


def _constants():
    inv = (1.0 / 10000.0 ** (np.arange(0, HD, 2, dtype=np.float32) / HD)).astype(np.float32)
    angle = (np.arange(L, dtype=np.float32)[:, None] * inv[None, :]).astype(np.float32)
    row = (np.arange(P) % HD) // 2
    sign = np.where(np.arange(P) % 2 == 0, -1.0, 1.0)[:, None]
    cos = np.cos(angle.astype(np.float64)).T[row].astype(np.float32)
    sin = (np.sin(angle.astype(np.float64)).T[row] * sign).astype(np.float32)
    causal = np.where(np.arange(L)[None, :] - (L - P) <= np.arange(P)[:, None], 0.0, NEG).astype(np.float32)
    iota = np.broadcast_to(np.arange(E, dtype=np.float32), (P, E)).copy()
    return {"cos": cos, "sin": sin, "causal": causal, "ident": np.eye(P, dtype=np.float32), "iota": iota}


def kernel(**inputs):
    import concourse.bacc as bacc
    from concourse.bass_utils import run_bass_kernel_spmd

    nc = bacc.Bacc("TRN2", target_bir_lowering=False, num_devices=1, dynamic_dma_scratch_size=1024)
    arrays, args = {}, []
    for name in _INS:
        a = np.ascontiguousarray(inputs[name])
        arrays[f"in_{name}"] = a
    for name, a in _constants().items():
        arrays[f"const_{name}"] = a
    for name, a in arrays.items():
        args.append(nc.dram_tensor(name, a.shape, mybir.dt.from_np(a.dtype), kind="ExternalInput").ap())
    out = nc.dram_tensor("out", (B, L, D), F32, kind="ExternalOutput").ap()
    decoder_layer(nc, *args, out)
    r = run_bass_kernel_spmd(nc, [arrays], core_ids=[0])
    return r.results[0]["out"]
```

```python
from contextlib import ExitStack

import numpy as np

import concourse.bass as bass
from concourse import mybir

F32 = mybir.dt.float32
F32R = mybir.dt.float32r
U32 = mybir.dt.uint32
U8 = mybir.dt.uint8
ALU = mybir.AluOpType
ACT = mybir.ActivationFunctionType
AX = mybir.AxisListType

P = 128
B, L, D = 4, 512, 512
T = B * L
TT = T // P
DC = D // P
HQ, HKV, HD = 32, 8, 64
G = HQ // HKV
QB = L // P
MEM = 64
E, I = 8, 512
IB = I // P
EPS = 1e-5
NEG = -3.0e38
MASKED = -1e30
M_SCALE = float(np.float32(1.0) / np.sqrt(np.float32(D)))
ALPHA, LIMIT = 1.702, 7.0
GROUPS = HKV
HEADS = B * G
PASSES = ((0, 0), (0, 1), (1, 0))

P_AT = [0, P, 3 * P, 6 * P]
P_LEN = 10 * P
PT_ZERO = 4 * P
PT_AT = [0, 5 * P, 9 * P, 8 * P]
PT_LEN = 12 * P
UNITS = [[(0, 0), (0, 1), (0, 2), (0, 3)], [(1, 1), (1, 2), (1, 3), (3, 3)], [(2, 2), (2, 3)]]
UNIT_PT = [0, PT_AT[1], PT_AT[2]]
W1_SLOTS = {(2, 1): 2, (2, 2): 0, (2, 3): 1}


def wait(eng, sem, value):
    if isinstance(value, int) and value <= 0:
        return
    eng.wait_ge(sem, value)


def ln_stats(nc, dve, s, norms):
    for pre, t, src, stats, mv, var_eps in norms:
        nc.vector.bn_stats(stats[:, t % 2, :], src).then_inc(s[pre + "stat_done"], 1)
    for pre, t, src, stats, mv, var_eps in norms:
        dve.wait_ge(s[pre + "stat_done"], t + 1)
        wait(dve, s[pre + "norm_done"], t - 1)
        nc.vector.bn_aggr(mv[:, t % 2, :], stats[:, t % 2, :]).then_inc(s[pre + "aggr_done"], 1)
    for pre, t, src, stats, mv, var_eps in norms:
        k = t % 2
        dve.wait_ge(s[pre + "aggr_done"], t + 1)
        nc.vector.tensor_scalar(var_eps[:, k, 0:1], mv[:, k, 1:2], EPS, None, ALU.add).then_inc(s[pre + "eps_done"], 1)
        nc.vector.tensor_scalar(var_eps[:, k, 1:2], mv[:, k, 0:1], -1.0, None, ALU.mult).then_inc(s[pre + "eps_done"], 1)


def ln_norm(nc, pool, s, pre, t, src, dst, var_eps, half, rstd):
    k = t % 2
    pool.wait_ge(s[pre + "eps_done"], 2 * t + 2)
    nc.gpsimd.tensor_tensor(rstd[:, k:k + 1], var_eps[:, k, 0:1], half[:, :], ALU.pow).then_inc(s[pre + "rstd_done"], 1)
    pool.wait_ge(s[pre + "rstd_done"], t + 1)
    nc.gpsimd.tensor_scalar(dst, src, var_eps[:, k, 1:2], rstd[:, k:k + 1], ALU.add, ALU.mult).then_inc(s[pre + "norm_done"], 1)


def decoder_layer(nc, x, ctx, ctx_cols, mem_mask, wqkv, wo_rows, router_cols, router_b, gu_w, gu_b, down_w, down_b,
                  cos_t, sin_t, causal_t, ident_t, iota_t, out):
    stack = ExitStack()
    with stack:
        def sb(name, shape, dt=F32):
            return stack.enter_context(nc.sbuf_tensor(name, shape, dt))

        def sem(name):
            return stack.enter_context(nc.semaphore(name))

        x_res = sb("x_res", [P, TT, D])
        xn = [sb("xn_hi", [P, DC, T], F32R), sb("xn_lo", [P, DC, T], F32R)]
        ident = sb("ident", [P, P])
        stats = sb("stats", [P, 2, 6])
        mv = sb("mv", [P, 2, 2])
        var_eps = sb("var_eps", [P, 2, 2])
        half = sb("half", [P, 1])
        rstd = sb("rstd", [P, 2])

        bank = [stack.enter_context(nc.psum_tensor(f"bank{i}", [P, 512], F32)) for i in range(8)]
        xr = x.rearrange("b (t p) d -> p (b t) d", p=P)
        outr = out.rearrange("b (t p) d -> p (b t) d", p=P)

        attn = ExitStack()

        def sa(name, shape, dt=F32):
            return attn.enter_context(nc.sbuf_tensor(name, shape, dt))

        w1_raw = sa("w1_raw", [P, DC, 3 * P])
        w2_raw = sa("w2_raw", [P, 2, D])
        w1 = [sa("w1_hi", [P, DC, 3 * P], F32R), sa("w1_lo", [P, DC, 3 * P], F32R)]
        w2 = [sa("w2_hi", [P, 2, D], F32R), sa("w2_lo", [P, 2, D], F32R)]
        cos = sa("cos", [P, L])
        sin = sa("sin", [P, L])
        causal = sa("causal", [P, L])
        probs = sa("probs", [P, 2, P_LEN])
        pt = [[sa(f"pt{b}_hi", [P, PT_LEN], F32R), sa(f"pt{b}_lo", [P, PT_LEN], F32R)] for b in range(2)]
        q_st = sa("q_st", [P, G, L], F32R)
        k_hi = sa("k_hi", [P, 2, L], F32R)
        k_lo = sa("k_lo", [P, 2, L], F32R)
        v_t = sa("v_t", [HD, L])
        v_st = sa("v_st", [P, 2, QB, P], F32R)
        rot = sa("rot", [P, L])
        rope = sa("rope", [P, 2, L])
        wo_out = sa("wo_out", [P, QB, D])
        o_part = sa("o_part", [HD, L])
        o_f = sa("o_f", [P, L])
        o_st = [sa("o_hi", [P, 4, L], F32R), sa("o_lo", [P, 4, L], F32R)]
        neg_max = sa("neg_max", [P, 2, QB])
        row_sum = sa("row_sum", [P, 2, QB])
        row_inv = sa("row_inv", [P, 2, QB])
        ln_out = probs

        S_BANK, T_BANK, O_BANK, PJ_BANK, WO_BANK = bank[0:3], bank[3:5], bank[5], bank[6], bank[7]

        s = {name: sem(name) for name in (
            "const_in", "ident_in", "x_first", "x_in0", "x_in1", "x_in2", "x_in3", "zero_done", "half_done",
            "stat_done", "aggr_done", "eps_done", "rstd_done", "norm_done", "lnt_done", "ln_hi", "ln_lo",
            "w1_in", "w2_in", "w1_hi_done", "w1_lo_done", "w2_hi_done",
            "w2_lo_done", "proj_done", "vt_done", "rope_in", "rot_sin", "rope_sum", "rope_hi", "k_lo_done", "q_lo_done",
            "v_tr", "v_hi_done", "v_lo_done", "scores_done", "masked_done", "exp_done",
            "recip_done", "pnorm_done", "ptrans_done", "pt_hi_done", "pt_lo_done", "pv_done", "opart_done",
            "oadd_done", "o_hi_done", "o_lo_done", "wo_done", "wo_out_done", "woacc_done")}

        def settled(eng):
            eng.nop(nofuse=True)

        def pe_ln(pe, t):
            pe.wait_ge(s["norm_done"], t + 1)
            wait(pe, s["ln_lo"], t - 3)
            for c in range(DC):
                last = nc.tensor.transpose(bank[t % 4][:, c * P:(c + 1) * P], ln_out[:, t % 2, c * P:(c + 1) * P], ident[:, :])
            last.then_inc(s["lnt_done"], 1)

        def pe_proj(pe, b, r):
            first = True
            for c in range(DC):
                for sp, mp in PASSES:
                    last = nc.tensor.matmul(PJ_BANK[:, :], w1[sp][:, c, r * P:(r + 1) * P], xn[mp][:, c, b * L:(b + 1) * L],
                                            start=first, stop=(c == DC - 1 and (sp, mp) == PASSES[-1]))
                    first = False
            last.then_inc(s["proj_done"], 1)

        def pe_vt(pe, m):
            pe.wait_ge(s["vt_done"], m + 1)
            settled(pe)
            for j in range(QB):
                last = nc.tensor.transpose(PJ_BANK[:, j * HD:(j + 1) * HD], v_t[:, j * P:(j + 1) * P], ident[0:HD, 0:HD])
            last.then_inc(s["v_tr"], 1)

        def pe_scores(pe, n, m, h, kb):
            pe.wait_ge(s["k_lo_done"], 2 * m + 2)
            pe.wait_ge(s["q_lo_done"], 2 * m + 1 + (h >= 2))
            for k, blocks in enumerate(((3,), (2,), (1, 0))):
                wait(pe, s["masked_done"], 4 * n - (3, 2, 0)[k])
                for i in blocks:
                    cols = P * (i + 1) if i else 2 * P
                    at = 2 * P if i == 0 else 0
                    for a, kk in enumerate((k_hi, k_lo)):
                        last = nc.tensor.matmul(S_BANK[k][:, at:at + cols], q_st[:, h, i * P:(i + 1) * P], kk[:, kb, 0:cols],
                                                start=(a == 0), stop=(a == 1))
                last.then_inc(s["scores_done"], 1)

        def pe_ptrans(pe, n, hb, u):
            if u == 0:
                pe.wait_ge(s["pnorm_done"], 4 * n + 4)
            wait(pe, s["pt_lo_done"], 3 * n + (0, 0, 1)[u])
            for k, (j, i) in enumerate(UNITS[u]):
                last = nc.tensor.transpose(T_BANK[u % 2][:, k * P:(k + 1) * P],
                                           probs[:, hb, P_AT[i] + j * P:P_AT[i] + (j + 1) * P], ident[:, :])
            last.then_inc(s["ptrans_done"], 1)

        def pe_pv(pe, n, m, hb, vb):
            pe.wait_ge(s["pt_lo_done"], 3 * n + 3)
            pe.wait_ge(s["v_lo_done"], m + 1)
            wait(pe, s["oadd_done"], n)
            for j in range(QB):
                for a in range(2):
                    if j == 3:
                        rhs = pt[hb][a][:, PT_ZERO:PT_ZERO + 8 * P].rearrange("p (z c) -> p z c", z=2)[:, :, 0:P]
                        dst = O_BANK[:, 2 * P:4 * P].rearrange("p (z c) -> p z c", z=2)
                    else:
                        rhs = pt[hb][a][:, PT_AT[j]:PT_AT[j] + (QB - j) * P]
                        dst = O_BANK[:, j * P:4 * P]
                    last = nc.tensor.matmul(dst, v_st[:, vb, j, :], rhs, start=(j == 0 and a == 0), stop=(j == QB - 1 and a == 1))
            last.then_inc(s["pv_done"], 1)

        def pe_wo(pe, m, mb, t, dst=None):
            pe.wait_ge(s["o_lo_done"], 2 * m + 2)
            if dst is None:
                dst = WO_BANK
                wait(pe, s["wo_out_done"], 4 * m + t)
            first = True
            for k in range(2):
                for sp, mp in PASSES:
                    last = nc.tensor.matmul(dst[:, :], o_st[sp][:, 2 * mb + k, t * P:(t + 1) * P], w2[mp][:, k, :],
                                            start=first, stop=(k == 1 and (sp, mp) == PASSES[-1]))
                    first = False
            last.then_inc(s["wo_done"], 1)

        def pe_group(pe, g):
            for c in range(HEADS):
                b, h = divmod(c, G)
                n, m = HEADS * g + c, B * g + b
                begun = not (isinstance(g, int) and g == 0 and c == 0)
                more = not (isinstance(g, int) and g == GROUPS - 1 and c == HEADS - 1)
                next_batch = not (isinstance(g, int) and g == GROUPS - 1 and b == B - 1)
                last_batch = not (isinstance(g, int) and g == 0 and b == 0)
                batch_before_last = not (isinstance(g, int) and g == 0 and b < 2)
                if begun:
                    pe_ptrans(pe, n - 1, (c + 1) % 2, 2)
                if more:
                    pe_scores(pe, n + 1, m if h < G - 1 else m + 1, (h + 1) % G, (b + (h == G - 1)) % 2)
                if h < 3 and b == 3 and next_batch:
                    pe.wait_ge(s["w1_lo_done"], 3 * g + 4 + h)
                if h == 0 and next_batch:
                    pe.wait_ge(s["v_lo_done"], m + 1)
                    pe_proj(pe, (b + 1) % B, 2)
                if h == 1 and next_batch:
                    pe.wait_ge(s["rope_in"], 3 * m + 4)
                    pe.wait_ge(s["vt_done"], m + 2)
                    pe_proj(pe, (b + 1) % B, 0)
                if h == 2 and next_batch:
                    pe.wait_ge(s["rope_in"], 3 * m + 5)
                    pe_proj(pe, (b + 1) % B, 1)
                if h == 3 and next_batch:
                    pe.wait_ge(s["rope_in"], 3 * m + 6)
                    pe_vt(pe, m + 1)
                if h == 3 and last_batch:
                    pe_wo(pe, m - 1, (b - 1) % 2, 2)
                pe_ptrans(pe, n, c % 2, 0)
                pe_ptrans(pe, n, c % 2, 1)
                if begun:
                    pe_pv(pe, n - 1, m if h else m - 1, (c + 1) % 2, (b if h else b + 1) % 2)
                if h in (1, 2) and last_batch:
                    if h == 1 and b == 1:
                        pe.wait_ge(s["w2_lo_done"], 2 * g + 2)
                    pe_wo(pe, m - 1, (b - 1) % 2, h - 1)
                if h == 0 and batch_before_last:
                    pe_wo(pe, m - 2, b % 2, 3)

        def act_split(dst, src, sem_):
            nc.scalar.activation(dst, src, ACT.Copy).then_inc(sem_, 1)

        def act_exp(act, n, hb):
            for i in (3, 2, 1, 0):
                act.wait_ge(s["masked_done"], 4 * n + 4 - i)
                row = probs[:, hb, P_AT[i]:P_AT[i] + (i + 1) * P]
                nc.scalar.activation(row, row, ACT.Exp, bias=neg_max[:, hb, i:i + 1], scale=-1.0,
                                     accum_out=row_sum[:, hb, i:i + 1]).then_inc(s["exp_done"], 1)

        def act_rope(act, m, r, mb):
            act.wait_ge(s["rope_sum"], 3 * m + r + 1)
            if r == 0:
                wait(act, s["scores_done"], 12 * m - 12)
                act_split(k_hi[0:HD, mb, :], rope[0:HD, mb, :], s["rope_hi"])
                act_split(k_hi[HD:P, mb, :], rope[0:HD, mb, :], s["rope_hi"])
            else:
                wait(act, s["scores_done"], 12 * m - 12 + 6 * r)
                act_split(q_st[0:HD, 2 * r - 2, :], rope[0:HD, (mb + r) % 2, :], s["rope_hi"])
                act_split(q_st[HD:P, 2 * r - 1, :], rope[HD:P, (mb + r) % 2, :], s["rope_hi"])

        def act_vt(act, m, r_sem_value):
            act.wait_ge(s["proj_done"], r_sem_value)
            wait(act, s["v_tr"], m)
            act_split(v_t[:, :], PJ_BANK[HD:P, :], s["vt_done"])

        def act_v(act, m, vb):
            act.wait_ge(s["v_tr"], m + 1)
            wait(act, s["pv_done"], 4 * m - 4)
            act_split(v_st[:, vb, :, 0:HD], PJ_BANK[:, 0:QB * HD].rearrange("p (j d) -> p j d", j=QB), s["v_hi_done"])

        def act_w1(act, g, r):
            act.wait_ge(s["w1_in"], 16 * g + 16)
            wait(act, s["proj_done"], 12 * g - (1, 0, 2)[r])
            act_split(w1[0][:, :, r * P:(r + 1) * P], w1_raw[:, :, r * P:(r + 1) * P], s["w1_hi_done"])

        def act_w2(act, g):
            act.wait_ge(s["w2_in"], 16 * g + 16)
            wait(act, s["wo_done"], 16 * g)
            for k in range(2):
                act_split(w2[0][:, k, :], w2_raw[:, k, :], s["w2_hi_done"])

        def act_pt(act, n, hb, u):
            act.wait_ge(s["ptrans_done"], 3 * n + u + 1)
            if u == 0:
                wait(act, s["pv_done"], n - 1)
            w = P * len(UNITS[u])
            act_split(pt[hb][0][:, UNIT_PT[u]:UNIT_PT[u] + w], T_BANK[u % 2][:, 0:w], s["pt_hi_done"])

        def act_opart(act, n):
            act.wait_ge(s["pv_done"], n + 1)
            wait(act, s["oadd_done"], n)
            act_split(o_part[:, :], O_BANK[HD:P, :], s["opart_done"])

        def act_o(act, n, m, k):
            act.wait_ge(s["oadd_done"], n + 1)
            wait(act, s["wo_done"], 4 * m - 4)
            act_split(o_st[0][:, k, :], o_f[:, :], s["o_hi_done"])

        def act_wo(act, m, t, src=WO_BANK):
            act.wait_ge(s["wo_done"], 4 * m + t + 1)
            wait(act, s["woacc_done"], 4 * m + t - 3)
            nc.scalar.activation(wo_out[:, t, :], src[:, :], ACT.Copy).then_inc(s["wo_out_done"], 1)

        def act_group(act, g):
            for c in range(HEADS):
                b, h = divmod(c, G)
                n, m = HEADS * g + c, B * g + b
                begun = not (isinstance(g, int) and g == 0 and c == 0)
                more = not (isinstance(g, int) and g == GROUPS - 1 and c == HEADS - 1)
                last_batch = not (isinstance(g, int) and g == 0 and b == 0)
                next_batch = not (isinstance(g, int) and g == GROUPS - 1 and b == B - 1)
                if begun:
                    act_pt(act, n - 1, (c + 1) % 2, 2)
                if h == 0 and begun:
                    act_rope(act, m, 2, b % 2)
                if h in (1, 2) and next_batch:
                    act_rope(act, m + 1, h - 1, (b + 1) % 2)
                if more:
                    act_exp(act, n + 1, (c + 1) % 2)
                if h == 0 and next_batch:
                    act_vt(act, m + 1, 3 * m + 4)
                act_pt(act, n, c % 2, 0)
                act_pt(act, n, c % 2, 1)
                if h == 3 and last_batch:
                    act_wo(act, m - 1, 2)
                if h == 3 and next_batch:
                    act_v(act, m + 1, (b + 1) % 2)
                if begun:
                    act_opart(act, n - 1)
                if h in (1, 2) and last_batch:
                    act_wo(act, m - 1, h - 1)
                if h == 0 and not (isinstance(g, int) and g == 0 and b < 2):
                    act_wo(act, m - 2, 3)
                if begun and h % 2 == 0:
                    act_o(act, n - 1, m if h else m - 1, (c // 2 - 1) % 4)
                if h == 0 and b == 1:
                    act_w2(act, g)
                if (b, h) in W1_SLOTS and not (isinstance(g, int) and g == GROUPS - 1):
                    act_w1(act, g + 1, W1_SLOTS[b, h])

        def dve_lo(dst, src, hi, sem_):
            nc.vector.tensor_tensor(dst, src, hi.bitcast(F32), ALU.subtract).then_inc(sem_, 1)

        def dve_masked(dve, n, hb):
            wait(dve, s["ptrans_done"], 3 * n - 3)
            for i in (3, 2, 1, 0):
                k = (2, 2, 1, 0)[i]
                if i:
                    dve.wait_ge(s["scores_done"], 3 * n + k + 1)
                    settled(dve)
                at = 2 * P if i == 0 else 0
                nc.vector.tensor_tensor_reduce(
                    out=probs[:, hb, P_AT[i]:P_AT[i] + (i + 1) * P], in0=S_BANK[k][:, at:at + (i + 1) * P],
                    in1=causal[:, (QB - 1 - i) * P:L], scale=-HD ** -0.5, scalar=-NEG, op0=ALU.add, op1=ALU.min,
                    accum_out=neg_max[:, hb, i:i + 1]).then_inc(s["masked_done"], 1)

        def dve_recip(dve, n, hb):
            dve.wait_ge(s["exp_done"], 4 * n + 4)
            nc.vector.reciprocal(row_inv[:, hb, :], row_sum[:, hb, :]).then_inc(s["recip_done"], 1)

        def dve_rope_in(dve, m, r, mb):
            dve.wait_ge(s["proj_done"], 3 * m + r + 1)
            wait(dve, s["rope_sum"], 3 * m + r)
            if r == 2:
                dve.wait_ge(s["k_lo_done"], 2 * m + 2)
            else:
                wait(dve, s["q_lo_done"], 2 * m + r - 1)
            rows = HD if r == 0 else P
            nc.vector.tensor_tensor(rope[0:rows, (mb + r) % 2, :], PJ_BANK[0:rows, :], cos[0:rows, :], ALU.mult)
            nc.vector.stream_shuffle(rot[0:rows, :], PJ_BANK[0:rows, :], [p ^ 1 for p in range(32)]).then_inc(s["rope_in"], 1)

        def dve_q_lo(dve, m, r, mb):
            dve.wait_ge(s["rope_hi"], 6 * m + 2 * r + 2)
            a, c = 2 * r - 2, 2 * r - 1
            nc.vector.tensor_tensor(q_st[HD:P, a, :], rope[0:HD, (mb + r) % 2, :], q_st[0:HD, a, :].bitcast(F32), ALU.subtract)
            nc.vector.tensor_tensor(q_st[0:HD, c, :], rope[HD:P, (mb + r) % 2, :], q_st[HD:P, c, :].bitcast(F32), ALU.subtract).then_inc(s["q_lo_done"], 1)

        def dve_v(dve, m, vb):
            dve.wait_ge(s["v_hi_done"], m + 1)
            dve_lo(v_st[:, vb, :, HD:P], PJ_BANK[:, 0:QB * HD].rearrange("p (j d) -> p j d", j=QB), v_st[:, vb, :, 0:HD], s["v_lo_done"])

        def w1_lo(vec, eng, g, r):
            eng.wait_ge(s["w1_hi_done"], 3 * g + (2, 3, 1)[r])
            vec.tensor_tensor(w1[1][:, :, r * P:(r + 1) * P], w1_raw[:, :, r * P:(r + 1) * P],
                              w1[0][:, :, r * P:(r + 1) * P].bitcast(F32), ALU.subtract).then_inc(s["w1_lo_done"], 1)

        def dve_w2(dve, g):
            for k in range(2):
                dve.wait_ge(s["w2_hi_done"], 2 * g + k + 1)
                dve_lo(w2[1][:, k, :], w2_raw[:, k, :], w2[0][:, k, :], s["w2_lo_done"])

        def dve_pt(dve, n, hb, u):
            dve.wait_ge(s["pt_hi_done"], 3 * n + u + 1)
            w = P * len(UNITS[u])
            dve_lo(pt[hb][1][:, UNIT_PT[u]:UNIT_PT[u] + w], T_BANK[u % 2][:, 0:w], pt[hb][0][:, UNIT_PT[u]:UNIT_PT[u] + w], s["pt_lo_done"])

        def dve_oadd(dve, n, odd, pairs_before):
            dve.wait_ge(s["opart_done"], n + 1)
            wait(dve, s["o_lo_done"], pairs_before)
            r = HD if odd else 0
            nc.vector.tensor_tensor(o_f[r:r + HD, :], O_BANK[0:HD, :], o_part[:, :], ALU.add).then_inc(s["oadd_done"], 1)

        def dve_o(dve, pair, k):
            dve.wait_ge(s["o_hi_done"], pair + 1)
            dve_lo(o_st[1][:, k, :], o_f[:, :], o_st[0][:, k, :], s["o_lo_done"])

        def dve_group(dve, g):
            for c in range(HEADS):
                b, h = divmod(c, G)
                n, m = HEADS * g + c, B * g + b
                begun = not (isinstance(g, int) and g == 0 and c == 0)
                more = not (isinstance(g, int) and g == GROUPS - 1 and c == HEADS - 1)
                next_batch = not (isinstance(g, int) and g == GROUPS - 1 and b == B - 1)
                if more:
                    dve_masked(dve, n + 1, (c + 1) % 2)
                if begun:
                    dve_pt(dve, n - 1, (c + 1) % 2, 2)
                if begun and h % 2 == 1 and c > 0 and not (isinstance(g, int) and g == 0 and c == 1):
                    dve_o(dve, HEADS // 2 * g + (c - 1) // 2 - 1, ((c - 1) // 2 - 1) % 4)
                if h == 0 and begun:
                    dve_q_lo(dve, m, 2, b % 2)
                if h == 2 and next_batch:
                    dve_q_lo(dve, m + 1, 1, (b + 1) % 2)
                if h == 1 and b == 1:
                    dve_w2(dve, g)
                if h < 3 and next_batch:
                    dve_rope_in(dve, m + 1, h, (b + 1) % 2)
                if more:
                    dve_recip(dve, n + 1, (c + 1) % 2)
                dve_pt(dve, n, c % 2, 0)
                dve_pt(dve, n, c % 2, 1)
                if h == 3 and next_batch:
                    dve_v(dve, m + 1, (b + 1) % 2)
                if begun:
                    dve_oadd(dve, n - 1, (c - 1) % 2, HEADS // 2 * g + ((c - 1) // 2 if c else -1))

        def pool_rope(pool, m, r, mb):
            pool.wait_ge(s["rope_in"], 3 * m + r + 1)
            rows = HD if r == 0 else P
            nc.gpsimd.tensor_tensor(rot[0:rows, :], rot[0:rows, :], sin[0:rows, :], ALU.mult).then_inc(s["rot_sin"], 1)
            pool.wait_ge(s["rot_sin"], 3 * m + r + 1)
            nc.gpsimd.tensor_tensor(rope[0:rows, (mb + r) % 2, :], rope[0:rows, (mb + r) % 2, :], rot[0:rows, :], ALU.add).then_inc(s["rope_sum"], 1)

        def pool_norm(pool, n, hb):
            pool.wait_ge(s["recip_done"], n + 1)
            settled(pool)
            for i in (3, 2, 1, 0):
                row = probs[:, hb, P_AT[i]:P_AT[i] + (i + 1) * P]
                nc.gpsimd.tensor_scalar(row, row, row_inv[:, hb, i:i + 1], 0.0, ALU.mult, ALU.add).then_inc(s["pnorm_done"], 1)

        def pool_k_lo(pool, m, mb):
            pool.wait_ge(s["rope_hi"], 6 * m + 2)
            wait(pool, s["pnorm_done"], 16 * m - 8)
            wait(pool, s["woacc_done"], 4 * m - 8)
            for half_ in range(2):
                nc.gpsimd.tensor_tensor(k_lo[half_ * HD:(half_ + 1) * HD, mb, :], rope[0:HD, mb, :], k_hi[0:HD, mb, :].bitcast(F32),
                                        ALU.subtract).then_inc(s["k_lo_done"], 1)
            pool.wait_ge(s["k_lo_done"], 2 * m + 2)

        def pool_woacc(pool, m, b, t):
            pool.wait_ge(s["wo_out_done"], 4 * m + t + 1)
            tile = x_res[:, b * QB + t, :]
            nc.gpsimd.tensor_tensor(tile, wo_out[:, t, :], tile, ALU.add).then_inc(s["woacc_done"], 1)

        def pool_group(pool, g):
            for c in range(HEADS):
                b, h = divmod(c, G)
                n, m = HEADS * g + c, B * g + b
                next_batch = not (isinstance(g, int) and g == GROUPS - 1 and b == B - 1)
                last_batch = not (isinstance(g, int) and g == 0 and b == 0)
                if h == 1 and next_batch:
                    pool_k_lo(pool, m + 1, (b + 1) % 2)
                if h < 3 and next_batch:
                    pool_rope(pool, m + 1, h, (b + 1) % 2)
                if not (isinstance(g, int) and g == GROUPS - 1 and c == HEADS - 1):
                    pool_norm(pool, n + 1, (c + 1) % 2)
                if h and last_batch:
                    pool_woacc(pool, m - 1, (b - 1) % B, h - 1)
                if h == 0 and not (isinstance(g, int) and g == 0 and b < 2):
                    pool_woacc(pool, m - 2, (b - 2) % B, 3)
                if (b, h) in W1_SLOTS and not (isinstance(g, int) and g == GROUPS - 1):
                    w1_lo(nc.gpsimd, pool, g + 1, W1_SLOTS[b, h])

        def sp_w1(sp, g):
            wait(sp, s["w1_lo_done"], 3 * g)
            if not isinstance(g, int):
                settled(sp)
            sp.dma_start(w1_raw[:, :, :], wqkv[bass.ds(g * P, P), :, :]).then_inc(s["w1_in"], 16)

        def sp_w2(sp, g):
            wait(sp, s["w2_lo_done"], 2 * g)
            if not isinstance(g, int):
                settled(sp)
            sp.dma_start(w2_raw[:, :, :], wo_rows[bass.ds(g * P, P), :, :]).then_inc(s["w2_in"], 16)

        with nc.Block() as block:

            @block.sync
            def _(sp):
                sp.dma_start(x_res[:, 0:1, :], xr[:, 0:1, :]).then_inc(s["x_first"], 16)
                sp.dma_start(x_res[:, 1:QB, :], xr[:, 1:QB, :]).then_inc(s["x_in0"], 16)
                sp_w1(sp, 0)
                for b in range(1, B):
                    sp.dma_start(x_res[:, b * QB:(b + 1) * QB, :], xr[:, b * QB:(b + 1) * QB, :]).then_inc(s[f"x_in{b}"], 16)
                    if b == 1:
                        sp.dma_start(cos[:, :], cos_t).then_inc(s["const_in"], 16)
                        sp.dma_start(sin[:, :], sin_t).then_inc(s["const_in"], 16)
                sp.dma_start(causal[:, :], causal_t).then_inc(s["const_in"], 16)
                sp_w2(sp, 0)
                with sp.Fori(1, GROUPS) as g:
                    sp_w1(sp, g)
                    sp_w2(sp, g)

            @block.tensor
            def _(pe):
                pe.wait_ge(s["ident_in"], 16)
                pe.wait_ge(s["zero_done"], 4)
                for t in range(TT):
                    pe_ln(pe, t)
                    if t == 6:
                        pe.wait_ge(s["w1_lo_done"], 3)
                        pe.wait_ge(s["ln_lo"], QB)
                        pe_proj(pe, 0, 2)
                    if t == 9:
                        pe.wait_ge(s["rope_in"], 1)
                        pe.wait_ge(s["vt_done"], 1)
                        pe_proj(pe, 0, 0)
                    if t == 12:
                        pe.wait_ge(s["rope_in"], 2)
                        pe_proj(pe, 0, 1)
                    if t == 14:
                        pe.wait_ge(s["rope_in"], 3)
                        pe_vt(pe, 0)
                pe.wait_ge(s["ln_lo"], TT)
                pe_scores(pe, 0, 0, 0, 0)
                pe_group(pe, 0)
                with pe.Fori(1, GROUPS - 1) as g:
                    pe_group(pe, g)
                pe_group(pe, GROUPS - 1)
                pe_ptrans(pe, HEADS * GROUPS - 1, 1, 2)
                pe_pv(pe, HEADS * GROUPS - 1, B * GROUPS - 1, 1, 1)
                pe_wo(pe, B * GROUPS - 2, 0, 3)
                for t in range(QB):
                    pe_wo(pe, B * GROUPS - 1, 1, t, (*S_BANK, PJ_BANK)[t])

            @block.scalar
            def _(act):
                act.dma_start(ident[:, :], ident_t).then_inc(s["ident_in"], 16)

                def ln_hi(t):
                    act.wait_ge(s["lnt_done"], t + 1)
                    act_split(xn[0][:, :, t * P:(t + 1) * P], bank[t % 4][:, :].rearrange("p (c n) -> p c n", c=DC), s["ln_hi"])

                for t in range(TT):
                    ln_hi(t)
                    if t == 3:
                        for r in W1_SLOTS.values():
                            act_w1(act, 0, r)
                    if t == 7:
                        act_vt(act, 0, 1)
                    if t == 10:
                        act_rope(act, 0, 0, 0)
                    if t == 13:
                        act_rope(act, 0, 1, 0)
                act_v(act, 0, 0)
                act_rope(act, 0, 2, 0)
                act_exp(act, 0, 0)
                act_group(act, 0)
                with act.Fori(1, GROUPS - 1) as g:
                    act_group(act, g)
                act_group(act, GROUPS - 1)
                act_pt(act, HEADS * GROUPS - 1, 1, 2)
                act_opart(act, HEADS * GROUPS - 1)
                act_o(act, HEADS * GROUPS - 1, B * GROUPS - 1, 3)
                act_wo(act, B * GROUPS - 2, 3)
                for t in range(QB):
                    act_wo(act, B * GROUPS - 1, t, (*S_BANK, PJ_BANK)[t])

            @block.vector
            def _(dve):
                for hb in range(2):
                    for a in range(2):
                        nc.vector.memset(pt[hb][a][:, PT_ZERO:PT_ZERO + P].bitcast(F32), 0.0).then_inc(s["zero_done"], 1)

                def ln_lo(t):
                    dve.wait_ge(s["ln_hi"], t + 1)
                    dve_lo(xn[1][:, :, t * P:(t + 1) * P], bank[t % 4][:, :].rearrange("p (c n) -> p c n", c=DC),
                           xn[0][:, :, t * P:(t + 1) * P], s["ln_lo"])

                for t in range(TT + 3):
                    if t < TT:
                        dve.wait_ge(s[f"x_in{t // QB}" if t else "x_first"], 16)
                        ln_stats(nc, dve, s, [("", t, x_res[:, t, :], stats, mv, var_eps)])
                    if t >= 3:
                        ln_lo(t - 3)
                    if t == 6:
                        for r in W1_SLOTS.values():
                            w1_lo(nc.vector, dve, 0, r)
                    if t == 9:
                        dve.wait_ge(s["const_in"], 48)
                        dve_rope_in(dve, 0, 0, 0)
                    if t == 13:
                        dve_rope_in(dve, 0, 1, 0)
                    if t == 16:
                        dve_rope_in(dve, 0, 2, 0)
                    if t == 17:
                        dve_q_lo(dve, 0, 1, 0)
                dve_v(dve, 0, 0)
                dve_q_lo(dve, 0, 2, 0)
                dve_masked(dve, 0, 0)
                dve_recip(dve, 0, 0)
                dve_group(dve, 0)
                with dve.Fori(1, GROUPS - 1) as g:
                    dve_group(dve, g)
                dve_group(dve, GROUPS - 1)
                dve_pt(dve, HEADS * GROUPS - 1, 1, 2)
                dve_oadd(dve, HEADS * GROUPS - 1, 1, HEADS * GROUPS // 2 - 1)
                dve_o(dve, HEADS * GROUPS // 2 - 1, 3)

            @block.gpsimd
            def _(pool):
                nc.gpsimd.memset(half[:, :], -0.5).then_inc(s["half_done"], 1)
                pool.wait_ge(s["half_done"], 1)
                for t in range(TT):
                    wait(pool, s["lnt_done"], t - 1)
                    ln_norm(nc, pool, s, "", t, x_res[:, t, :], ln_out[:, t % 2, 0:D], var_eps, half, rstd)
                    if t == 10:
                        pool.wait_ge(s["const_in"], 48)
                        pool_rope(pool, 0, 0, 0)
                    if t == 12:
                        pool.wait_ge(s["norm_done"], 13)
                        pool_k_lo(pool, 0, 0)
                    if t == 14:
                        pool_rope(pool, 0, 1, 0)
                pool_rope(pool, 0, 2, 0)
                pool_norm(pool, 0, 0)
                pool_group(pool, 0)
                with pool.Fori(1, GROUPS - 1) as g:
                    pool_group(pool, g)
                pool_group(pool, GROUPS - 1)
                pool_woacc(pool, B * GROUPS - 2, B - 2, 3)
                for t in range(QB):
                    pool_woacc(pool, B * GROUPS - 1, B - 1, t)

        attn.close()

        def st(name, shape, dt=F32):
            return stack.enter_context(nc.sbuf_tensor(name, shape, dt))

        ctx_raw = st("ctx_raw", [P, B, D])
        ctx_hi = st("ctx_hi", [P, B, D], F32R)
        ctx_lo = st("ctx_lo", [P, B, D], F32R)
        ctx_t = st("ctx_t", [P, B, DC, MEM])
        mask_u8 = st("mask_u8", [P, B * MEM], U8)
        mask_f = st("mask_f", [P, B, MEM])
        mask_add = st("mask_add", [P, B, MEM])
        valid = st("valid", [P, B])
        ln_t = st("ln_t", [P, 2, D])
        ln_h = st("ln_h", [P, 2, D])
        xt = st("xt", [P, DC, P])
        mv_h = st("mv_h", [P, 2, 2])
        var_eps_h = st("var_eps_h", [P, 2, 2])
        rstd_h = st("rstd_h", [P, 2])
        stats_h = st("stats_h", [P, 2, 6])
        m_sc = st("m_sc", [P, 2, MEM])
        m_neg = st("m_neg", [P, 2, 3])
        m_inv = st("m_inv", [P, 2, 2])
        a_st = st("a_st", [P, P], F32R)
        rw_raw = st("rw_raw", [P, DC, E])
        rw_t = st("rw_t", [P, DC, 2 * E], F32R)
        rb = st("rb", [P, E])
        iota = st("iota", [P, E])
        logits = st("logits", [P, 2, E])
        top = st("top", [P, 8])
        top_at = st("top_at", [P, 8], U32)
        top_f = st("top_f", [P, 2])
        gate2 = st("gate2", [P, 6])
        pick = st("pick", [P, 2, E])
        share = st("share", [P, TT, E])
        share_e = st("share_e", [P, TT, 1])
        share_parts = st("share_parts", [P, 2, P])
        share_t = st("share_t", [P, P], F32R)
        bias_rows = st("bias_rows", [P, D])
        down_bias = st("down_bias", [P, D], F32R)
        bias_out = st("bias_out", [P, 2, D])
        gu_raw = st("gu_raw", [P, 2, DC, 2, P])
        dn_raw = st("dn_raw", [P, 2, D])
        bias_raw = st("bias_raw", [P, 2, 2])
        gu = [st("gu_hi", [P, 2, DC, 2, P], F32R), st("gu_lo", [P, 2, DC, 2, P], F32R)]
        dn = [st("dn_hi", [P, 2, D], F32R), st("dn_lo", [P, 2, D], F32R)]
        bias = st("bias", [P, 2, 2])
        gate = st("gate", [P, 2, L])
        up = st("up", [P, 2, L])
        sig = st("sig", [P, 2, L])
        act_st = [st("act_hi", [P, 2, L], F32R), st("act_lo", [P, 2, L], F32R)]

        names2 = []
        for pre in ("m_", "h_"):
            names2 += [pre + e for e in ("stat_done", "aggr_done", "eps_done", "rstd_done", "norm_done")]
        names2 += ["mem_in", "mask_in", "rw_in", "small_in", "bd_in", "ctx_hi_done", "ctx_lo_done", "ctx_t_in",
                   "mask_f_done", "mask_tab", "rw_hi_done", "rw_lo_done",
                   "mt_tr", "mt_done", "msc_done", "m1", "m3", "mexp_done", "msum_inv", "m_inv_done", "at_tr", "at_hi", "at_lo",
                   "read_done", "x_mem", "ht_tr", "ht_hi", "ht_lo", "log_done", "l1", "l2", "top_done", "topi_done", "diff_done",
                   "gexp_done", "g1", "g2", "g3", "topf_done", "p1", "share_done", "st_tr", "st_done", "bias_mm", "x_bias",
                   "share_e_done", "parts_zero", "parts_done", "bias_hi_done", "bias_lo_done", "bias_out_done",
                   "gu_in0", "gu_in1", "gu_hi_done", "gu_lo_done", "dn_hi_done", "dn_lo_done", "bias_done", "gu_mm", "gate_done", "up_done",
                   "sig_done", "glu_done", "act_done", "ah_done", "al_done", "dn_mm", "x_moe", "out_done"]
        z = {name: sem("z_" + name) for name in names2}
        STEPS = IB * B

        M_TR, M_SC, A_TR, A_OUT, H_TR, H_LOG, S_TR, S_OUT = bank

        def pe_m_trans(pe, t):
            pe.wait_ge(z["m_norm_done"], t + 1)
            wait(pe, z["mt_done"], t)
            for c in range(DC):
                last = nc.tensor.transpose(M_TR[:, c * P:(c + 1) * P], ln_t[:, t % 2, c * P:(c + 1) * P], ident[:, :])
            last.then_inc(z["mt_tr"], 1)

        def pe_m_scores(pe, t):
            if t == 0:
                pe.wait_ge(z["ctx_t_in"], 16)
            pe.wait_ge(z["mt_done"], t + 1)
            wait(pe, z["m1"], t)
            for c in range(DC):
                last = nc.tensor.matmul(M_SC[:, 0:MEM], xt[:, c, :], ctx_t[:, t // QB, c, :], start=(c == 0), stop=(c == DC - 1))
            last.then_inc(z["msc_done"], 1)

        def pe_a_trans(pe, t):
            pe.wait_ge(z["mexp_done"], t + 1)
            wait(pe, z["at_lo"], t)
            nc.tensor.transpose(A_TR[0:MEM, 0:P], m_sc[:, t % 2, :], ident[:, :]).then_inc(z["at_tr"], 1)

        def pe_read(pe, t):
            if t % QB == 0:
                pe.wait_ge(z["ctx_lo_done"], t // QB + 1)
            pe.wait_ge(z["at_lo"], t + 1)
            wait(pe, z["x_mem"], t)
            nc.tensor.matmul(A_OUT[:, :], a_st[:, :], ctx_hi[:, t // QB, :], start=True, stop=False)
            nc.tensor.matmul(A_OUT[:, :], a_st[:, :], ctx_lo[:, t // QB, :], start=False, stop=True).then_inc(z["read_done"], 1)

        def pe_h_trans(pe, t):
            pe.wait_ge(z["h_norm_done"], t + 1)
            wait(pe, z["ht_lo"], t)
            for c in range(DC):
                last = nc.tensor.transpose(H_TR[:, c * P:(c + 1) * P], ln_h[:, t % 2, c * P:(c + 1) * P], ident[:, :])
            last.then_inc(z["ht_tr"], 1)

        def pe_logits(pe, t):
            if t == 0:
                pe.wait_ge(z["rw_lo_done"], 1)
            pe.wait_ge(z["ht_lo"], t + 1)
            wait(pe, z["l2"], t)
            for a in range(2):
                for c in range(DC):
                    last = nc.tensor.matmul(H_LOG[:, 0:2 * E], xn[a][:, c, t * P:(t + 1) * P], rw_t[:, c, :],
                                            start=(a == 0 and c == 0), stop=(a == 1 and c == DC - 1))
            last.then_inc(z["log_done"], 1)

        def pe_s_trans(pe, t):
            pe.wait_ge(z["parts_done"], 3 * t + 3)
            wait(pe, z["st_done"], t)
            nc.tensor.transpose(S_TR[:, 0:P], share_parts[:, t % 2, :], ident[:, :]).then_inc(z["st_tr"], 1)

        def pe_bias(pe, t):
            if t == 0:
                pe.wait_ge(z["bias_lo_done"], 1)
            pe.wait_ge(z["st_done"], t + 1)
            wait(pe, z["bias_out_done"], t)
            nc.tensor.matmul(S_OUT[:, :], share_t[:, :], down_bias[:, :], start=True, stop=True).then_inc(z["bias_mm"], 1)

        def act_ctx(act, b):
            act.wait_ge(z["mem_in"], 32)
            act_split(ctx_hi[:, b, :], ctx_raw[:, b, :], z["ctx_hi_done"])

        def pool_ctx(pool, b):
            pool.wait_ge(z["ctx_hi_done"], b + 1)
            nc.gpsimd.tensor_tensor(ctx_lo[:, b, :], ctx_raw[:, b, :], ctx_hi[:, b, :].bitcast(F32), ALU.subtract).then_inc(z["ctx_lo_done"], 1)

        def act_mt(act, t):
            act.wait_ge(z["mt_tr"], t + 1)
            wait(act, z["msc_done"], t)
            nc.scalar.activation(xt[:, :, :], M_TR[:, :].rearrange("p (c n) -> p c n", c=DC), ACT.Copy).then_inc(z["mt_done"], 1)

        def act_m_exp(act, t):
            act.wait_ge(z["m3"], t + 1)
            k = t % 2
            nc.scalar.activation(m_sc[:, k, :], m_sc[:, k, :], ACT.Exp, bias=m_neg[:, k, 1:2], accum_out=m_neg[:, k, 2:3]).then_inc(z["mexp_done"], 1)

        def act_at(act, t):
            act.wait_ge(z["at_tr"], t + 1)
            wait(act, z["read_done"], t)
            act_split(a_st[0:MEM, :], A_TR[0:MEM, 0:P], z["at_hi"])

        def act_ht(act, t):
            act.wait_ge(z["ht_tr"], t + 1)
            act_split(xn[0][:, :, t * P:(t + 1) * P], H_TR[:, :].rearrange("p (c n) -> p c n", c=DC), z["ht_hi"])

        def act_gate_exp(act, t):
            act.wait_ge(z["diff_done"], t + 1)
            nc.scalar.activation(gate2[:, 1:2], gate2[:, 0:1], ACT.Exp).then_inc(z["gexp_done"], 1)

        def act_share_t(act, t):
            act.wait_ge(z["st_tr"], t + 1)
            wait(act, z["bias_mm"], t)
            nc.scalar.activation(share_t[:, :], S_TR[:, 0:P], ACT.Copy).then_inc(z["st_done"], 1)

        def act_bias_out(act, t):
            act.wait_ge(z["bias_mm"], t + 1)
            wait(act, z["x_bias"], t - 1)
            nc.scalar.activation(bias_out[:, t % 2, :], S_OUT[:, :], ACT.Copy).then_inc(z["bias_out_done"], 1)

        def dve_scores_and_top(dve, tm, th):
            m, h = tm is not None, th is not None
            if h:
                dve.wait_ge(z["log_done"], th + 1)
                nc.vector.tensor_tensor(logits[:, 0, :], H_LOG[:, 0:E], rb[:, :], ALU.add).then_inc(z["l1"], 1)
            if m:
                b, k = tm // QB, tm % 2
                dve.wait_ge(z["msc_done"], tm + 1)
                wait(dve, z["at_tr"], tm - 1)
                nc.vector.tensor_tensor_reduce(out=m_sc[:, k, :], in0=M_SC[:, 0:MEM], in1=mask_add[:, b, :], scale=M_SCALE, scalar=NEG,
                                               op0=ALU.add, op1=ALU.max, accum_out=m_neg[:, k, 0:1]).then_inc(z["m1"], 1)
            if h:
                dve.wait_ge(z["l1"], th + 1)
                nc.vector.tensor_tensor(logits[:, 1, :], H_LOG[:, E:2 * E], logits[:, 0, :], ALU.add).then_inc(z["l2"], 1)
            if h:
                dve.wait_ge(z["l2"], th + 1)
                nc.vector.max(top[:, :], logits[:, 1, :]).then_inc(z["top_done"], 1)
            if m:
                dve.wait_ge(z["m1"], tm + 1)
                nc.vector.tensor_scalar(m_neg[:, k, 1:2], m_neg[:, k, 0:1], -1.0, None, ALU.mult).then_inc(z["m3"], 1)
            if h:
                dve.wait_ge(z["top_done"], th + 1)
                nc.vector.tensor_tensor(gate2[:, 0:1], top[:, 1:2], top[:, 0:1], ALU.subtract).then_inc(z["diff_done"], 1)
                nc.vector.max_index(top_at[:, :], top[:, :], logits[:, 1, :]).then_inc(z["topi_done"], 1)

        def dve_sum_and_shares(dve, tm, th):
            m, h = tm is not None, th is not None
            k = (tm or 0) % 2
            if h:
                dve.wait_ge(z["topi_done"], th + 1)
                nc.vector.tensor_copy(top_f[:, :], top_at[:, 0:2]).then_inc(z["topf_done"], 1)
                dve.wait_ge(z["gexp_done"], th + 1)
                nc.vector.tensor_scalar(gate2[:, 2:3], gate2[:, 1:2], 1.0, None, ALU.add).then_inc(z["g1"], 1)
            if m:
                dve.wait_ge(z["mexp_done"], tm + 1)
                wait(dve, z["x_mem"], tm - 1)
                nc.vector.reciprocal(m_inv[:, k, 0:1], m_neg[:, k, 2:3]).then_inc(z["msum_inv"], 1)
            if h:
                dve.wait_ge(z["g1"], th + 1)
                nc.vector.reciprocal(gate2[:, 3:4], gate2[:, 2:3]).then_inc(z["g2"], 1)
            if m:
                dve.wait_ge(z["msum_inv"], tm + 1)
                nc.vector.tensor_tensor(m_inv[:, k, 1:2], m_inv[:, k, 0:1], valid[:, tm // QB:tm // QB + 1], ALU.mult).then_inc(z["m_inv_done"], 1)
            if h:
                dve.wait_ge(z["g2"], th + 1)
                nc.vector.tensor_tensor(gate2[:, 4:5], gate2[:, 3:4], gate2[:, 1:2], ALU.mult).then_inc(z["g3"], 1)
                dve.wait_ge(z["topf_done"], th + 1)
                dve.wait_ge(z["g3"], th + 1)
                for j in range(2):
                    nc.vector.tensor_scalar(pick[:, j, :], iota[:, :], top_f[:, j:j + 1], gate2[:, 3 + j:4 + j], ALU.is_equal, ALU.mult).then_inc(z["p1"], 1)
                dve.wait_ge(z["p1"], 2 * th + 2)
                nc.vector.tensor_tensor(share[:, th, :], pick[:, 0, :], pick[:, 1, :], ALU.add).then_inc(z["share_done"], 1)

        def dve_at(dve, t):
            dve.wait_ge(z["at_hi"], t + 1)
            nc.vector.tensor_tensor(a_st[MEM:P, :], A_TR[0:MEM, 0:P], a_st[0:MEM, :].bitcast(F32), ALU.subtract).then_inc(z["at_lo"], 1)

        def dve_ht(dve, t):
            dve.wait_ge(z["ht_hi"], t + 1)
            dve_lo(xn[1][:, :, t * P:(t + 1) * P], H_TR[:, :].rearrange("p (c n) -> p c n", c=DC), xn[0][:, :, t * P:(t + 1) * P], z["ht_lo"])

        def dve_x_mem(dve, t):
            dve.wait_ge(z["read_done"], t + 1)
            dve.wait_ge(z["m_inv_done"], t + 1)
            nc.vector.scalar_tensor_tensor(out=x_res[:, t, :], in0=A_OUT[:, :], scalar=m_inv[:, t % 2, 1:2], in1=x_res[:, t, :],
                                           op0=ALU.mult, op1=ALU.add).then_inc(z["x_mem"], 1)

        def pool_parts(pool, t):
            k = t % 2
            if t == 0:
                pool.wait_ge(z["parts_zero"], 2)
            pool.wait_ge(z["share_done"], t + 1)
            wait(pool, z["st_tr"], t - 1)
            for at in (0, 2 * 32):
                nc.gpsimd.tensor_scalar(share_parts[:, k, at:at + E].bitcast(F32R), share[:, t, :], 1.0, 0.0, ALU.mult, ALU.add).then_inc(z["parts_done"], 1)
            pool.wait_ge(z["parts_done"], 3 * t + 2)
            nc.gpsimd.tensor_tensor(share_parts[:, k, 32:32 + E], share[:, t, :], share_parts[:, k, 0:E], ALU.subtract).then_inc(z["parts_done"], 1)

        def pool_bias(pool, t):
            pool.wait_ge(z["bias_out_done"], t + 1)
            nc.gpsimd.tensor_tensor(x_res[:, t, :], bias_out[:, t % 2, :], x_res[:, t, :], ALU.add).then_inc(z["x_bias"], 1)

        M_AT, EXP_AT, READ_AT, ADD_AT, H_AT, TOP_AT, S_AT, B_AT = range(1, 9)
        ROUNDS = TT + B_AT

        def on(step, k, t_of):
            if 0 <= k - t_of < TT:
                step(k - t_of)

        def sp_weights(sp, e, ib):
            k, u = ib % 2, IB * e + ib
            wait(sp, z["gu_lo_done"], u - 1)
            wait(sp, z["gu_hi_done"], u - 1)
            wait(sp, z["dn_lo_done"], u - 1)
            wait(sp, z["bias_done"], 2 * u - 2)
            if not isinstance(e, int):
                settled(sp)
            sp.dma_start(gu_raw[:, k, :, :, :], gu_w[bass.ds((e * IB + ib) * P, P), :, :, :]).then_inc(z[f"gu_in{k}"], 16)
            sp.dma_start(dn_raw[:, k, :], down_w.rearrange("e i h -> (e i) h")[bass.ds(e * I + ib * P, P), :]).then_inc(z[f"gu_in{k}"], 16)
            sp.dma_start(bias_raw[:, k, :], gu_b.rearrange("e (q s) -> (e q) s", s=2)[bass.ds(e * I + ib * P, P), :]).then_inc(z[f"gu_in{k}"], 16)

        def raw_in(ib, e):
            return 96 * e + 48 * (ib // 2) + 48

        def act_weights(act, e, ib):
            k, u = ib % 2, IB * e + ib
            act.wait_ge(z[f"gu_in{k}"], raw_in(ib, e))
            wait(act, z["dn_mm"], 4 * B * (u - 1))
            act_split(gu[0][:, k, :, :, :], gu_raw[:, k, :, :, :], z["gu_hi_done"])
            act_split(dn[0][:, k, :], dn_raw[:, k, :], z["dn_hi_done"])

        def pool_weights(pool, e, ib):
            k, u = ib % 2, IB * e + ib
            pool.wait_ge(z[f"gu_in{k}"], raw_in(ib, e))
            pool.wait_ge(z["gu_hi_done"], u + 1)
            nc.gpsimd.tensor_tensor(gu[1][:, k, :, :, :], gu_raw[:, k, :, :, :], gu[0][:, k, :, :, :].bitcast(F32), ALU.subtract).then_inc(z["gu_lo_done"], 1)
            pool.wait_ge(z["dn_hi_done"], u + 1)
            nc.gpsimd.tensor_tensor(dn[1][:, k, :], dn_raw[:, k, :], dn[0][:, k, :].bitcast(F32), ALU.subtract).then_inc(z["dn_lo_done"], 1)

        def dve_bias(dve, e, ib):
            k, u = ib % 2, IB * e + ib
            dve.wait_ge(z[f"gu_in{k}"], raw_in(ib, e))
            wait(dve, z["up_done"], B * (u - 1))
            nc.vector.tensor_scalar(bias[:, k, 0:1], bias_raw[:, k, 0:1], 0.0, None, ALU.add).then_inc(z["bias_done"], 1)
            nc.vector.tensor_scalar(bias[:, k, 1:2], bias_raw[:, k, 1:2], 1.0, None, ALU.add).then_inc(z["bias_done"], 1)

        def pe_gu(pe, e, st_, sides=(0, 1)):
            ib, b = divmod(st_, B)
            k, i = ib % 2, STEPS * e + st_
            pe.wait_ge(z["gu_lo_done"], IB * e + ib + 1)
            wait(pe, z["up_done"], i - 1)
            for side in sides:
                first = True
                for c in range(DC):
                    for sp_, mp in PASSES:
                        last = nc.tensor.matmul(bank[2 * (st_ % 2) + side][:, :], gu[sp_][:, k, c, side, :], xn[mp][:, c, b * L:(b + 1) * L],
                                                start=first, stop=(c == DC - 1 and (sp_, mp) == PASSES[-1]))
                        first = False
                last.then_inc(z["gu_mm"], 1)

        def pe_dn(pe, e, st_):
            ib = st_ // B
            k, i = ib % 2, STEPS * e + st_
            pe.wait_ge(z["al_done"], i + 1)
            pe.wait_ge(z["dn_lo_done"], IB * e + ib + 1)
            for t in range(QB):
                wait(pe, z["x_moe"], QB * i - QB + t + 1)
                for sp_, mp in PASSES:
                    last = nc.tensor.matmul(bank[4 + t][:, :], act_st[sp_][:, st_ % 2, t * P:(t + 1) * P], dn[mp][:, k, :],
                                            start=((sp_, mp) == PASSES[0]), stop=((sp_, mp) == PASSES[-1]))
                last.then_inc(z["dn_mm"], 1)

        def dve_gu(dve, e, st_):
            ib = st_ // B
            k, i, w = ib % 2, STEPS * e + st_, st_ % 2
            dve.wait_ge(z["bias_done"], 2 * (IB * e + ib) + 2)
            dve.wait_ge(z["gu_mm"], 2 * i + 1)
            nc.vector.tensor_scalar(gate[:, w, :], bank[2 * w][:, :], bias[:, k, 0:1], LIMIT, ALU.add, ALU.min).then_inc(z["gate_done"], 1)
            dve.wait_ge(z["gu_mm"], 2 * i + 2)
            wait(dve, z["ah_done"], i - 1)
            nc.vector.tensor_scalar(up[:, w, :], bank[2 * w + 1][:, :], bias[:, k, 1:2], LIMIT + 1.0, ALU.add, ALU.min).then_inc(z["up_done"], 1)

        def dve_act(dve, e, st_):
            i, w = STEPS * e + st_, st_ % 2
            dve.wait_ge(z["sig_done"], i + 1)
            nc.vector.tensor_tensor(sig[:, w, :], sig[:, w, :], gate[:, w, :], ALU.mult).then_inc(z["glu_done"], 1)
            dve.wait_ge(z["glu_done"], i + 1)
            nc.vector.scalar_tensor_tensor(out=up[:, w, :], in0=up[:, w, :], scalar=1.0 - LIMIT, in1=sig[:, w, :],
                                           op0=ALU.max, op1=ALU.mult).then_inc(z["act_done"], 1)

        def dve_al(dve, e, st_):
            i, w = STEPS * e + st_, st_ % 2
            dve.wait_ge(z["ah_done"], i + 1)
            dve_lo(act_st[1][:, w, :], up[:, w, :], act_st[0][:, w, :], z["al_done"])

        def dve_moe(dve, e, st_, t):
            b = st_ % B
            i = STEPS * e + st_
            tt = b * QB + t
            dve.wait_ge(z["dn_mm"], QB * i + t + 1)
            wait(dve, z["x_moe"], QB * i + t - STEPS)
            nc.vector.scalar_tensor_tensor(out=x_res[:, tt, :], in0=bank[4 + t][:, :], scalar=share_e[:, tt, :], in1=x_res[:, tt, :],
                                           op0=ALU.mult, op1=ALU.add).then_inc(z["x_moe"], 1)

        def act_sigmoid(act, e, st_):
            i, w = STEPS * e + st_, st_ % 2
            act.wait_ge(z["gate_done"], i + 1)
            wait(act, z["act_done"], i - 1)
            nc.scalar.activation(sig[:, w, :], gate[:, w, :], ACT.Sigmoid, scale=ALPHA).then_inc(z["sig_done"], 1)

        def act_hi(act, e, st_):
            i, w = STEPS * e + st_, st_ % 2
            act.wait_ge(z["act_done"], i + 1)
            wait(act, z["dn_mm"], QB * (i - 1))
            act_split(act_st[0][:, w, :], up[:, w, :], z["ah_done"])

        def act_step(act, e, st_):
            act_sigmoid(act, e, st_)
            act_hi(act, e, st_)

        def next_unit(e, ib):
            return (e, ib + 1) if ib + 1 < IB else (e + 1, 0)

        def pe_expert(pe, e, final):
            for st_ in range(STEPS):
                if st_ + 1 < STEPS and (st_ or not isinstance(e, int) or e):
                    pe_gu(pe, e, st_ + 1)
                elif st_ + 1 == STEPS and not final:
                    pe_gu(pe, e + 1, 0)
                pe_dn(pe, e, st_)

        def act_expert(act, e, final):
            for st_ in range(STEPS):
                if st_ + 1 < STEPS:
                    act_step(act, e, st_ + 1)
                elif not final:
                    act_step(act, e + 1, 0)
                if st_ % B == 1 and not (final and st_ // B == IB - 1):
                    act_weights(act, *next_unit(e, st_ // B))

        def dve_expert(dve, e, final):
            wait(dve, z["x_moe"], QB * STEPS * e)
            nc.vector.tensor_copy(share_e[:, :, :], share_of(e)).then_inc(z["share_e_done"], 1)
            dve.wait_ge(z["share_e_done"], e + 1)
            for st_ in range(STEPS):
                ne, ns = (e, st_ + 1) if st_ + 1 < STEPS else (e + 1, 0)
                more = not (final and st_ + 1 == STEPS)
                if more:
                    dve_gu(dve, ne, ns)
                dve_moe(dve, e, st_, 0)
                if more:
                    dve_act(dve, ne, ns)
                dve_moe(dve, e, st_, 1)
                if more:
                    dve_al(dve, ne, ns)
                dve_moe(dve, e, st_, 2)
                dve_moe(dve, e, st_, 3)
                if st_ % B == 1 and not (final and st_ // B == IB - 1):
                    dve_bias(dve, *next_unit(e, st_ // B))

        def share_of(e):
            return share[:, :, bass.ds(e, 1)]

        def pool_expert(pool, e, final):
            for ib in range(IB):
                if not (final and ib == IB - 1):
                    pool_weights(pool, *next_unit(e, ib))

        with nc.Block() as block:

            @block.sync
            def _(sp):
                ctx_tokens = ctx.rearrange("b m d -> m b d")
                sp.dma_start(ctx_t[:, :, :, :], ctx_cols).then_inc(z["ctx_t_in"], 16)
                sp.dma_start(mask_u8[:, :], mem_mask.rearrange("(o b) m -> o (b m)", o=1).partition_broadcast(P)).then_inc(z["mask_in"], 16)
                sp.dma_start(rw_raw[:, :, :], router_cols).then_inc(z["rw_in"], 16)
                for half_ in range(2):
                    sp.dma_start(ctx_raw[half_ * MEM:(half_ + 1) * MEM, :, :], ctx_tokens).then_inc(z["mem_in"], 16)
                sp.dma_start(rb[:, :], router_b.rearrange("(o e) -> o e", o=1).partition_broadcast(P)).then_inc(z["small_in"], 16)
                sp.dma_start(iota[:, :], iota_t).then_inc(z["small_in"], 16)
                sp.wait_ge(z["parts_zero"], 1)
                for at in (0, 32, 2 * 32):
                    sp.dma_start(bias_rows[at:at + E, :], down_b).then_inc(z["bd_in"], 16)
                for ib in range(IB):
                    sp_weights(sp, 0, ib)
                with sp.Fori(1, E) as e:
                    for ib in range(IB):
                        sp_weights(sp, e, ib)
                for b in range(B):
                    sp.wait_ge(z["x_moe"], QB * (E * STEPS - B + b + 1))
                    sp.dma_start(outr[:, b * QB:(b + 1) * QB, :], x_res[:, b * QB:(b + 1) * QB, :]).then_inc(z["out_done"], 16)
                sp.wait_ge(z["out_done"], 16 * B)

            @block.tensor
            def _(pe):
                for k in range(ROUNDS):
                    on(lambda t: pe_m_trans(pe, t), k, M_AT)
                    on(lambda t: pe_a_trans(pe, t), k, READ_AT)
                    on(lambda t: pe_h_trans(pe, t), k, H_AT)
                    on(lambda t: pe_s_trans(pe, t), k, S_AT)
                    on(lambda t: pe_m_scores(pe, t), k, M_AT)
                    on(lambda t: pe_read(pe, t), k, READ_AT)
                    if k == TT + READ_AT:
                        pe.wait_ge(z["mt_done"], TT)
                        pe.wait_ge(z["m1"], TT)
                        pe_gu(pe, 0, 0, (0,))
                    if k == TT + READ_AT + 1:
                        pe_gu(pe, 0, 0, (1,))
                        pe.wait_ge(z["x_mem"], TT)
                    if k == TT + READ_AT + 2:
                        pe_gu(pe, 0, 1, (0,))
                    if k == TT + READ_AT + 3:
                        pe_gu(pe, 0, 1, (1,))
                    on(lambda t: pe_logits(pe, t), k, H_AT)
                    on(lambda t: pe_bias(pe, t), k, S_AT)
                pe.wait_ge(z["l2"], TT)
                pe.wait_ge(z["bias_out_done"], TT)
                pe_expert(pe, 0, False)
                with pe.Fori(1, E - 1) as e:
                    pe_expert(pe, e, False)
                pe_expert(pe, E - 1, True)

            @block.scalar
            def _(act):
                for k in range(ROUNDS + 1):
                    on(lambda t: act_bias_out(act, t), k, B_AT)
                    on(lambda t: act_mt(act, t), k, M_AT)
                    if k == M_AT:
                        act_ctx(act, 0)
                        act.wait_ge(z["rw_in"], 16)
                        act_split(rw_t[:, :, 0:E], rw_raw[:, :, :], z["rw_hi_done"])
                    on(lambda t: act_at(act, t), k, READ_AT)
                    on(lambda t: act_ht(act, t), k, H_AT)
                    on(lambda t: act_m_exp(act, t), k, EXP_AT)
                    if M_AT < k < M_AT + B:
                        act_ctx(act, k - M_AT)
                    on(lambda t: act_gate_exp(act, t), k, TOP_AT)
                    on(lambda t: act_share_t(act, t), k, S_AT)
                    if k == H_AT:
                        act.wait_ge(z["bd_in"], 48)
                        act_split(down_bias[:, :], bias_rows[:, :], z["bias_hi_done"])
                    if k == TT:
                        act_weights(act, 0, 0)
                    if k == ROUNDS - 2:
                        act_sigmoid(act, 0, 0)
                    if k == ROUNDS - 1:
                        act_hi(act, 0, 0)
                act_expert(act, 0, False)
                with act.Fori(1, E - 1) as e:
                    act_expert(act, e, False)
                act_expert(act, E - 1, True)

            @block.vector
            def _(dve):
                def tile_in(k, t_of):
                    return k - t_of if 0 <= k - t_of < TT else None

                for k in range(ROUNDS):
                    dve_scores_and_top(dve, tile_in(k, EXP_AT), tile_in(k, TOP_AT))
                    on(lambda t: dve_x_mem(dve, t), k, ADD_AT)
                    norms = [("m_", k, x_res[:, k, :], stats, mv, var_eps)] if k < TT else []
                    t = k - ADD_AT
                    if 0 <= t < TT:
                        dve.wait_ge(z["x_mem"], t + 1)
                        norms.append(("h_", t, x_res[:, t, :], stats_h, mv_h, var_eps_h))
                    ln_stats(nc, dve, z, norms)
                    if k == M_AT:
                        dve.wait_ge(z["mask_in"], 16)
                        nc.vector.tensor_copy(mask_f[:, :, :], mask_u8[:, :].rearrange("p (b m) -> p b m", b=B)).then_inc(z["mask_f_done"], 1)
                        dve.wait_ge(z["mask_f_done"], 1)
                        nc.vector.tensor_scalar(mask_add[:, :, :], mask_f[:, :, :], -1.0, -MASKED / M_SCALE, ALU.add, ALU.mult).then_inc(z["mask_tab"], 1)
                        nc.vector.reduce_max(valid[:, :], mask_f[:, :, :], AX.X).then_inc(z["mask_tab"], 1)
                        dve.wait_ge(z["mask_tab"], 2)
                    on(lambda t: dve_at(dve, t), k, READ_AT)
                    on(lambda t: dve_ht(dve, t), k, H_AT)
                    dve_sum_and_shares(dve, tile_in(k, EXP_AT), tile_in(k, TOP_AT))
                    if k == EXP_AT:
                        dve.wait_ge(z["rw_hi_done"], 1)
                        dve_lo(rw_t[:, :, E:2 * E], rw_raw[:, :, :], rw_t[:, :, 0:E], z["rw_lo_done"])
                        dve.wait_ge(z["small_in"], 32)
                    if k == TOP_AT:
                        dve.wait_ge(z["bias_hi_done"], 1)
                        nc.vector.tensor_tensor(down_bias[2 * 32:P, :], bias_rows[2 * 32:P, :], down_bias[2 * 32:P, :].bitcast(F32), ALU.subtract).then_inc(z["bias_lo_done"], 1)
                    if k == ROUNDS - 3:
                        dve_bias(dve, 0, 0)
                        dve_gu(dve, 0, 0)
                    if k == ROUNDS - 2:
                        dve_act(dve, 0, 0)
                    if k == ROUNDS - 1:
                        dve_al(dve, 0, 0)
                dve.wait_ge(z["share_done"], TT)
                dve.wait_ge(z["x_bias"], TT)
                dve_expert(dve, 0, False)
                with dve.Fori(1, E - 1) as e:
                    dve_expert(dve, e, False)
                dve_expert(dve, E - 1, True)

            @block.gpsimd
            def _(pool):
                nc.gpsimd.memset(bias_rows[:, :], 0.0).then_inc(z["parts_zero"], 1)
                nc.gpsimd.memset(share_parts[:, :, :], 0.0).then_inc(z["parts_zero"], 1)
                for k in range(ROUNDS + 1):
                    if k < TT:
                        wait(pool, z["mt_tr"], k - 1)
                        ln_norm(nc, pool, z, "m_", k, x_res[:, k, :], ln_t[:, k % 2, :], var_eps, half, rstd)
                    t = k - ADD_AT
                    if 0 <= t < TT:
                        wait(pool, z["ht_tr"], t - 1)
                        ln_norm(nc, pool, z, "h_", t, x_res[:, t, :], ln_h[:, t % 2, :], var_eps_h, half, rstd_h)
                    if M_AT <= k < M_AT + B:
                        pool_ctx(pool, k - M_AT)
                    on(lambda t: pool_parts(pool, t), k, TOP_AT)
                    on(lambda t: pool_bias(pool, t), k, B_AT)
                    if k == TT:
                        pool_weights(pool, 0, 0)
                pool_expert(pool, 0, False)
                with pool.Fori(1, E - 1) as e:
                    pool_expert(pool, e, False)
                pool_expert(pool, E - 1, True)


def _laid_out(inputs):
    x, ctx = inputs["x"], inputs["ctx_2048"]
    wq, wk, wv, wo = (inputs[f"L0_attn_W{n}"] for n in "qkvo")
    router, gate_up = inputs["L0_ffn_router_weight"], inputs["L0_ffn_gate_up_proj"]
    by_group = np.concatenate([w.reshape(GROUPS, -1, D) for w in (wq, wk, wv)], axis=1)
    return {
        "x": x,
        "ctx": ctx,
        "ctx_cols": ctx.reshape(B, MEM, DC, P).transpose(3, 0, 2, 1),
        "mask": inputs["mask_BxS2_bk0"],
        "wqkv": by_group.reshape(GROUPS, 3 * P, DC, P).transpose(0, 3, 2, 1).reshape(GROUPS * P, DC, 3 * P),
        "wo_rows": wo.reshape(D, GROUPS, 2, P).transpose(1, 3, 2, 0).reshape(GROUPS * P, 2, D),
        "router_cols": router.reshape(E, DC, P).transpose(2, 1, 0),
        "router_bias": inputs["L0_ffn_router_bias"],
        "gate_up": gate_up.reshape(E, DC, P, IB, P, 2).transpose(0, 3, 2, 1, 5, 4).reshape(E * IB * P, DC, 2, P),
        "gate_up_bias": inputs["L0_ffn_gate_up_proj_bias"],
        "down": inputs["L0_ffn_down_proj"],
        "down_bias": inputs["L0_ffn_down_proj_bias"],
    }


def _constants():
    inv = (1.0 / 10000.0 ** (np.arange(0, HD, 2, dtype=np.float32) / HD)).astype(np.float32)
    angle = (np.arange(L, dtype=np.float32)[:, None] * inv[None, :]).astype(np.float32)
    row = (np.arange(P) % HD) // 2
    sign = np.where(np.arange(P) % 2 == 0, -1.0, 1.0)[:, None]
    cos = np.cos(angle.astype(np.float64)).T[row].astype(np.float32)
    sin = (np.sin(angle.astype(np.float64)).T[row] * sign).astype(np.float32)
    causal = np.where(np.arange(L)[None, :] - (L - P) <= np.arange(P)[:, None], 0.0, NEG).astype(np.float32)
    iota = np.broadcast_to(np.arange(E, dtype=np.float32), (P, E)).copy()
    return {"cos": cos, "sin": sin, "causal": causal, "ident": np.eye(P, dtype=np.float32), "iota": iota}


def kernel(**inputs):
    import concourse.bacc as bacc
    from concourse.bass_utils import run_bass_kernel_spmd

    nc = bacc.Bacc("TRN2", target_bir_lowering=False, num_devices=1, dynamic_dma_scratch_size=1024)
    arrays, args = {}, []
    for name, a in _laid_out({name: np.asarray(a) for name, a in inputs.items()}).items():
        arrays[f"in_{name}"] = np.ascontiguousarray(a)
    for name, a in _constants().items():
        arrays[f"const_{name}"] = a
    for name, a in arrays.items():
        args.append(nc.dram_tensor(name, a.shape, mybir.dt.from_np(a.dtype), kind="ExternalInput").ap())
    out = nc.dram_tensor("out", (B, L, D), F32, kind="ExternalOutput").ap()
    decoder_layer(nc, *args, out)
    r = run_bass_kernel_spmd(nc, [arrays], core_ids=[0])
    return r.results[0]["out"]
```
